# Optimizing a Trainium2 kernel written in Bass

```python
import numpy as np
import jax
import jax.numpy as jnp

def _softmax(x, axis=-1):
    return jax.nn.softmax(x, axis=axis)

def _gelu(x):
    return jax.nn.gelu(x, approximate=True)

def _silu(x):
    return jax.nn.silu(x)

def _sigmoid(x):
    return jax.nn.sigmoid(x)

def _layernorm(x, axis=-1, eps=1e-05):
    m = jnp.mean(x, axis=axis, keepdims=True)
    v = jnp.var(x, axis=axis, keepdims=True)
    return (x - m) / jnp.sqrt(v + eps)

def _scatter_add(tgt, idx, src, axis=0):
    return tgt.at[idx].add(src)

def _segment_sum(src, seg, n):
    return jax.ops.segment_sum(src, seg, n)
kernel_name = 'mk_gnn_ffn_d1_gnn_r64_0a989c'

def setup_inputs(seed: int=0):
    np.random.seed(seed)
    _w = jnp.asarray

    def _rec_inputs():
        import jax
        import jax.numpy as jnp
        _gk = jax.random.key(seed)
        x = -6.415e-05 + 1 * jax.random.normal(jax.random.fold_in(_gk, 1), (10000, 512), jnp.float32)
        src = jax.random.randint(jax.random.fold_in(_gk, 2), (5000,), 0, 10000, jnp.int32)
        dst = jax.random.randint(jax.random.fold_in(_gk, 3), (5000,), 0, 10000, jnp.int32)
        _o = jnp.argsort(dst, stable=True)
        src = src[_o]
        dst = dst[_o]
        edge_attr_64 = 0.000279952 + 1.00013 * jax.random.normal(jax.random.fold_in(_gk, 11), (5000, 64), jnp.float32)
        return (x, src, dst, edge_attr_64)
    x, src, dst, edge_attr_64 = _rec_inputs()

    def _L0_gnn_setup():
        import jax, jax.numpy as jnp
        import numpy as np
        N_NODES = 20000
        N_EDGES = 5000
        HIDDEN = 512
        EDGE_DIM = 64
        LN_EPS = 1e-05

        def mish(x):
            return x * jnp.tanh(jax.nn.softplus(x))
        key = jax.random.key(seed)
        ks = jax.random.split(key, 8)
        s = lambda fan_in: 1.0 / np.sqrt(fan_in)
        return {'x': jax.random.normal(ks[0], (N_NODES, HIDDEN), dtype=jnp.float32), 'edge_index': jax.random.randint(ks[1], (2, N_EDGES), 0, N_NODES, dtype=jnp.int64), 'edge_attr': jax.random.normal(ks[2], (N_EDGES, EDGE_DIM), dtype=jnp.float32), 'W1': jax.random.normal(ks[3], (2 * HIDDEN + EDGE_DIM, HIDDEN), dtype=jnp.float32) * s(2 * HIDDEN + EDGE_DIM), 'b1': jnp.zeros((HIDDEN,), dtype=jnp.float32), 'W2': jax.random.normal(ks[4], (HIDDEN, HIDDEN), dtype=jnp.float32) * s(HIDDEN), 'b2': jnp.zeros((HIDDEN,), dtype=jnp.float32), 'W3': jax.random.normal(ks[5], (2 * HIDDEN, HIDDEN), dtype=jnp.float32) * s(2 * HIDDEN), 'b3': jnp.zeros((HIDDEN,), dtype=jnp.float32), 'W4': jax.random.normal(ks[6], (HIDDEN, HIDDEN), dtype=jnp.float32) * s(HIDDEN), 'b4': jnp.zeros((HIDDEN,), dtype=jnp.float32), 'gamma': jnp.ones((HIDDEN,), dtype=jnp.float32), 'beta': jnp.zeros((HIDDEN,), dtype=jnp.float32)}
    _L0_gnn_all = _L0_gnn_setup()
    _L0_gnn_in = {k: v for k, v in _L0_gnn_all.items() if k in ('W1', 'b1', 'W2', 'b2', 'W3', 'b3', 'W4', 'b4', 'gamma', 'beta')}
    del _L0_gnn_all

    def _L0_ffn_setup():
        import jax, jax.numpy as jnp
        import numpy as np
        STEP_SIZE = 0.1

        def _mlp(y, W1, b1, W2, b2, W3, b3):
            h = jnp.tanh(y @ W1.T + b1)
            h = jnp.tanh(h @ W2.T + b2)
            return h @ W3.T + b3

        def _rk4_step(y, dt, params):
            f = lambda z: _mlp(z, *params)
            k1 = f(y)
            k2 = f(y + dt / 2 * k1)
            k3 = f(y + dt / 2 * k2)
            k4 = f(y + dt * k3)
            return y + dt * (k1 + 2 * k2 + 2 * k3 + k4) / 6
        key = jax.random.key(seed)
        ks = jax.random.split(key, 7)
        B, S, D, H = (256, 64, 512, 32)
        return {'x': jax.random.normal(ks[0], (B, S, D), dtype=jnp.float32), 'W1': jax.random.normal(ks[1], (H, D), dtype=jnp.float32) * (1.0 / np.sqrt(D)), 'b1': jax.random.normal(ks[2], (H,), dtype=jnp.float32) * 0.01, 'W2': jax.random.normal(ks[3], (H, H), dtype=jnp.float32) * (1.0 / np.sqrt(H)), 'b2': jax.random.normal(ks[4], (H,), dtype=jnp.float32) * 0.01, 'W3': jax.random.normal(ks[5], (D, H), dtype=jnp.float32) * (1.0 / np.sqrt(H)), 'b3': jax.random.normal(ks[6], (D,), dtype=jnp.float32) * 0.01}
    _L0_ffn_all = _L0_ffn_setup()
    _L0_ffn_in = {k: v for k, v in _L0_ffn_all.items() if k in ('W1', 'b1', 'W2', 'b2', 'W3', 'b3')}
    del _L0_ffn_all
    return {'x': x, 'src': src, 'dst': dst, 'edge_attr_64': edge_attr_64, 'L0_gnn_W1': _L0_gnn_in['W1'], 'L0_gnn_b1': _L0_gnn_in['b1'], 'L0_gnn_W2': _L0_gnn_in['W2'], 'L0_gnn_b2': _L0_gnn_in['b2'], 'L0_gnn_W3': _L0_gnn_in['W3'], 'L0_gnn_b3': _L0_gnn_in['b3'], 'L0_gnn_W4': _L0_gnn_in['W4'], 'L0_gnn_b4': _L0_gnn_in['b4'], 'L0_gnn_gamma': _L0_gnn_in['gamma'], 'L0_gnn_beta': _L0_gnn_in['beta'], 'L0_ffn_W1': _L0_ffn_in['W1'], 'L0_ffn_b1': _L0_ffn_in['b1'], 'L0_ffn_W2': _L0_ffn_in['W2'], 'L0_ffn_b2': _L0_ffn_in['b2'], 'L0_ffn_W3': _L0_ffn_in['W3'], 'L0_ffn_b3': _L0_ffn_in['b3']}

def reference(x, src, dst, edge_attr_64, L0_gnn_W1, L0_gnn_b1, L0_gnn_W2, L0_gnn_b2, L0_gnn_W3, L0_gnn_b3, L0_gnn_W4, L0_gnn_b4, L0_gnn_gamma, L0_gnn_beta, L0_ffn_W1, L0_ffn_b1, L0_ffn_W2, L0_ffn_b2, L0_ffn_W3, L0_ffn_b3):
    import jax
    import jax.numpy as jnp

    def _L0_gnn_ref(x, edge_index, edge_attr, W1, b1, W2, b2, W3, b3, W4, b4, gamma, beta):
        import jax, jax.numpy as jnp
        import numpy as np
        N_NODES = 20000
        N_EDGES = 5000
        HIDDEN = 512
        EDGE_DIM = 64
        LN_EPS = 1e-05

        def mish(x):
            return x * jnp.tanh(jax.nn.softplus(x))
        src, dst = (edge_index[0], edge_index[1])
        edge_feat = jnp.concatenate([x[src], x[dst], edge_attr], axis=-1)
        h = mish(edge_feat @ W1 + b1)
        messages = mish(h @ W2 + b2)
        agg = jax.ops.segment_sum(messages, dst, num_segments=x.shape[0])
        u = mish(jnp.concatenate([x, agg], axis=-1) @ W3 + b3)
        out = u @ W4 + b4
        y = x + out
        mu = jnp.mean(y, axis=-1, keepdims=True)
        var = jnp.mean(jnp.square(y - mu), axis=-1, keepdims=True)
        return (y - mu) * jax.lax.rsqrt(var + LN_EPS) * gamma + beta

    def _L0_ffn_ref(x, W1, b1, W2, b2, W3, b3):
        import jax, jax.numpy as jnp
        import numpy as np
        STEP_SIZE = 0.1

        def _mlp(y, W1, b1, W2, b2, W3, b3):
            h = jnp.tanh(y @ W1.T + b1)
            h = jnp.tanh(h @ W2.T + b2)
            return h @ W3.T + b3

        def _rk4_step(y, dt, params):
            f = lambda z: _mlp(z, *params)
            k1 = f(y)
            k2 = f(y + dt / 2 * k1)
            k3 = f(y + dt / 2 * k2)
            k4 = f(y + dt * k3)
            return y + dt * (k1 + 2 * k2 + 2 * k3 + k4) / 6
        B, S, D = x.shape
        params = (W1, b1, W2, b2, W3, b3)
        span = 1.0 / (S - 1)
        steps = max(1, int(span / STEP_SIZE))
        dt = span / steps

        def interval(y, _):
            for _s in range(steps):
                y = _rk4_step(y, dt, params)
            return (y, y)
        y0 = x[:, 0]
        _, ys = jax.lax.scan(interval, y0, None, length=S - 1)
        return jnp.concatenate([y0[:, None], jnp.moveaxis(ys, 0, 1)], axis=1)
    edge_index = jnp.stack([src, dst])
    x = x + _L0_gnn_ref(_layernorm(x, axis=-1), edge_index, edge_attr_64, L0_gnn_W1, L0_gnn_b1, L0_gnn_W2, L0_gnn_b2, L0_gnn_W3, L0_gnn_b3, L0_gnn_W4, L0_gnn_b4, L0_gnn_gamma, L0_gnn_beta)
    x = x + _L0_ffn_ref(_layernorm(x, axis=-1)[None], L0_ffn_W1, L0_ffn_b1, L0_ffn_W2, L0_ffn_b2, L0_ffn_W3, L0_ffn_b3)[0]
    return x

_drawn_inputs = setup_inputs


def setup_inputs(seed=0):
    import zlib

    import numpy as np

    out = dict(_drawn_inputs(seed))
    spreads = {'L0_gnn_b1': (0.0, 0.8),
     'L0_gnn_b2': (0.0, 0.743),
     'L0_gnn_b3': (0.0, 0.1),
     'L0_gnn_b4': (0.0, 0.1),
     'L0_gnn_gamma': (1.0, 0.2),
     'L0_gnn_beta': (0.0, 0.1)}
    factors = {'edge_attr_64': 3.688, 'L0_ffn_b1': 32.479, 'L0_ffn_b2': 25.688, 'L0_ffn_b3': 8.0}
    for name, (base, spread) in spreads.items():
        noise = np.random.default_rng([zlib.crc32(name.encode()), seed]).standard_normal(out[name].shape)
        drawn = base * np.exp(spread * noise) if base else spread * noise
        out[name] = jnp.asarray(drawn.astype(out[name].dtype))
    for name, factor in factors.items():
        out[name] = (out[name] * factor).astype(out[name].dtype)
    return out
```

```python
import concourse.bass as bass
from concourse import mybir
from contextlib import ExitStack


def gnn_ffn_kernel(
    nc: bass.Bass,
    x: bass.AP,
    src_cols: bass.AP,
    dst: bass.AP,
    dst_cols: bass.AP,
    edge_attr: bass.AP,
    W1: bass.AP,
    b1: bass.AP,
    W2: bass.AP,
    b2: bass.AP,
    W3: bass.AP,
    b3: bass.AP,
    W4: bass.AP,
    b4: bass.AP,
    gamma: bass.AP,
    beta: bass.AP,
    F_W1T: bass.AP,
    F_b1: bass.AP,
    F_W2T: bass.AP,
    F_b2: bass.AP,
    F_W3: bass.AP,
    F_W3T: bass.AP,
    F_b3: bass.AP,
    node_rule: bass.AP,
    time_rule: bass.AP,
    out: bass.AP,
    message_sums: bass.AP,
    sums_by_time: bass.AP,
):
    f32 = mybir.dt.float32
    f32r = mybir.dt.float32r
    i32 = mybir.dt.int32
    ALU = mybir.AluOpType
    ACT = mybir.ActivationFunctionType
    AX = mybir.AxisListType

    N, D = x.shape
    E = dst.shape[0]
    DE = edge_attr.shape[1]
    H = F_b1.shape[0]
    P = 125
    S = 4
    R = P * S
    KD = D // 128
    KF = 2 * KD + 1
    NE = E // R
    NN = N // R
    NT = 2 * S + 1
    EPS = 1e-5
    EXP_MAX = 4.0e8
    SPLIT = 112

    DT = 1.0 / (N - 1)
    G = 4
    T = N // G
    C = 500
    NC = T // C
    NQ = node_rule.shape[1]
    PICARD = 13
    KV = node_rule.shape[0]
    TOL = 1.5e-5

    ctx = ExitStack()
    with ctx:
        def sem(name):
            return ctx.enter_context(nc.semaphore(name))

        def psum(name, n=1):
            return ctx.enter_context(nc.psum_tensor(name, [128, n * 512], f32))

        def sb_in(scope):
            return lambda name, shape, dt=f32: scope.enter_context(nc.sbuf_tensor(name, shape, dt))

        banks = [psum(f"bank{i}") for i in range(8)]

        sb = sb_in(ctx)
        ident = sb("ident", [128, 128])
        eps_col = sb("eps_col", [128, 1])
        one_col = sb("one_col", [128, 1])
        two_col = sb("two_col", [128, 1])
        gamma_bc = sb("gamma_bc", [P, D])
        beta_bc = sb("beta_bc", [P, D])
        b4_bc = sb("b4_bc", [P, D])
        b3_bc = sb("b3_bc", [128, D])
        b1_col = sb("b1_col", [128, KD])
        b2_col = sb("b2_col", [128, KD])
        src_all = sb("src_all", [P, NE * S], i32)
        dst_all = sb("dst_all", [P, NE * S], i32)
        dst_allf = sb("dst_allf", [P, NE * S])
        steps_rhs = sb("steps_rhs", [KV, D])

        edge_scope = ExitStack()
        sb = sb_in(edge_scope)
        W1h = sb("W1h", [128, KF, D], f32r)
        W1l = sb("W1l", [128, KF, D], f32r)
        W2h = sb("W2h", [128, KD, D], f32r)
        W2l = sb("W2l", [128, KD, D], f32r)
        W3h = sb("W3h", [128, KD, D], f32r)
        W3l = sb("W3l", [128, KD, D], f32r)
        rows = sb("rows", [P, 2 * S, D])
        attr = sb("attr", [P, S, DE])
        fTh = sb("fTh", [128, KF, R], f32r)
        fTl = sb("fTl", [128, KF, R], f32r)
        h1h = sb("h1h", [128, KD, R], f32r)
        h1l = sb("h1l", [128, KD, R], f32r)
        msgh = sb("msgh", [128, KD, R], f32r)
        msgl = sb("msgl", [128, KD, R], f32r)
        tmp = sb("tmp", [128, 8, 512])
        zh = sb("zh", [P, 2, D], f32r)
        zl = sb("zl", [P, 2, D], f32r)
        zsum = sb("zsum", [P, S, D])
        e_stats = sb("e_stats", [P, 2 * S, 6])
        e_mv = sb("e_mv", [P, 2 * S, 2])
        e_lnv = sb("e_lnv", [P, 2 * S])
        e_rstd = sb("e_rstd", [P, 2 * S])
        e_var = sb("e_var", [P, 2 * S])
        e_sq = sb("e_sq", [P, 2 * S])
        src_cur = sb("src_cur", [P, S], i32)
        dst_cur = sb("dst_cur", [P, S], i32)
        drow_i = sb("drow_i", [P, R], i32)
        drow_f = sb("drow_f", [P, R])
        dcol_f = sb("dcol_f", [P, S])
        same = sb("same", [P, S, 126], f32r)
        earlier = sb("earlier", [P, P])
        same_earlier = sb("same_earlier", [P, S, P])
        n_earlier = sb("n_earlier", [P, S])
        spare_i = sb("spare_i", [P, 1], i32)
        spare_row = sb("spare_row", [P, 1])
        to_spare = sb("to_spare", [P, S])
        sum_row = sb("sum_row", [P, S])
        sum_row_i = sb("sum_row_i", [P, S], i32)
        edge_scope.close()

        node_scope = ExitStack()
        sb = sb_in(node_scope)
        W3ah = sb("W3ah", [128, KD, D], f32r)
        W3al = sb("W3al", [128, KD, D], f32r)
        W4h = sb("W4h", [128, KD, D], f32r)
        W4l = sb("W4l", [128, KD, D], f32r)
        x1_first = sb("x1_first", [P, S, D])
        steps_lhs = sb("steps_lhs", [KV, R])
        keep_top = ExitStack()
        sb = sb_in(keep_top)
        xraw = sb("xraw", [P, S, D])
        xn = sb("xn", [P, S, D])
        agg = sb("agg", [P, S, D])
        xTh = sb("xTh", [128, S, KD, P + 1], f32r)
        xTl = sb("xTl", [128, S, KD, P + 1], f32r)
        nz = sb("nz", [P, 2, D])
        ne = sb("ne", [P, 2, D])
        nt = sb("nt", [P, 2, D])
        nr = sb("nr", [P, 2, D])
        u = sb("u", [P, S, D])
        uTh = sb("uTh", [128, S, KD, P + 1], f32r)
        uTl = sb("uTl", [128, S, KD, P + 1], f32r)
        xnb = sb("xnb", [P, 2, S, D])
        pre = sb("pre", [P, 2, S, D])
        yb = sb("yb", [P, S, D])
        ob = sb("ob", [P, S, D])
        nstage = sb("nstage", [128, 2, KD, D])
        stx = sb("stx", [P, S, 6])
        sty = sb("sty", [P, S, 6])
        mvx = sb("mvx", [P, S, 2])
        mvy = sb("mvy", [P, S, 2])
        smx = sb("smx", [P, 4, S])
        smy = sb("smy", [P, 4, S])
        keep_top.close()

        ode_scope = ExitStack()
        sb = sb_in(ode_scope)
        ruleT = sb("ruleT", [KV, N])
        rule = sb("rule", [KV, NQ])
        fW1T = sb("fW1T", [128, KD, 128])
        fW3 = sb("fW3", [128, KD, 128])
        fb3 = sb("fb3", [128, KD])
        fW2 = sb("fW2", [128, 128])
        fb1 = sb("fb1", [128, 1])
        fb2 = sb("fb2", [128, 1])
        blocks = sb("blocks", [128, 128])
        groups_before = sb("groups_before", [128, 128])
        M_T = sb("M_T", [H, H])
        M_half = sb("M_half", [128, 128])
        M_full = sb("M_full", [128, 128])
        M_six = sb("M_six", [128, 128])
        slope = sb("slope", [128, 1])
        bias_half = sb("bias_half", [128, 1])
        bias_full = sb("bias_full", [128, 1])
        y0 = sb("y0", [1, D])
        y0_st = sb("y0_st", [1, 6])
        y0_mv = sb("y0_mv", [1, 2])
        y0_s = sb("y0_s", [1, 4])
        y0b3 = sb("y0b3", [128, KD, 2])
        a0 = sb("a0", [128, 1])
        V = sb("V", [64, H])
        gq = sb("gq", [H, NQ])
        hq = sb("hq", [H, NQ])
        A_guess = sb("A_guess", [128, T])
        A_base = sb("A_base", [128, T])
        times = sb("times", [128, T])
        zst = sb("zst", [128, 2, C])
        gst = sb("gst", [128, 4, C])
        hst = sb("hst", [128, NC + 1, C])
        Ssum = sb("Ssum", [128, NC, C])
        zeros = sb("zeros", [128, C])
        Pex = sb("Pex", [128, T + 1])
        off = sb("off", [128, 1])
        base = sb("base", [128, 1])
        dev = sb("dev", [128, 2, C])
        devmax = sb("devmax", [128, NC])
        devtop = sb("devtop", [128, 1])
        devrow = sb("devrow", [1, 1])
        flag = sb("flag", [1, 1], i32)
        seq_a = sb("seq_a", [H, 1])
        seq_bias = sb("seq_bias", [H, 3])
        seq_g = sb("seq_g", [H, 1])
        seq_h = sb("seq_h", [H, 4])
        seq_P = sb("seq_P", [H, 1])
        seq_S = sb("seq_S", [H, 3])
        seq_blk = sb("seq_blk", [H, C])
        seq_t = sb("seq_t", [H, C])
        ode_scope.close()
        node_scope.close()

        s = {}
        for name in (
            "consts_set diag_made spare_made smalls_in dstf_made table_filled staged split_hi split_lo "
            "staged1 idx_copied rows_in attr_in stats_done aggr_done ln_log ln_guess newton rows_normed groups_up "
            "group_hi group_lo layer_up exp_done cut_done t_done log_done r_done w_done m_done hi_done lo_done "
            "z_up z_hi z_lo c_up c_out drow_in seg same_made sumrow_made scattered "
            "n_staged1 n_staged n_hi n_lo x_in agg_in xs_done xa_done xl_log xl_guess xl_newton xn_done pre_done xnb_done "
            "xt_up xt_hi xt_lo ut_up ut_hi ut_lo u_up z_done ne_done nc_done nt_done nl_done nr_done nw_done u_done "
            "y_up y_added ys_done ya_done yl_log yl_guess yl_newton yn_done yg_done o_up o_added out_ready stored "
            "p_in first_done "
            "o_set o_loaded o_mat_up o_mats o_slope_up o_slope y0_stat y0_log y0_guess y0_newton y0_made y0T_up y0T "
            "y0_row a_up a_made V_made q_a q_g q_w q_h q_v ag_up ag_out ab_made st_z st_zs st_g st_x st_h st_acc "
            "scan_done of_up of_done bs_up bs_done an_up an_dev an_dif an_max dv_row dv_rowed dv_top flag_made "
            "pg_made sums_out sq_in sq_set sq_bias sq_pre sq_g sq_x sq_h sq_sum sq_blk sq_stored "
            "edges_over first_over scan_over"
        ).split():
            s[name] = sem(name)

        x_rows = x.rearrange("(j p s) d -> j p s d", p=P, s=S)
        out_rows = out.rearrange("(j p s) d -> j p s d", p=P, s=S)
        agg_rows = message_sums[0:N, :].rearrange("(j p s) d -> j p s d", p=P, s=S)
        attr_rows = edge_attr.rearrange("(i s p) d -> i p s d", s=S, p=P)
        dst_rows = dst.rearrange("(i r) -> i r", r=R)
        W1v = W1[0:2 * D, :].rearrange("(k p) n -> p k n", p=128)
        W2v = W2.rearrange("(k p) n -> p k n", p=128)
        W3av = W3[0:D, :].rearrange("(k p) n -> p k n", p=128)
        W3bv = W3[D:2 * D, :].rearrange("(k p) n -> p k n", p=128)
        W4v = W4.rearrange("(k p) n -> p k n", p=128)
        EW = 5
        staging = [tmp[:, 0:4, :], tmp[:, 4:8, :]]
        edge_pieces = [
            (W1v[:, 0:KD, :], W1h[:, 0:KD, :], W1l[:, 0:KD, :], 128),
            (W1v[:, KD:2 * KD, :], W1h[:, KD:2 * KD, :], W1l[:, KD:2 * KD, :], 128),
            (W1[2 * D:2 * D + DE, :], W1h[0:DE, 2 * KD, :], W1l[0:DE, 2 * KD, :], DE),
            (W2v, W2h[:, :, :], W2l[:, :, :], 128),
            (W3bv, W3h[:, :, :], W3l[:, :, :], 128),
        ]
        node_pieces = [(W3av, W3ah[:, :, :], W3al[:, :, :]), (W4v, W4h[:, :, :], W4l[:, :, :])]

        def piece_in(n):
            st = staging[n % 2]
            return st[0:DE, 0, :] if edge_pieces[n][3] == DE else st

        SMALLS = 10
        STAGED = ("staged", "staged1")
        FILLS = 20
        FILL_ROWS = message_sums.shape[0] // FILLS
        assert FILL_ROWS == 4 * 128 and FILLS * FILL_ROWS >= N + P
        CHUNKS = [(g, c) for c in range(NC) for g in range(G)]
        STAGES = [(st, c) for st in range(4) for c in range(NC)]

        L3_ORDER = [("z", 0), ("z", 1), ("c", 0), ("z", 2), ("c", 1), ("z", 3), ("c", 2), ("c", 3)]
        O_LOADS = 2 + 2 + 5 * G + G
        O_SET = 6 + G + G * (G - 1) // 2
        STAGE_LAG = 2
        SUM_LAG = 3

        def group_of(g):
            bank = banks[4 + g % 4]
            if g == 2 * S:
                return bank[0:DE, 0:R]
            return bank[:, :].rearrange("p (k c) -> p k c", k=KD)[:, :, 0:P]

        def group_to(g, to):
            if g == 2 * S:
                return to[0:DE, 2 * KD, :]
            side, q = g // S, g % S
            return to[:, side * KD:(side + 1) * KD, q * P:(q + 1) * P]

        def turned_of(bank):
            return banks[bank][:, :].rearrange("p (k c) -> p k c", k=KD)[:, :, 0:P]

        def wait_apart(eng, semaphore, value):
            if isinstance(value, int):
                eng.wait_ge(semaphore, value)
            else:
                held = eng.to_reg(value)
                eng.wait_ge(s["consts_set"], 5)
                eng.wait_ge(semaphore, held)

        block = ctx.enter_context(nc.Block())

        @block.sync
        def _(sp):
            def row(v):
                return v.rearrange("(a n) -> a n", a=1)

            for to, of in (
                (b3_bc[:, :], row(b3).to_broadcast([128, D])),
                (src_all[:, :], src_cols),
                (dst_all[:, :], dst_cols),
                (b1_col[:, :], b1.rearrange("(k p) -> p k", p=128)),
                (b2_col[:, :], b2.rearrange("(k p) -> p k", p=128)),
                (gamma_bc[:, :], row(gamma).to_broadcast([P, D])),
                (beta_bc[:, :], row(beta).to_broadcast([P, D])),
                (b4_bc[:, :], row(b4).to_broadcast([P, D])),
                (steps_rhs[H + 1:H + 2, :], row(F_b3)),
                (steps_rhs[0:H, :], F_W3T),
            ):
                sp.dma_start(to, of, allow_slow_non_contiguous=True).then_inc(s["smalls_in"], 16)
            for n in range(EW):
                if n >= 2:
                    sp.wait_ge(s["split_lo"], n - 1)
                sp.dma_start(piece_in(n), edge_pieces[n][0]).then_inc(s[STAGED[n % 2]], 16)
            sp.dma_start(attr[:, :, :], attr_rows[0]).then_inc(s["attr_in"], 16)
            sp.wait_ge(s["smalls_in"], 16 * SMALLS)
            with sp.Fori(0, FILLS) as f:
                sp.dma_start(
                    message_sums[bass.ds(f * FILL_ROWS, FILL_ROWS), :].rearrange("(p s) d -> p s d", p=128),
                    b3_bc[:, :].unsqueeze(1).to_broadcast([128, S, D]),
                ).then_inc(s["table_filled"], 16)

            def attr_load(i):
                sp.wait_ge(s["groups_up"], NT * i)
                sp.dma_start(attr[:, :, :], attr_rows[i]).then_inc(s["attr_in"], 16)

            def dst_row_load(i):
                sp.dma_start(drow_i[:, :], dst_rows[bass.ds(i, 1), :].to_broadcast([P, R])).then_inc(s["drow_in"], 16)

            attr_load(1)
            dst_row_load(0)
            with sp.Fori(1, NE - 1) as i:
                attr_load(i + 1)
                sp.wait_ge(s["same_made"], S * i)
                dst_row_load(i)
            sp.wait_ge(s["same_made"], S * (NE - 1))
            dst_row_load(NE - 1)
            sp.drain().then_inc(s["edges_over"], 1)
            sp.wait_ge(s["edges_over"], 5)

            for n in range(2):
                sp.dma_start(nstage[:, n, :, :], node_pieces[n][0]).then_inc(s[("n_staged", "n_staged1")[n]], 16)

            def x_load(j):
                sp.dma_start(xraw[0:SPLIT], x_rows[j, 0:SPLIT]).then_inc(s["x_in"], 16)
                sp.dma_start(xraw[SPLIT:P], x_rows[j, SPLIT:P]).then_inc(s["x_in"], 16)

            def agg_load(j):
                sp.dma_start(agg[0:SPLIT], agg_rows[j, 0:SPLIT]).then_inc(s["agg_in"], 16)
                sp.dma_start(agg[SPLIT:P], agg_rows[j, SPLIT:P]).then_inc(s["agg_in"], 16)

            def steps_load(j):
                sp.dma_start(steps_lhs[0:H, :], sums_by_time[:, bass.ds(j * R, R)]).then_inc(s["p_in"], 16)
                sp.dma_start(steps_lhs[H:KV, :], time_rule[H:KV, bass.ds(j * R, R)]).then_inc(s["p_in"], 16)

            def store(j):
                sp.wait_ge(s["out_ready"], S * (j + 1))
                sp.dma_start(out_rows[j, 0:SPLIT], ob[0:SPLIT]).then_inc(s["stored"], 16)
                sp.dma_start(out_rows[j, SPLIT:P], ob[SPLIT:P]).then_inc(s["stored"], 16)

            x_load(0)
            agg_load(0)
            sp.drain().then_inc(s["first_over"], 1)
            sp.wait_ge(s["first_over"], 5)

            sp.dma_start(ruleT[0:H, :], time_rule[0:H, :]).then_inc(s["o_loaded"], 16)
            sp.dma_start(ruleT[H:KV, :], time_rule[H:KV, :]).then_inc(s["o_loaded"], 16)
            sp.wait_ge(s["y0_made"], 1)
            sp.dma_start(steps_rhs[H:H + 1, :], y0[:, :]).then_inc(s["y0_row"], 16)
            sp.wait_ge(s["pg_made"], 1)
            for g in range(G):
                sp.dma_start(sums_by_time[:, g * T:(g + 1) * T], A_base[H * g:H * (g + 1), :]).then_inc(s["sums_out"], 16)
            sp.wait_ge(s["sums_out"], 16 * G)
            sp.wait_ge(s["flag_made"], 1)
            checked = sp.value_load(flag[0:1, 0:1], min_val=0, max_val=1)
            with sp.If(checked == 0):
                with sp.Fori(0, N // C) as b:
                    sp.dma_start(
                        seq_t[:, :], time_rule[KV - 1:KV, bass.ds(b * C, C)].to_broadcast([H, C])
                    ).then_inc(s["sq_in"], 16)
                    wait_apart(sp, s["sq_sum"], (b + 1) * C + 1)
                    sp.dma_start(sums_by_time[:, bass.ds(b * C, C)], seq_blk[:, :]).then_inc(s["sq_stored"], 16)
                    wait_apart(sp, s["sq_stored"], 16 * (b + 1))
            sp.drain().then_inc(s["scan_over"], 1)
            sp.wait_ge(s["scan_over"], 5)

            steps_load(0)
            x_load(1)
            agg_load(1)

            def loads_and_store(j, x_ahead=True, agg_ahead=True, put=True):
                if agg_ahead:
                    sp.wait_ge(s["z_done"], S * (j + 1))
                    agg_load(j + 1)
                if x_ahead:
                    sp.wait_ge(s["xn_done"], S * (j + 2))
                    sp.wait_ge(s["pre_done"], j + 2)
                    x_load(j + 2)
                wait_apart(sp, s["o_up"], S * j)
                steps_load(j)
                if put:
                    store(j - 1)

            sp.wait_ge(s["xn_done"], S * 2)
            sp.wait_ge(s["pre_done"], 2)
            x_load(2)
            store(0)
            loads_and_store(1, put=False)
            with sp.Fori(2, NN - 2) as j:
                loads_and_store(j)
            loads_and_store(NN - 2, x_ahead=False)
            loads_and_store(NN - 1, x_ahead=False, agg_ahead=False)
            store(NN - 1)
            sp.wait_ge(s["stored"], 32 * NN)

        @block.gpsimd
        def _(pool):
            nc.gpsimd.memset(ident[:, :], 0.0).then_inc(s["consts_set"], 1)
            nc.gpsimd.memset(earlier[:, :], 1.0).then_inc(s["consts_set"], 1)
            nc.gpsimd.memset(eps_col[:, :], EPS).then_inc(s["consts_set"], 1)
            nc.gpsimd.memset(one_col[:, :], 1.0).then_inc(s["consts_set"], 1)
            nc.gpsimd.memset(two_col[:, :], 2.0).then_inc(s["consts_set"], 1)
            pool.wait_ge(s["consts_set"], 5)
            nc.gpsimd.affine_select(
                out=ident[:, :], in_=ident[:, :], compare_op=ALU.not_equal, fill=1.0,
                base=0, pattern=[[-1, 128]], channel_multiplier=1,
            ).then_inc(s["diag_made"], 1)
            nc.gpsimd.affine_select(
                out=earlier[:, :], in_=earlier[:, :], compare_op=ALU.is_gt, fill=0.0,
                base=0, pattern=[[-1, P]], channel_multiplier=1,
            ).then_inc(s["diag_made"], 1)
            nc.gpsimd.iota(spare_i[:, :], pattern=[[0, 1]], base=N, channel_multiplier=1).then_inc(s["diag_made"], 1)
            pool.wait_ge(s["diag_made"], 3)
            nc.gpsimd.tensor_copy(spare_row[:, :], spare_i[:, :]).then_inc(s["spare_made"], 1)

            def gather(i):
                nc.gpsimd.tensor_copy(src_cur[:, :], src_all[:, bass.ds(i * S, S)]).then_inc(s["idx_copied"], 1)
                nc.gpsimd.tensor_copy(dst_cur[:, :], dst_all[:, bass.ds(i * S, S)]).then_inc(s["idx_copied"], 1)
                wait_apart(pool, s["idx_copied"], 2 * i + 2)
                for side, idx in ((0, src_cur), (1, dst_cur)):
                    for q in range(S):
                        nc.gpsimd.indirect_dma_start(
                            rows[:, side * S + q, :], None, x[:, :],
                            bass.IndirectOffsetOnAxis(ap=idx[:, q:q + 1], axis=0),
                        ).then_inc(s["rows_in"], 16)

            def scatter(i, first=False):
                pool.wait_ge(s["sumrow_made"], i + 1)
                for q in range(S):
                    pool.wait_ge(s["c_out"], S * i + q + 1)
                    if not (first and q == 0):
                        wait_apart(pool, s["scattered"], 16 * (S * i + q))
                    nc.gpsimd.indirect_dma_start(
                        message_sums[:, :], bass.IndirectOffsetOnAxis(ap=sum_row_i[:, q:q + 1], axis=0),
                        zsum[:, q, :], None, compute_op=ALU.add,
                    ).then_inc(s["scattered"], 16)

            pool.wait_ge(s["smalls_in"], 16 * SMALLS)
            gather(0)
            pool.wait_ge(s["groups_up"], NT)
            gather(1)
            pool.wait_ge(s["groups_up"], 2 * NT)
            gather(2)
            pool.wait_ge(s["table_filled"], 16 * FILLS)
            scatter(0, first=True)
            pool.wait_ge(s["groups_up"], 3 * NT)
            gather(3)
            with pool.Fori(2, NE - 2) as i:
                scatter(i - 1)
                pool.wait_ge(s["groups_up"], NT * (i + 2))
                gather(i + 2)
            for i in range(NE - 2, NE + 1):
                scatter(i - 1)
            pool.wait_ge(s["scattered"], 16 * S * NE)
            pool.drain().then_inc(s["edges_over"], 1)
            pool.wait_ge(s["edges_over"], 5)

            def x_plus(j, b, peeled=False):
                pool.wait_ge(s["x_in"], 32 * (j + 1))
                if not peeled:
                    pool.wait_ge(s["out_ready"], S * (j - 1))
                nc.gpsimd.tensor_tensor(
                    pre[:, b], xraw[:, :, :], beta_bc[:, :].unsqueeze(1).to_broadcast([P, S, D]), ALU.add
                ).then_inc(s["pre_done"], 1)

            def norm_plus(j, b, peeled=False):
                pool.wait_ge(s["xn_done"], S * (j + 1))
                if not peeled:
                    pool.wait_ge(s["y_added"], S * (j - 1))
                nc.gpsimd.tensor_tensor(
                    xnb[:, b], xn[:, :, :], b4_bc[:, :].unsqueeze(1).to_broadcast([P, S, D]), ALU.add
                ).then_inc(s["xnb_done"], 1)

            def times_gamma(j):
                for q in range(S):
                    pool.wait_ge(s["yn_done"], S * j + q + 1)
                    nc.gpsimd.tensor_tensor(yb[:, q, :], yb[:, q, :], gamma_bc[:, :], ALU.mult).then_inc(s["yg_done"], 1)

            def result(j, b):
                pool.wait_ge(s["stored"], 32 * j)
                for q in range(S):
                    pool.wait_ge(s["o_added"], S * j + q + 1)
                    nc.gpsimd.tensor_tensor(ob[:, q, :], yb[:, q, :], pre[:, b, q, :], ALU.add).then_inc(s["out_ready"], 1)

            x_plus(0, 0, peeled=True)
            norm_plus(0, 0, peeled=True)
            times_gamma(0)
            pool.wait_ge(s["yg_done"], S)
            nc.gpsimd.tensor_tensor(x1_first[:, :, :], yb[:, :, :], pre[:, 0], ALU.add).then_inc(s["first_done"], 1)
            pool.drain().then_inc(s["first_over"], 1)
            pool.wait_ge(s["first_over"], 5)

            nc.gpsimd.memset(blocks[:, :], 0.0).then_inc(s["o_set"], 1)
            nc.gpsimd.memset(groups_before[:, :], 0.0).then_inc(s["o_set"], 1)
            nc.gpsimd.memset(fW2[:, :], 0.0).then_inc(s["o_set"], 1)
            nc.gpsimd.memset(V[:, :], 0.0).then_inc(s["o_set"], 1)
            nc.gpsimd.memset(zeros[:, :], 0.0).then_inc(s["o_set"], 1)
            nc.gpsimd.memset(Pex[:, 0:1], 0.0).then_inc(s["o_set"], 1)
            pool.wait_ge(s["o_set"], 6)
            for g in range(G):
                nc.gpsimd.memset(blocks[H * g:H * (g + 1), H * g:H * (g + 1)], 1.0).then_inc(s["o_set"], 1)
                for later in range(g + 1, G):
                    nc.gpsimd.tensor_copy(
                        groups_before[H * g:H * (g + 1), H * later:H * (later + 1)],
                        ident[H * g:H * (g + 1), H * g:H * (g + 1)],
                    ).then_inc(s["o_set"], 1)
            pool.drain().then_inc(s["scan_over"], 1)
            pool.wait_ge(s["scan_over"], 5)

            x_plus(1, 1, peeled=True)
            norm_plus(1, 1, peeled=True)
            for q in range(S):
                pool.wait_ge(s["o_added"], q + 1)
                nc.gpsimd.tensor_copy(ob[:, q, :], yb[:, q, :]).then_inc(s["out_ready"], 1)

            def nodes(j, b, ahead=True, behind=True):
                if behind:
                    times_gamma(j - 1)
                if ahead:
                    norm_plus(j + 1, 1 - b)
                if behind:
                    result(j - 1, 1 - b)
                if ahead:
                    x_plus(j + 1, 1 - b)

            nodes(1, 1, behind=False)
            with pool.Fori(2, NN - 2, 2) as j:
                nodes(j, 0)
                nodes(j + 1, 1)
            nodes(NN - 2, 0)
            nodes(NN - 1, 1, ahead=False)
            times_gamma(NN - 1)
            result(NN - 1, 1)

        @block.scalar
        def _(act):
            def split_high(n, to, of):
                nc.scalar.activation(to, of, ACT.Copy).then_inc(s["split_hi"], 1)

            act.preload_act_table_set("natural_log_exp_and_others")
            act.wait_ge(s["consts_set"], 5)
            for n in range(EW):
                act.wait_ge(s[STAGED[n % 2]], 16 * (n // 2 + 1))
                split_high(n, edge_pieces[n][1], piece_in(n))

            def rows_rstd(i):
                act.wait_ge(s["aggr_done"], 2 * S * (i + 1))
                nc.scalar.activation(e_lnv[:, :], e_mv[:, :, 1], ACT.Ln, bias=eps_col[0:P, :]).then_inc(s["ln_log"], 1)
                act.wait_ge(s["ln_log"], i + 1)
                nc.scalar.activation(e_rstd[:, :], e_lnv[:, :], ACT.Exp, scale=-0.5).then_inc(s["ln_guess"], 1)

            def groups(i):
                for g in range(NT):
                    act.wait_ge(s["groups_up"], NT * i + g + 1)
                    nc.scalar.activation(group_to(g, fTh), group_of(g), ACT.Copy).then_inc(s["group_hi"], 1)

            def layer(i, which, bias, hi, between=None, first=False):
                n0 = 2 * KD * i + KD * which
                for step in range(KD + 2):
                    if step < KD:
                        n, k = n0 + step, step % 2
                        act.wait_ge(s["layer_up"], n + 1)
                        if not (first and step < 2):
                            act.wait_ge(s["t_done"], n - 1)
                        nc.scalar.activation(tmp[:, k, 0:R], banks[step][:, 0:R], ACT.Exp,
                                             bias=bias[:, step:step + 1]).then_inc(s["exp_done"], 1)
                    if 1 <= step <= KD:
                        n, k = n0 + step - 1, (step - 1) % 2
                        act.wait_ge(s["t_done"], n + 1)
                        if not (first and step < 3):
                            act.wait_ge(s["m_done"], n - 1)
                        nc.scalar.activation(tmp[:, 4 + k, 0:R], tmp[:, 2 + k, 0:R], ACT.Ln,
                                             bias=two_col[:, :]).then_inc(s["log_done"], 1)
                        act.wait_ge(s["log_done"], n + 1)
                        nc.scalar.activation(tmp[:, 4 + k, 0:R], tmp[:, 4 + k, 0:R], ACT.Exp,
                                             scale=-1.0).then_inc(s["r_done"], 1)
                    if step >= 2:
                        n, k = n0 + step - 2, (step - 2) % 2
                        act.wait_ge(s["m_done"], n + 1)
                        nc.scalar.activation(hi[:, step - 2, :], tmp[:, 6 + k, 0:R], ACT.Copy).then_inc(s["hi_done"], 1)
                    if step == 2 and between:
                        between()

            def sums(i, first=False):
                for kind, q in L3_ORDER:
                    n = S * i + q
                    if kind == "z":
                        act.wait_ge(s["z_up"], n + 1)
                        if not (first and q < 2):
                            act.wait_ge(s["c_up"], n - 1)
                        nc.scalar.activation(zh[:, q % 2, :], banks[4 + q % 2][0:P, :], ACT.Copy).then_inc(s["z_hi"], 1)
                    else:
                        act.wait_ge(s["c_up"], n + 1)
                        if not first:
                            act.wait_ge(s["scattered"], 16 * S * i)
                        nc.scalar.activation(zsum[:, q, :], banks[6 + q % 2][0:P, :], ACT.Copy).then_inc(s["c_out"], 1)

            rows_rstd(0)
            groups(0)
            layer(0, 0, b1_col, h1h, between=lambda: rows_rstd(1), first=True)
            groups(1)
            layer(0, 1, b2_col, msgh)
            layer(1, 0, b1_col, h1h, between=lambda: rows_rstd(2))
            sums(0, first=True)
            groups(2)
            layer(1, 1, b2_col, msgh)
            with act.Fori(2, NE - 1) as i:
                layer(i, 0, b1_col, h1h, between=lambda: rows_rstd(i + 1))
                sums(i - 1)
                groups(i + 1)
                layer(i, 1, b2_col, msgh)
            layer(NE - 1, 0, b1_col, h1h)
            sums(NE - 2)
            layer(NE - 1, 1, b2_col, msgh)
            sums(NE - 1)
            act.drain().then_inc(s["edges_over"], 1)
            act.wait_ge(s["edges_over"], 5)

            for n in range(2):
                act.wait_ge(s[("n_staged", "n_staged1")[n]], 16)
                nc.scalar.activation(node_pieces[n][1], nstage[:, n, :, :], ACT.Copy).then_inc(s["n_hi"], 1)

            def rstd(j, made, stats, small, log, guess):
                act.wait_ge(s[made], S * (j + 1))
                nc.scalar.activation(small[:, 0, :], stats[:, :, 1], ACT.Ln, bias=eps_col[0:P, :]).then_inc(s[log], 1)
                act.wait_ge(s[log], j + 1)
                nc.scalar.activation(small[:, 1, :], small[:, 0, :], ACT.Exp, scale=-0.5).then_inc(s[guess], 1)

            def x_rstd(j):
                rstd(j, "xa_done", mvx, smx, "xl_log", "xl_guess")

            def y_rstd(j):
                rstd(j, "ya_done", mvy, smy, "yl_log", "yl_guess")

            def turned(j, up, done, bank, to):
                for q in range(S):
                    act.wait_ge(s[up], S * j + q + 1)
                    nc.scalar.activation(to[:, q, :, 0:P], turned_of(bank), ACT.Copy).then_inc(s[done], 1)

            def unit(j, peeled=False):
                for step in range(S + 1):
                    if step < S:
                        n, k = S * j + step, step % 2
                        act.wait_ge(s["z_done"], n + 1)
                        if not (peeled and step < 2):
                            act.wait_ge(s["nt_done"], n - 1)
                        nc.scalar.activation(ne[:, k, :], nz[:, k, :], ACT.Exp).then_inc(s["ne_done"], 1)
                    if step >= 1:
                        n, k = S * j + step - 1, (step - 1) % 2
                        act.wait_ge(s["nt_done"], n + 1)
                        if not (peeled and step < 3):
                            act.wait_ge(s["u_done"], n - 1)
                        nc.scalar.activation(nr[:, k, :], nt[:, k, :], ACT.Ln, bias=two_col[0:P, :]).then_inc(s["nl_done"], 1)
                        act.wait_ge(s["nl_done"], n + 1)
                        nc.scalar.activation(nr[:, k, :], nr[:, k, :], ACT.Exp, scale=-1.0).then_inc(s["nr_done"], 1)

            x_rstd(0)
            turned(0, "xt_up", "xt_hi", 4, xTh)
            unit(0, peeled=True)
            turned(0, "ut_up", "ut_hi", 5, uTh)
            y_rstd(0)
            act.drain().then_inc(s["first_over"], 1)
            act.wait_ge(s["first_over"], 5)

            for to, of in (
                [(rule[:, :], node_rule), (fb3[:, :], F_b3.rearrange("(k p) -> p k", p=128))]
                + [(fW1T[:, :, H * g:H * (g + 1)], F_W1T.rearrange("(k p) h -> p k h", p=128)) for g in range(G)]
                + [(fW3[:, :, H * g:H * (g + 1)], F_W3.rearrange("(k p) h -> p k h", p=128)) for g in range(G)]
                + [(fb1[H * g:H * (g + 1), :], F_b1.rearrange("(h a) -> h a", a=1)) for g in range(G)]
                + [(fb2[H * g:H * (g + 1), :], F_b2.rearrange("(h a) -> h a", a=1)) for g in range(G)]
                + [(times[H * g:H * (g + 1), :], time_rule[KV - 1:KV, g * T:(g + 1) * T].to_broadcast([H, T]))
                   for g in range(G)]
            ):
                act.dma_start(to, of, allow_slow_non_contiguous=True).then_inc(s["o_loaded"], 16)
            act.wait_ge(s["o_set"], 6)
            for g in range(G):
                act.dma_start(fW2[H * g:H * (g + 1), H * g:H * (g + 1)], F_W2T).then_inc(s["o_loaded"], 16)
            act.wait_ge(s["y0_stat"], 2)
            nc.scalar.activation(y0_s[:, 0:1], y0_mv[:, 1:2], ACT.Ln, bias=eps_col[0:1, :]).then_inc(s["y0_log"], 1)
            act.wait_ge(s["y0_log"], 1)
            nc.scalar.activation(y0_s[:, 1:2], y0_s[:, 0:1], ACT.Exp, scale=-0.5).then_inc(s["y0_guess"], 1)
            act.wait_ge(s["o_loaded"], 16 * O_LOADS)
            with act.Fori(0, PICARD) as it:
                act.wait_ge(s["q_a"], it + 1)
                nc.scalar.activation(gq[:, :], banks[0][0:H, 0:NQ], ACT.Tanh, bias=fb1[0:H, :]).then_inc(s["q_g"], 1)
                act.wait_ge(s["q_w"], it + 1)
                nc.scalar.activation(hq[:, :], banks[1][0:H, 0:NQ], ACT.Tanh, bias=fb2[0:H, :]).then_inc(s["q_h"], 1)
            act.wait_ge(s["o_slope"], 3)
            for n in range(len(STAGES) + STAGE_LAG):
                if n < len(STAGES):
                    st, c = STAGES[n]
                    bias = (fb1, bias_half, bias_half, bias_full)[st]
                    if n >= 4:
                        act.wait_ge(s["st_x"], n - 3)
                    if st == 0:
                        act.wait_ge(s["ag_out"], c + 1)
                        of = A_guess[:, c * C:(c + 1) * C]
                    else:
                        act.wait_ge(s["st_zs"], n - NC + 1)
                        of = zst[:, n % 2, :]
                    nc.scalar.activation(gst[:, n % 4, :], of, ACT.Tanh, bias=bias[:, :]).then_inc(s["st_g"], 1)
                if n >= STAGE_LAG:
                    m = n - STAGE_LAG
                    st, c = STAGES[m]
                    act.wait_ge(s["st_x"], m + 1)
                    if st > 0:
                        act.wait_ge(s["st_acc"], m - NC + 1)
                    nc.scalar.activation(hst[:, c, :], banks[4 + m % 4][:, 0:C], ACT.Tanh, bias=fb2[:, :]).then_inc(s["st_h"], 1)
            act.wait_ge(s["flag_made"], 1)
            checked = act.value_load(flag[0:1, 0:1], min_val=0, max_val=1)
            with act.If(checked == 0):
                with act.Fori(0, N) as t:
                    act.wait_ge(s["sq_bias"], t + 1)
                    for st in range(4):
                        act.wait_ge(s["sq_pre"], 4 * t + st + 1)
                        nc.scalar.activation(seq_g[:, :], banks[0][0:H, 0:1], ACT.Tanh,
                                             bias=seq_bias[:, (0, 1, 1, 2)[st]:(0, 1, 1, 2)[st] + 1]).then_inc(s["sq_g"], 1)
                        act.wait_ge(s["sq_x"], 4 * t + st + 1)
                        nc.scalar.activation(seq_h[:, st:st + 1], banks[1][0:H, 0:1], ACT.Tanh,
                                             bias=fb2[0:H, :]).then_inc(s["sq_h"], 1)
            act.drain().then_inc(s["scan_over"], 1)
            act.wait_ge(s["scan_over"], 5)

            act.preload_act_table_set("natural_log_exp_and_others")
            x_rstd(1)
            turned(1, "xt_up", "xt_hi", 4, xTh)

            def nodes(j, ahead=True, behind=True):
                unit(j)
                if behind:
                    y_rstd(j - 1)
                if ahead:
                    x_rstd(j + 1)
                    turned(j + 1, "xt_up", "xt_hi", 4, xTh)
                turned(j, "ut_up", "ut_hi", 5, uTh)

            nodes(1, behind=False)
            with act.Fori(2, NN - 1) as j:
                nodes(j)
            nodes(NN - 1, ahead=False)
            y_rstd(NN - 1)

        @block.vector
        def _(dve):
            dve.wait_ge(s["smalls_in"], 16 * SMALLS)
            nc.vector.tensor_copy(dst_allf[:, :], dst_all[:, :]).then_inc(s["dstf_made"], 1)
            for n in range(EW):
                _, hi, lo, _ = edge_pieces[n]
                dve.wait_ge(s["split_hi"], n + 1)
                nc.vector.tensor_tensor(lo, piece_in(n), hi.bitcast(f32), ALU.subtract).then_inc(s["split_lo"], 1)
            dve.wait_ge(s["dstf_made"], 1)
            dve.wait_ge(s["spare_made"], 1)

            def refine(small, var, chain, count):
                v, r, sq = small
                nc.vector.tensor_scalar(v, var, EPS, None, ALU.add).then_inc(s[chain], 1)
                nc.vector.tensor_tensor(sq, r, r, ALU.mult).then_inc(s[chain], 1)
                dve.wait_ge(s[chain], count + 2)
                nc.vector.tensor_tensor(sq, sq, v, ALU.mult).then_inc(s[chain], 1)
                dve.wait_ge(s[chain], count + 3)
                nc.vector.tensor_scalar(sq, sq, -0.5, 1.5, ALU.mult, ALU.add).then_inc(s[chain], 1)
                dve.wait_ge(s[chain], count + 4)
                nc.vector.tensor_tensor(r, r, sq, ALU.mult).then_inc(s[chain], 1)
                dve.wait_ge(s[chain], count + 5)

            def norm_rows(i):
                dve.wait_ge(s["rows_in"], 16 * 2 * S * (i + 1))
                for a in range(2 * S):
                    nc.vector.bn_stats(e_stats[:, a, :], rows[:, a, :]).then_inc(s["stats_done"], 1)
                wait_apart(dve, s["stats_done"], 2 * S * (i + 1))
                for a in range(2 * S):
                    nc.vector.bn_aggr(e_mv[:, a, :], e_stats[:, a, :]).then_inc(s["aggr_done"], 1)
                dve.wait_ge(s["aggr_done"], 2 * S * (i + 1))
                dve.wait_ge(s["ln_guess"], i + 1)
                refine((e_var[:, :], e_rstd[:, :], e_sq[:, :]), e_mv[:, :, 1], "newton", 5 * i)
                for a in range(2 * S):
                    nc.vector.tensor_scalar(rows[:, a, :], rows[:, a, :], e_mv[:, a, 0:1], e_rstd[:, a:a + 1],
                                            ALU.subtract, ALU.mult).then_inc(s["rows_normed"], 1)

            def groups(i):
                for g in range(NT):
                    dve.wait_ge(s["group_hi"], NT * i + g + 1)
                    nc.vector.tensor_tensor(group_to(g, fTl), group_of(g), group_to(g, fTh).bitcast(f32),
                                            ALU.subtract).then_inc(s["group_lo"], 1)

            def layer(i, which, bias, hi, lo, between=None, first=False):
                n0 = 2 * KD * i + KD * which
                for step in range(KD + 2):
                    if step < KD:
                        n, k = n0 + step, step % 2
                        e, t = tmp[:, k, 0:R], tmp[:, 2 + k, 0:R]
                        dve.wait_ge(s["exp_done"], n + 1)
                        nc.vector.tensor_scalar(e, e, EXP_MAX, None, ALU.min).then_inc(s["cut_done"], 1)
                        dve.wait_ge(s["cut_done"], n + 1)
                        if not (first and step < 2):
                            dve.wait_ge(s["log_done"], n - 1)
                            dve.wait_ge(s["w_done"], n - 1)
                        nc.vector.scalar_tensor_tensor(t, e, 2.0, e, ALU.add, ALU.mult).then_inc(s["t_done"], 1)
                    if 1 <= step <= KD:
                        n, k, m = n0 + step - 1, (step - 1) % 2, step - 1
                        t, r, v = tmp[:, 2 + k, 0:R], tmp[:, 4 + k, 0:R], tmp[:, 6 + k, 0:R]
                        dve.wait_ge(s["t_done"], n + 1)
                        if not (first and step < 3):
                            dve.wait_ge(s["lo_done"], n - 1)
                        nc.vector.scalar_tensor_tensor(v, banks[m][:, 0:R], bias[:, m:m + 1], t, ALU.add,
                                                       ALU.mult).then_inc(s["w_done"], 1)
                        dve.wait_ge(s["w_done"], n + 1)
                        dve.wait_ge(s["r_done"], n + 1)
                        nc.vector.tensor_tensor(v, v, r, ALU.mult).then_inc(s["m_done"], 1)
                    if step >= 2:
                        n, k = n0 + step - 2, (step - 2) % 2
                        dve.wait_ge(s["hi_done"], n + 1)
                        nc.vector.tensor_tensor(lo[:, step - 2, :], tmp[:, 6 + k, 0:R], hi[:, step - 2, :].bitcast(f32),
                                                ALU.subtract).then_inc(s["lo_done"], 1)
                    if step == 2 and between:
                        between()

            def segments(i, first=False):
                dve.wait_ge(s["drow_in"], 16 * (i + 1))
                nc.vector.tensor_copy(drow_f[:, :], drow_i[:, :]).then_inc(s["seg"], 1)
                nc.vector.tensor_copy(dcol_f[:, :], dst_allf[:, bass.ds(i * S, S)]).then_inc(s["seg"], 1)
                dve.wait_ge(s["seg"], 7 * i + 2)
                if not first:
                    dve.wait_ge(s["c_up"], S * i)
                for q in range(S):
                    nc.vector.tensor_scalar(same[:, q, 0:P], drow_f[:, q * P:(q + 1) * P], dcol_f[:, q:q + 1], None,
                                            ALU.is_equal).then_inc(s["same_made"], 1)
                dve.wait_ge(s["same_made"], S * (i + 1))
                nc.vector.tensor_tensor(same_earlier[:, :, :], same[:, :, 0:P].bitcast(f32),
                                        earlier[:, :].unsqueeze(1).to_broadcast([P, S, P]), ALU.mult).then_inc(s["seg"], 1)
                dve.wait_ge(s["seg"], 7 * i + 3)
                nc.vector.tensor_reduce(n_earlier[:, :], same_earlier[:, :, :], AX.X, ALU.add).then_inc(s["seg"], 1)
                nc.vector.tensor_scalar(to_spare[:, :], dcol_f[:, :], -1.0, spare_row[:, :], ALU.mult, ALU.add).then_inc(s["seg"], 1)
                dve.wait_ge(s["seg"], 7 * i + 5)
                nc.vector.tensor_scalar(n_earlier[:, :], n_earlier[:, :], 1.0, None, ALU.min).then_inc(s["seg"], 1)
                dve.wait_ge(s["seg"], 7 * i + 6)
                nc.vector.tensor_tensor(sum_row[:, :], to_spare[:, :], n_earlier[:, :], ALU.mult).then_inc(s["seg"], 1)
                dve.wait_ge(s["seg"], 7 * i + 7)
                if not first:
                    dve.wait_ge(s["scattered"], 16 * S * i)
                nc.vector.tensor_tensor(sum_row_i[:, :], sum_row[:, :], dcol_f[:, :], ALU.add).then_inc(s["sumrow_made"], 1)

            def z_low(i):
                for q in range(S):
                    n = S * i + q
                    dve.wait_ge(s["z_hi"], n + 1)
                    nc.vector.tensor_tensor(zl[:, q % 2, :], banks[4 + q % 2][0:P, :], zh[:, q % 2, :].bitcast(f32),
                                            ALU.subtract).then_inc(s["z_lo"], 1)

            norm_rows(0)
            groups(0)
            layer(0, 0, b1_col, h1h, h1l, between=lambda: norm_rows(1), first=True)
            groups(1)
            layer(0, 1, b2_col, msgh, msgl)
            layer(1, 0, b1_col, h1h, h1l, between=lambda: norm_rows(2))
            segments(0, first=True)
            z_low(0)
            groups(2)
            layer(1, 1, b2_col, msgh, msgl)
            with dve.Fori(2, NE - 1) as i:
                layer(i, 0, b1_col, h1h, h1l, between=lambda: norm_rows(i + 1))
                segments(i - 1)
                z_low(i - 1)
                groups(i + 1)
                layer(i, 1, b2_col, msgh, msgl)
            layer(NE - 1, 0, b1_col, h1h, h1l)
            segments(NE - 2)
            z_low(NE - 2)
            layer(NE - 1, 1, b2_col, msgh, msgl)
            segments(NE - 1)
            z_low(NE - 1)
            dve.drain().then_inc(s["edges_over"], 1)
            dve.wait_ge(s["edges_over"], 5)

            for n in range(2):
                _, hi, lo = node_pieces[n]
                dve.wait_ge(s["n_hi"], n + 1)
                nc.vector.tensor_tensor(lo, nstage[:, n, :, :], hi.bitcast(f32), ALU.subtract).then_inc(s["n_lo"], 1)

            def x_norm(j, first=False):
                dve.wait_ge(s["x_in"], 32 * (j + 1))
                for q in range(S):
                    nc.vector.bn_stats(stx[:, q, :], xraw[:, q, :]).then_inc(s["xs_done"], 1)
                wait_apart(dve, s["xs_done"], S * (j + 1))
                for q in range(S):
                    nc.vector.bn_aggr(mvx[:, q, :], stx[:, q, :]).then_inc(s["xa_done"], 1)
                dve.wait_ge(s["xa_done"], S * (j + 1))

            def x_scale(j, first=False):
                dve.wait_ge(s["xl_guess"], j + 1)
                refine((smx[:, 2, :], smx[:, 1, :], smx[:, 3, :]), mvx[:, :, 1], "xl_newton", 5 * j)
                if not first:
                    dve.wait_ge(s["xt_up"], S * j)
                    dve.wait_ge(s["xnb_done"], j)
                for q in range(S):
                    nc.vector.tensor_scalar(xn[:, q, :], xraw[:, q, :], mvx[:, q, 0:1], smx[:, 1, q:q + 1],
                                            ALU.subtract, ALU.mult).then_inc(s["xn_done"], 1)

            def y_norm(j, b):
                dve.wait_ge(s["xnb_done"], j + 1)
                for q in range(S):
                    dve.wait_ge(s["y_up"], S * j + q + 1)
                    nc.vector.tensor_tensor(yb[:, q, :], banks[2 + q % 2][0:P, :], xnb[:, b, q, :], ALU.add).then_inc(s["y_added"], 1)
                dve.wait_ge(s["y_added"], S * (j + 1))
                for q in range(S):
                    nc.vector.bn_stats(sty[:, q, :], yb[:, q, :]).then_inc(s["ys_done"], 1)
                wait_apart(dve, s["ys_done"], S * (j + 1))
                for q in range(S):
                    nc.vector.bn_aggr(mvy[:, q, :], sty[:, q, :]).then_inc(s["ya_done"], 1)
                dve.wait_ge(s["ya_done"], S * (j + 1))

            def y_scale(j):
                dve.wait_ge(s["yl_guess"], j + 1)
                refine((smy[:, 2, :], smy[:, 1, :], smy[:, 3, :]), mvy[:, :, 1], "yl_newton", 5 * j)
                for q in range(S):
                    nc.vector.tensor_scalar(yb[:, q, :], yb[:, q, :], mvy[:, q, 0:1], smy[:, 1, q:q + 1],
                                            ALU.subtract, ALU.mult).then_inc(s["yn_done"], 1)

            def turned(j, high, done, bank, hi, lo):
                for q in range(S):
                    dve.wait_ge(s[high], S * j + q + 1)
                    nc.vector.tensor_tensor(lo[:, q, :, 0:P], turned_of(bank), hi[:, q, :, 0:P].bitcast(f32),
                                            ALU.subtract).then_inc(s[done], 1)

            def unit(j, peeled=False):
                dve.wait_ge(s["agg_in"], 32 * (j + 1))
                for step in range(S + 2):
                    if step >= 2:
                        n, k, q = S * j + step - 2, (step - 2) % 2, step - 2
                        dve.wait_ge(s["nt_done"], n + 1)
                        if not peeled:
                            dve.wait_ge(s["ut_up"], S * j)
                        nc.vector.tensor_tensor(u[:, q, :], nz[:, k, :], nt[:, k, :], ALU.mult).then_inc(s["nw_done"], 1)
                        dve.wait_ge(s["nw_done"], n + 1)
                        dve.wait_ge(s["nr_done"], n + 1)
                        nc.vector.tensor_tensor(u[:, q, :], u[:, q, :], nr[:, k, :], ALU.mult).then_inc(s["u_done"], 1)
                    if step < S:
                        n, k = S * j + step, step % 2
                        dve.wait_ge(s["u_up"], n + 1)
                        if not (peeled and step < 2):
                            dve.wait_ge(s["ne_done"], n - 1)
                            dve.wait_ge(s["nw_done"], n - 1)
                        nc.vector.tensor_tensor(nz[:, k, :], banks[k][0:P, :], agg[:, step, :], ALU.add).then_inc(s["z_done"], 1)
                    if 1 <= step <= S:
                        n, k = S * j + step - 1, (step - 1) % 2
                        dve.wait_ge(s["ne_done"], n + 1)
                        nc.vector.tensor_scalar(ne[:, k, :], ne[:, k, :], EXP_MAX, None, ALU.min).then_inc(s["nc_done"], 1)
                        dve.wait_ge(s["nc_done"], n + 1)
                        if not (peeled and step < 3):
                            dve.wait_ge(s["nl_done"], n - 1)
                            dve.wait_ge(s["nw_done"], n - 1)
                        nc.vector.scalar_tensor_tensor(nt[:, k, :], ne[:, k, :], 2.0, ne[:, k, :], ALU.add,
                                                       ALU.mult).then_inc(s["nt_done"], 1)

            x_norm(0)
            x_scale(0, first=True)
            turned(0, "xt_hi", "xt_lo", 4, xTh, xTl)
            unit(0, peeled=True)
            turned(0, "ut_hi", "ut_lo", 5, uTh, uTl)
            y_norm(0, 0)
            y_scale(0)
            dve.wait_ge(s["first_done"], 1)
            dve.drain().then_inc(s["first_over"], 1)
            dve.wait_ge(s["first_over"], 5)

            nc.vector.bn_stats(y0_st[:, :], x1_first[0:1, 0, :]).then_inc(s["y0_stat"], 1)
            dve.wait_ge(s["y0_stat"], 1)
            nc.vector.bn_aggr(y0_mv[:, :], y0_st[:, :]).then_inc(s["y0_stat"], 1)
            dve.wait_ge(s["y0_stat"], 2)
            dve.wait_ge(s["y0_guess"], 1)
            refine((y0_s[:, 2:3], y0_s[:, 1:2], y0_s[:, 3:4]), y0_mv[:, 1:2], "y0_newton", 0)
            nc.vector.tensor_scalar(y0[:, :], x1_first[0:1, 0, :], y0_mv[:, 0:1], y0_s[:, 1:2],
                                    ALU.subtract, ALU.mult).then_inc(s["y0_made"], 1)
            dve.wait_ge(s["o_loaded"], 16 * O_LOADS)
            dve.wait_ge(s["o_set"], O_SET)
            dve.wait_ge(s["o_mat_up"], 1)
            nc.vector.tensor_copy(M_T[:, :], banks[0][0:H, 0:H]).then_inc(s["o_mats"], 1)
            for to, scale in ((M_half, DT / 2), (M_full, DT), (M_six, DT / 6)):
                nc.vector.scalar_tensor_tensor(to[:, :], banks[0][:, 0:128], scale, blocks[:, :], ALU.mult,
                                               ALU.mult).then_inc(s["o_mats"], 1)
            dve.wait_ge(s["o_slope_up"], 1)
            nc.vector.tensor_copy(slope[:, :], banks[1][:, 0:1]).then_inc(s["o_slope"], 1)
            dve.wait_ge(s["o_slope"], 1)
            nc.vector.tensor_scalar(bias_half[:, :], slope[:, :], DT / 2, fb1[:, :], ALU.mult, ALU.add).then_inc(s["o_slope"], 1)
            nc.vector.tensor_scalar(bias_full[:, :], slope[:, :], DT, fb1[:, :], ALU.mult, ALU.add).then_inc(s["o_slope"], 1)
            nc.vector.tensor_copy(y0b3[:, :, 1], fb3[:, :]).then_inc(s["y0T"], 1)
            dve.wait_ge(s["y0T_up"], 1)
            nc.vector.tensor_copy(y0b3[:, :, 0], banks[2][:, 0:KD]).then_inc(s["y0T"], 1)
            dve.wait_ge(s["a_up"], 2)
            nc.vector.tensor_copy(a0[:, :], banks[3][:, 0:1]).then_inc(s["a_made"], 1)
            nc.vector.tensor_copy(V[H:KV, :], banks[4][H:KV, 0:H]).then_inc(s["V_made"], 1)
            with dve.Fori(0, PICARD) as it:
                dve.wait_ge(s["q_v"], it + 1)
                nc.vector.tensor_copy(V[0:NQ, :], banks[2][0:NQ, 0:H]).then_inc(s["V_made"], 1)
            for c in range(NC):
                dve.wait_ge(s["ag_up"], c + 1)
                nc.vector.tensor_copy(A_guess[:, c * C:(c + 1) * C], banks[c % 4][:, 0:C]).then_inc(s["ag_out"], 1)
            for n in range(NC, len(STAGES) + SUM_LAG):
                if n < len(STAGES):
                    st, c = STAGES[n]
                    dve.wait_ge(s["st_z"], n - NC + 1)
                    dve.wait_ge(s["ag_out"], c + 1)
                    if n >= NC + 2:
                        dve.wait_ge(s["st_g"], n - 1)
                    nc.vector.tensor_tensor(zst[:, n % 2, :], banks[n % 4][:, 0:C], A_guess[:, c * C:(c + 1) * C],
                                            ALU.add).then_inc(s["st_zs"], 1)
                for m in ((n - SUM_LAG,) if n > NC else range(n - SUM_LAG + 1)):
                    st, c = STAGES[m]
                    dve.wait_ge(s["st_h"], m + 1)
                    h, S_c = hst[:, c, :], Ssum[:, c, :]
                    if st > 0:
                        dve.wait_ge(s["st_acc"], m - NC + 1)
                    if st == 0:
                        op = nc.vector.tensor_copy(S_c, h)
                    elif st < 3:
                        op = nc.vector.scalar_tensor_tensor(S_c, h, 2.0, S_c, ALU.mult, ALU.add)
                    else:
                        op = nc.vector.tensor_tensor(S_c, h, S_c, ALU.add)
                    op.then_inc(s["st_acc"], 1)
            for c in range(NC):
                dve.wait_ge(s["st_acc"], 3 * NC + c + 1)
                if c:
                    dve.wait_ge(s["scan_done"], c)
                nc.vector.tensor_tensor_scan(Pex[:, 1 + c * C:1 + (c + 1) * C], zeros[:, :], Ssum[:, c, :],
                                             Pex[:, c * C:c * C + 1], ALU.add, ALU.add).then_inc(s["scan_done"], 1)
            dve.wait_ge(s["of_up"], 1)
            nc.vector.tensor_copy(off[:, :], banks[4][:, 0:1]).then_inc(s["of_done"], 1)
            dve.wait_ge(s["bs_up"], 1)
            dve.wait_ge(s["a_made"], 1)
            nc.vector.tensor_tensor(base[:, :], banks[5][:, 0:1], a0[:, :], ALU.add).then_inc(s["bs_done"], 1)
            dve.wait_ge(s["bs_done"], 1)
            nc.vector.tensor_scalar(A_base[:, :], times[:, :], slope[:, :], base[:, :], ALU.mult, ALU.add).then_inc(s["ab_made"], 1)
            dve.wait_ge(s["ab_made"], 1)
            for c in range(NC):
                dve.wait_ge(s["an_up"], c + 1)
                if c >= 2:
                    dve.wait_ge(s["an_max"], c - 1)
                nc.vector.tensor_tensor(dev[:, c % 2, :], banks[c % 4][:, 0:C], A_base[:, c * C:(c + 1) * C],
                                        ALU.add).then_inc(s["an_dev"], 1)
                dve.wait_ge(s["an_dev"], c + 1)
                nc.vector.tensor_tensor(dev[:, c % 2, :], dev[:, c % 2, :], A_guess[:, c * C:(c + 1) * C],
                                        ALU.subtract).then_inc(s["an_dif"], 1)
                dve.wait_ge(s["an_dif"], c + 1)
                nc.vector.tensor_reduce(devmax[:, c:c + 1], dev[:, c % 2, :], AX.X, ALU.max,
                                        apply_absolute_value=True).then_inc(s["an_max"], 1)
            dve.wait_ge(s["an_max"], NC)
            nc.vector.tensor_reduce(devtop[:, :], devmax[:, :], AX.X, ALU.max).then_inc(s["dv_top"], 1)
            nc.vector.tensor_scalar(A_base[:, :], Pex[:, 0:T], off[:, :], DT / 6, ALU.add, ALU.mult).then_inc(s["pg_made"], 1)
            dve.wait_ge(s["dv_row"], 1)
            nc.vector.tensor_reduce(devrow[:, :], banks[6][0:1, 0:128], AX.X, ALU.max).then_inc(s["dv_rowed"], 1)
            dve.wait_ge(s["dv_rowed"], 1)
            nc.vector.tensor_scalar(flag[:, :], devrow[:, :], TOL, None, ALU.is_le).then_inc(s["flag_made"], 1)
            dve.wait_ge(s["flag_made"], 1)
            checked = dve.value_load(flag[0:1, 0:1], min_val=0, max_val=1)
            with dve.If(checked == 0):
                nc.vector.memset(seq_P[:, :], 0.0).then_inc(s["sq_sum"], 1)
                nc.vector.tensor_tensor(seq_a[:, :], a0[0:H, :], fb1[0:H, :], ALU.add).then_inc(s["sq_set"], 1)
                dve.wait_ge(s["sq_set"], 1)
                dve.wait_ge(s["sq_sum"], 1)
                with dve.Fori(0, N // C) as b:
                    wait_apart(dve, s["sq_in"], 16 * (b + 1))
                    with dve.Fori(0, C) as i:
                        t = b * C + i
                        nc.vector.tensor_scalar(seq_blk[:, bass.ds(i, 1)], seq_P[:, :], DT / 6, None, ALU.mult).then_inc(s["sq_blk"], 1)
                        nc.vector.tensor_scalar(seq_bias[:, 0:1], seq_t[:, bass.ds(i, 1)], slope[0:H, :], seq_a[:, :],
                                                ALU.mult, ALU.add).then_inc(s["sq_blk"], 1)
                        dve.wait_ge(s["sq_blk"], 3 * t + 2)
                        nc.vector.tensor_scalar(seq_bias[:, 1:2], slope[0:H, :], DT / 2, seq_bias[:, 0:1],
                                                ALU.mult, ALU.add).then_inc(s["sq_blk"], 1)
                        nc.vector.tensor_scalar(seq_bias[:, 2:3], slope[0:H, :], DT, seq_bias[:, 0:1],
                                                ALU.mult, ALU.add).then_inc(s["sq_bias"], 1)
                        dve.wait_ge(s["sq_h"], 4 * t + 4)
                        nc.vector.tensor_tensor(seq_S[:, 0:1], seq_h[:, 1:2], seq_h[:, 2:3], ALU.add).then_inc(s["sq_set"], 1)
                        dve.wait_ge(s["sq_set"], 3 * t + 2)
                        nc.vector.scalar_tensor_tensor(seq_S[:, 1:2], seq_S[:, 0:1], 2.0, seq_h[:, 0:1],
                                                       ALU.mult, ALU.add).then_inc(s["sq_set"], 1)
                        dve.wait_ge(s["sq_set"], 3 * t + 3)
                        nc.vector.tensor_tensor(seq_S[:, 2:3], seq_S[:, 1:2], seq_h[:, 3:4], ALU.add).then_inc(s["sq_set"], 1)
                        dve.wait_ge(s["sq_set"], 3 * t + 4)
                        nc.vector.tensor_tensor(seq_P[:, :], seq_P[:, :], seq_S[:, 2:3], ALU.add).then_inc(s["sq_sum"], 1)
                        dve.wait_ge(s["sq_sum"], t + 2)
            dve.drain().then_inc(s["scan_over"], 1)
            dve.wait_ge(s["scan_over"], 5)

            x_norm(1)
            x_scale(1)
            turned(1, "xt_hi", "xt_lo", 4, xTh, xTl)
            for q in range(S):
                dve.wait_ge(s["o_up"], q + 1)
                nc.vector.tensor_tensor(yb[:, q, :], banks[6 + q % 2][0:P, :], x1_first[:, q, :], ALU.add).then_inc(s["o_added"], 1)

            def add_steps(j):
                for q in range(S):
                    dve.wait_ge(s["o_up"], S * j + q + 1)
                    dve.wait_ge(s["yg_done"], S * j + q + 1)
                    nc.vector.tensor_tensor(yb[:, q, :], banks[6 + q % 2][0:P, :], yb[:, q, :], ALU.add).then_inc(s["o_added"], 1)

            def nodes(j, b, ahead=True, behind=True):
                unit(j)
                if behind:
                    dve.wait_ge(s["out_ready"], S * (j - 1))
                    y_norm(j - 1, 1 - b)
                if ahead:
                    x_norm(j + 1)
                if behind:
                    y_scale(j - 1)
                if ahead:
                    x_scale(j + 1)
                if behind:
                    add_steps(j - 1)
                if ahead:
                    turned(j + 1, "xt_hi", "xt_lo", 4, xTh, xTl)
                turned(j, "ut_hi", "ut_lo", 5, uTh, uTl)

            nodes(1, 1, behind=False)
            with dve.Fori(2, NN - 2, 2) as j:
                nodes(j, 0)
                nodes(j + 1, 1)
            nodes(NN - 2, 0)
            nodes(NN - 1, 1, ahead=False)
            dve.wait_ge(s["out_ready"], S * (NN - 1))
            y_norm(NN - 1, 1)
            y_scale(NN - 1)
            add_steps(NN - 1)

        @block.tensor
        def _(pe):
            def product(to, chunks, signal):
                passes = [(l[a], r[b]) for l, r in chunks for a, b in ((0, 0), (0, 1), (1, 0))]
                for m, (l, r) in enumerate(passes):
                    op = nc.tensor.matmul(to, l, r, start=(m == 0), stop=(m == len(passes) - 1))
                op.then_inc(signal, 1)

            def turn(to, of, signal=None):
                op = nc.tensor.transpose(to, of, ident[0:P, 0:P])
                if signal is not None:
                    op.then_inc(signal, 1)

            def groups(i, peeled=False):
                pe.wait_ge(s["rows_normed"], 2 * S * (i + 1))
                pe.wait_ge(s["attr_in"], 16 * (i + 1))
                for g in range(NT):
                    bank = banks[4 + g % 4]
                    if g >= 4:
                        wait_apart(pe, s["group_lo"], NT * i + g - 3)
                    elif not peeled:
                        wait_apart(pe, s["z_lo"] if g < 2 else s["c_out"], S * (i - 1))
                    for k in range(KD):
                        of = rows[:, g, k * 128:(k + 1) * 128] if g < 2 * S else attr[:, k, :]
                        to = bank[:, k * 128:k * 128 + P] if g < 2 * S else bank[0:DE, k * P:(k + 1) * P]
                        turn(to, of, s["groups_up"] if k == KD - 1 else None)

            def layer1(i, first=False):
                pe.wait_ge(s["group_lo"], NT * (i + 1))
                if first:
                    pe.wait_ge(s["split_lo"], 3)
                for m in range(KD):
                    cols = slice(m * 128, (m + 1) * 128)
                    if not first:
                        pe.wait_ge(s["w_done"], 2 * KD * i + m - 3)
                    product(banks[m][:, 0:R],
                            [((W1h[0:w, k, cols], W1l[0:w, k, cols]), (fTh[0:w, k, :], fTl[0:w, k, :]))
                             for k, w in [(k, 128) for k in range(2 * KD)] + [(2 * KD, DE)]], s["layer_up"])

            def layer2(i, first=False):
                pe.wait_ge(s["lo_done"], 2 * KD * i + KD)
                if first:
                    pe.wait_ge(s["split_lo"], EW)
                for m in range(KD):
                    cols = slice(m * 128, (m + 1) * 128)
                    pe.wait_ge(s["w_done"], 2 * KD * i + KD + m - 3)
                    product(banks[m][:, 0:R],
                            [((W2h[:, k, cols], W2l[:, k, cols]), (h1h[:, k, :], h1l[:, k, :])) for k in range(KD)],
                            s["layer_up"])

            def sums(i):
                pe.wait_ge(s["lo_done"], 2 * KD * (i + 1))
                for kind, q in L3_ORDER:
                    n = S * i + q
                    cols = slice(q * P, (q + 1) * P)
                    if kind == "z":
                        if q >= 2:
                            pe.wait_ge(s["z_lo"], n - 1)
                        product(banks[4 + q % 2][0:P, :],
                                [((msgh[:, k, cols], msgl[:, k, cols]), (W3h[:, k, :], W3l[:, k, :])) for k in range(KD)],
                                s["z_up"])
                    else:
                        pe.wait_ge(s["z_lo"], n + 1)
                        pe.wait_ge(s["same_made"], S * (i + 1))
                        if q >= 2:
                            pe.wait_ge(s["c_out"], n - 1)
                        nc.tensor.matmul(banks[6 + q % 2][0:P, :], same[:, q, 0:P], zh[:, q % 2, :], start=True, stop=False)
                        nc.tensor.matmul(banks[6 + q % 2][0:P, :], same[:, q, 0:P], zl[:, q % 2, :], start=False,
                                         stop=True).then_inc(s["c_up"], 1)

            pe.wait_ge(s["diag_made"], 3)
            groups(0, peeled=True)
            layer1(0, first=True)
            groups(1, peeled=True)
            layer2(0, first=True)
            layer1(1)
            sums(0)
            groups(2)
            layer2(1)
            with pe.Fori(2, NE - 1) as i:
                layer1(i)
                sums(i - 1)
                groups(i + 1)
                layer2(i)
            layer1(NE - 1)
            sums(NE - 2)
            layer2(NE - 1)
            sums(NE - 1)
            pe.drain().then_inc(s["edges_over"], 1)
            pe.wait_ge(s["edges_over"], 5)

            def turn_x(j, first=False):
                pe.wait_ge(s["xn_done"], S * (j + 1))
                for q in range(S):
                    if not (first and q == 0):
                        pe.wait_ge(s["xt_lo"], S * j + q)
                    for k in range(KD):
                        turn(banks[4][:, k * 128:k * 128 + P], xn[:, q, k * 128:(k + 1) * 128],
                             s["xt_up"] if k == KD - 1 else None)

            def turn_u(j, first=False):
                for q in range(S):
                    pe.wait_ge(s["u_done"], S * j + q + 1)
                    if not (first and q == 0):
                        pe.wait_ge(s["ut_lo"], S * j + q)
                    for k in range(KD):
                        turn(banks[5][:, k * 128:k * 128 + P], u[:, q, k * 128:(k + 1) * 128],
                             s["ut_up"] if k == KD - 1 else None)

            def update1(j, first=False):
                pe.wait_ge(s["xt_lo"], S * (j + 1))
                for q in range(S):
                    if not (first and q < 2):
                        pe.wait_ge(s["z_done"], S * j + q - 1)
                    product(banks[q % 2][0:P, :],
                            [((xTh[:, q, k, 0:P], xTl[:, q, k, 0:P]), (W3ah[:, k, :], W3al[:, k, :])) for k in range(KD)],
                            s["u_up"])

            def update2(j, first=False):
                pe.wait_ge(s["ut_lo"], S * (j + 1))
                for q in range(S):
                    if not (first and q < 2):
                        pe.wait_ge(s["y_added"], S * j + q - 1)
                    product(banks[2 + q % 2][0:P, :],
                            [((uTh[:, q, k, 0:P], uTl[:, q, k, 0:P]), (W4h[:, k, :], W4l[:, k, :])) for k in range(KD)],
                            s["y_up"])

            def steps(j, first=False):
                pe.wait_ge(s["p_in"], 32 * (j + 1))
                for q in range(S):
                    if not (first and q < 2):
                        pe.wait_ge(s["o_added"], S * j + q - 1)
                    lhs = steps_lhs[:, :].rearrange("k (p s) -> k s p", s=S)[:, q, :]
                    nc.tensor.matmul(banks[6 + q % 2][0:P, :], lhs, steps_rhs[:, :], start=True, stop=True).then_inc(s["o_up"], 1)

            turn_x(0, first=True)
            pe.wait_ge(s["n_lo"], 2)
            update1(0, first=True)
            turn_u(0, first=True)
            update2(0, first=True)
            pe.drain().then_inc(s["first_over"], 1)
            pe.wait_ge(s["first_over"], 5)

            pe.wait_ge(s["o_loaded"], 16 * O_LOADS)
            pe.wait_ge(s["o_set"], O_SET)
            for k in range(KD):
                op = nc.tensor.matmul(banks[0][:, 0:128], fW3[:, k, :], fW1T[:, k, :], start=(k == 0), stop=(k == KD - 1))
            op.then_inc(s["o_mat_up"], 1)
            for k in range(KD):
                op = nc.tensor.matmul(banks[1][:, 0:1], fW1T[:, k, :], fb3[:, k:k + 1], start=(k == 0), stop=(k == KD - 1))
            op.then_inc(s["o_slope_up"], 1)
            pe.wait_ge(s["y0_made"], 1)
            for k in range(KD):
                op = nc.tensor.matmul(banks[2][:, k:k + 1], y0[:, k * 128:(k + 1) * 128], one_col[0:1, :], start=True, stop=True)
            op.then_inc(s["y0T_up"], 1)
            pe.wait_ge(s["y0T"], 2)
            for k in range(KD):
                op = nc.tensor.matmul(banks[3][:, 0:1], fW1T[:, k, :], y0b3[:, k, 0:1], start=(k == 0), stop=(k == KD - 1))
            op.then_inc(s["a_up"], 1)
            for k in range(KD):
                op = nc.tensor.matmul(banks[4][H:KV, 0:H], y0b3[:, k, :], fW1T[:, k, 0:H], start=(k == 0), stop=(k == KD - 1))
            op.then_inc(s["a_up"], 1)
            pe.wait_ge(s["o_mats"], 4)
            pe.wait_ge(s["o_slope"], 3)
            with pe.Fori(0, PICARD) as it:
                wait_apart(pe, s["V_made"], it + 1)
                nc.tensor.matmul(banks[0][0:H, 0:NQ], V[0:KV, :], rule[:, :], start=True, stop=True).then_inc(s["q_a"], 1)
                wait_apart(pe, s["q_g"], it + 1)
                nc.tensor.matmul(banks[1][0:H, 0:NQ], fW2[0:H, 0:H], gq[:, :], start=True, stop=True).then_inc(s["q_w"], 1)
                wait_apart(pe, s["q_h"], it + 1)
                nc.tensor.matmul(banks[2][0:NQ, 0:H], hq[:, :], M_T[:, :], start=True, stop=True).then_inc(s["q_v"], 1)
            pe.wait_ge(s["V_made"], PICARD + 1)
            for c in range(NC):
                if c >= 4:
                    pe.wait_ge(s["ag_out"], c - 3)
                for g in range(G):
                    at = g * T + c * C
                    op = nc.tensor.matmul(banks[c % 4][H * g:H * (g + 1), 0:C], V[0:KV, :], ruleT[:, at:at + C],
                                          start=True, stop=True)
                op.then_inc(s["ag_up"], 1)
            pe.wait_ge(s["ag_out"], NC)
            for n in range(len(STAGES) + STAGE_LAG):
                if NC <= n < len(STAGES):
                    st, c = STAGES[n]
                    pe.wait_ge(s["st_h"], n - NC + 1)
                    if n >= NC + 4:
                        pe.wait_ge(s["st_zs"], n - NC - 3)
                    nc.tensor.matmul(banks[n % 4][:, 0:C], (M_full if st == 3 else M_half)[:, :], hst[:, c, :],
                                     start=True, stop=True).then_inc(s["st_z"], 1)
                if n >= STAGE_LAG:
                    m = n - STAGE_LAG
                    pe.wait_ge(s["st_g"], m + 1)
                    if m >= 4:
                        pe.wait_ge(s["st_h"], m - 3)
                    nc.tensor.matmul(banks[4 + m % 4][:, 0:C], fW2[:, :], gst[:, m % 4, :], start=True,
                                     stop=True).then_inc(s["st_x"], 1)
            pe.wait_ge(s["scan_done"], NC)
            nc.tensor.matmul(banks[4][:, 0:1], groups_before[:, :], Pex[:, T:T + 1], start=True, stop=True).then_inc(s["of_up"], 1)
            pe.wait_ge(s["of_done"], 1)
            nc.tensor.matmul(banks[5][:, 0:1], M_six[:, :], off[:, :], start=True, stop=True).then_inc(s["bs_up"], 1)
            for c in range(NC):
                if c >= 4:
                    pe.wait_ge(s["an_dev"], c - 3)
                nc.tensor.matmul(banks[c % 4][:, 0:C], M_six[:, :], Pex[:, c * C:(c + 1) * C], start=True, stop=True).then_inc(s["an_up"], 1)
            pe.wait_ge(s["dv_top"], 1)
            nc.tensor.transpose(banks[6][0:1, 0:128], devtop[:, :], ident[:, :]).then_inc(s["dv_row"], 1)
            pe.wait_ge(s["flag_made"], 1)
            checked = pe.value_load(flag[0:1, 0:1], min_val=0, max_val=1)
            with pe.If(checked == 0):
                with pe.Fori(0, N) as t:
                    wait_apart(pe, s["sq_sum"], t + 1)
                    for st in range(4):
                        if st == 0:
                            nc.tensor.matmul(banks[0][0:H, 0:1], M_six[0:H, 0:H], seq_P[:, :], start=True, stop=True).then_inc(s["sq_pre"], 1)
                        else:
                            wait_apart(pe, s["sq_h"], 4 * t + st)
                            nc.tensor.matmul(banks[0][0:H, 0:1], M_six[0:H, 0:H], seq_P[:, :], start=True, stop=False)
                            nc.tensor.matmul(banks[0][0:H, 0:1], (M_full if st == 3 else M_half)[0:H, 0:H],
                                             seq_h[:, st - 1:st], start=False, stop=True).then_inc(s["sq_pre"], 1)
                        wait_apart(pe, s["sq_g"], 4 * t + st + 1)
                        nc.tensor.matmul(banks[1][0:H, 0:1], fW2[0:H, 0:H], seq_g[:, :], start=True, stop=True).then_inc(s["sq_x"], 1)
            pe.drain().then_inc(s["scan_over"], 1)
            pe.wait_ge(s["scan_over"], 5)

            turn_x(1)
            pe.wait_ge(s["y0_row"], 16)
            steps(0, first=True)

            def nodes(j, ahead=True, behind=True):
                update1(j)
                if behind:
                    update2(j - 1)
                    steps(j - 1)
                if ahead:
                    turn_x(j + 1)
                turn_u(j)

            nodes(1, behind=False)
            with pe.Fori(2, NN - 1) as j:
                nodes(j)
            nodes(NN - 1, ahead=False)
            update2(NN - 1)
            steps(NN - 1)


NODES = 16


def rules(n_times):
    import numpy as np

    k = np.arange(NODES)
    at = 0.5 * (1 - np.cos((2 * k + 1) * np.pi / (2 * NODES)))
    cheb = np.polynomial.chebyshev
    unit = np.eye(NODES)
    inverse = np.linalg.inv(np.stack([cheb.chebval(2 * at - 1, unit[j]) for j in range(NODES)]))

    def table(t):
        whole = [cheb.chebint(unit[j]) * 0.5 for j in range(NODES)]
        to_t = np.stack([cheb.chebval(2 * t - 1, w) - cheb.chebval(-1, w) for w in whole])
        out = np.zeros((34, t.size))
        out[0:NODES] = inverse @ to_t
        out[32] = 1.0
        out[33] = t
        return out.astype(np.float32)

    return table(at), table(np.arange(n_times) / (n_times - 1))


_NAMES = ["x", "src_cols", "dst", "dst_cols", "edge_attr_64"] + [
    "L0_gnn_" + n for n in ("W1", "b1", "W2", "b2", "W3", "b3", "W4", "b4", "gamma", "beta")]


def kernel(**inputs):
    import numpy as _np
    import concourse.bacc as _bacc
    from concourse import mybir as _mybir
    from concourse.bass_utils import run_bass_kernel_spmd as _run

    nc = _bacc.Bacc("TRN2", target_bir_lowering=False, num_devices=1)
    f = {n: _np.asarray(inputs["L0_ffn_" + n]) for n in ("W1", "b1", "W2", "b2", "W3", "b3")}
    n_rows, d = inputs["x"].shape
    node_rule, time_rule = rules(n_rows)
    for side in ("src", "dst"):
        inputs[side + "_cols"] = _np.asarray(inputs[side]).reshape(-1, 125).T
    given = [(n, inputs[n]) for n in _NAMES] + [
        ("F_W1T", f["W1"].T), ("F_b1", f["b1"]), ("F_W2T", f["W2"].T), ("F_b2", f["b2"]),
        ("F_W3", f["W3"]), ("F_W3T", f["W3"].T), ("F_b3", f["b3"]), ("node_rule", node_rule), ("time_rule", time_rule)]
    arrays, args = {}, []
    for name, a in given:
        a = _np.ascontiguousarray(a)
        arrays[f"in_{name}_dram"] = a
        args.append(nc.dram_tensor(f"in_{name}_dram", a.shape, _mybir.dt.from_np(a.dtype), kind="ExternalInput").ap())
    f32 = _mybir.dt.float32
    args.append(nc.dram_tensor("out_0_dram", (n_rows, d), f32, kind="ExternalOutput").ap())
    args.append(nc.dram_tensor("message_sums", (10240, d), f32).ap())
    args.append(nc.dram_tensor("sums_by_time", (f["b1"].shape[0], n_rows), f32).ap())
    gnn_ffn_kernel(nc, *args)
    r = _run(nc, [arrays], core_ids=[0])
    return r.results[0]["out_0_dram"]
```

```python
import concourse.bass as bass
from concourse import mybir
from contextlib import ExitStack


def gnn_ffn_kernel(
    nc: bass.Bass,
    x: bass.AP,
    src_cols: bass.AP,
    dst: bass.AP,
    dst_cols: bass.AP,
    edge_attr: bass.AP,
    W1: bass.AP,
    b1: bass.AP,
    W2: bass.AP,
    b2: bass.AP,
    W3: bass.AP,
    b3: bass.AP,
    W4: bass.AP,
    b4: bass.AP,
    gamma: bass.AP,
    beta: bass.AP,
    F_W1T: bass.AP,
    F_b1: bass.AP,
    F_W2T: bass.AP,
    F_b2: bass.AP,
    F_W3: bass.AP,
    F_W3T: bass.AP,
    F_b3: bass.AP,
    node_rule: bass.AP,
    time_rule: bass.AP,
    out: bass.AP,
    message_sums: bass.AP,
    sums_by_time: bass.AP,
):
    f32 = mybir.dt.float32
    f32r = mybir.dt.float32r
    i32 = mybir.dt.int32
    ALU = mybir.AluOpType
    ACT = mybir.ActivationFunctionType
    AX = mybir.AxisListType

    N, D = x.shape
    E = dst.shape[0]
    DE = edge_attr.shape[1]
    H = F_b1.shape[0]
    P = 125
    S = 4
    R = P * S
    KD = D // 128
    KF = 2 * KD + 1
    NE = E // R
    NN = N // R
    NT = 2 * S + 1
    EPS = 1e-5
    EXP_MAX = 4.0e8
    SPLIT = 112

    DT = 1.0 / (N - 1)
    G = 4
    T = N // G
    C = 500
    NC = T // C
    NQ = node_rule.shape[1]
    PICARD = 13
    KV = node_rule.shape[0]
    TOL = 1.5e-5

    ctx = ExitStack()
    with ctx:
        def sem(name):
            return ctx.enter_context(nc.semaphore(name))

        def psum(name, n=1):
            return ctx.enter_context(nc.psum_tensor(name, [128, n * 512], f32))

        def sb_in(scope):
            return lambda name, shape, dt=f32: scope.enter_context(nc.sbuf_tensor(name, shape, dt))

        banks = [psum(f"bank{i}") for i in range(8)]

        sb = sb_in(ctx)
        ident = sb("ident", [128, 128])
        eps_col = sb("eps_col", [128, 1])
        one_col = sb("one_col", [128, 1])
        two_col = sb("two_col", [128, 1])
        gamma_bc = sb("gamma_bc", [P, D])
        beta_bc = sb("beta_bc", [P, D])
        b4_bc = sb("b4_bc", [P, D])
        b3_bc = sb("b3_bc", [128, D])
        b1_col = sb("b1_col", [128, KD])
        b2_col = sb("b2_col", [128, KD])
        src_all = sb("src_all", [P, NE * S], i32)
        dst_all = sb("dst_all", [P, NE * S], i32)
        dst_allf = sb("dst_allf", [P, NE * S])
        steps_rhs = sb("steps_rhs", [KV, D])

        edge_scope = ExitStack()
        sb = sb_in(edge_scope)
        W1h = sb("W1h", [128, KF, D], f32r)
        W1l = sb("W1l", [128, KF, D], f32r)
        W2h = sb("W2h", [128, KD, D], f32r)
        W2l = sb("W2l", [128, KD, D], f32r)
        W3h = sb("W3h", [128, KD, D], f32r)
        W3l = sb("W3l", [128, KD, D], f32r)
        rows = sb("rows", [P, 2 * S, D])
        attr = sb("attr", [P, S, DE])
        fTh = sb("fTh", [128, KF, R], f32r)
        fTl = sb("fTl", [128, KF, R], f32r)
        h1h = sb("h1h", [128, KD, R], f32r)
        h1l = sb("h1l", [128, KD, R], f32r)
        msgh = sb("msgh", [128, KD, R], f32r)
        msgl = sb("msgl", [128, KD, R], f32r)
        tmp = sb("tmp", [128, 8, 512])
        zh = sb("zh", [P, 2, D], f32r)
        zl = sb("zl", [P, 2, D], f32r)
        zsum = sb("zsum", [P, S, D])
        e_stats = sb("e_stats", [P, 2 * S, 6])
        e_mv = sb("e_mv", [P, 2 * S, 2])
        e_lnv = sb("e_lnv", [P, 2 * S])
        e_rstd = sb("e_rstd", [P, 2 * S])
        e_var = sb("e_var", [P, 2 * S])
        e_sq = sb("e_sq", [P, 2 * S])
        e_shift = sb("e_shift", [P, 2 * S])
        src_cur = sb("src_cur", [P, S], i32)
        dst_cur = sb("dst_cur", [P, S], i32)
        drow_i = sb("drow_i", [P, R], i32)
        drow_f = sb("drow_f", [P, R])
        dcol_f = sb("dcol_f", [P, S])
        same = sb("same", [P, S, 126], f32r)
        earlier = sb("earlier", [P, P])
        same_earlier = sb("same_earlier", [P, S, P])
        n_earlier = sb("n_earlier", [P, S])
        spare_i = sb("spare_i", [P, 1], i32)
        spare_row = sb("spare_row", [P, 1])
        to_spare = sb("to_spare", [P, S])
        sum_row = sb("sum_row", [P, S])
        sum_row_i = sb("sum_row_i", [P, S], i32)
        edge_scope.close()

        node_scope = ExitStack()
        sb = sb_in(node_scope)
        W3ah = sb("W3ah", [128, KD, D], f32r)
        W3al = sb("W3al", [128, KD, D], f32r)
        W4h = sb("W4h", [128, KD, D], f32r)
        W4l = sb("W4l", [128, KD, D], f32r)
        x1_first = sb("x1_first", [P, S, D])
        steps_lhs = sb("steps_lhs", [KV, 2, R])
        keep_top = ExitStack()
        sb = sb_in(keep_top)
        xraw = sb("xraw", [P, 2, S, D])
        xn = sb("xn", [P, S, D])
        agg = sb("agg", [P, S, D])
        xTh = sb("xTh", [128, S, KD, P + 1], f32r)
        xTl = sb("xTl", [128, S, KD, P + 1], f32r)
        nz = sb("nz", [P, 2, D])
        ne = sb("ne", [P, 2, D])
        nt = sb("nt", [P, 2, D])
        nr = sb("nr", [P, 2, D])
        u = sb("u", [P, 2, D])
        uTh = sb("uTh", [128, S, KD, P + 1], f32r)
        uTl = sb("uTl", [128, S, KD, P + 1], f32r)
        xnb = sb("xnb", [P, 2, S, D])
        yb = sb("yb", [P, 2, S, D])
        ob = sb("ob", [128, 2, S, D])
        stats = sb("stats", [P, 2 * S, 6])
        mv = sb("mv", [P, 2 * S, 2])
        lnv = sb("lnv", [P, 2 * S])
        rstd = sb("rstd", [P, 2 * S])
        var_eps = sb("var_eps", [P, 2 * S])
        sq = sb("sq", [P, 2 * S])
        shift = sb("shift", [P, 2 * S])
        keep_top.close()

        ode_scope = ExitStack()
        sb = sb_in(ode_scope)
        ruleT = sb("ruleT", [KV, N])
        rule = sb("rule", [KV, NQ])
        fW1T = sb("fW1T", [128, KD, 128])
        fW3 = sb("fW3", [128, KD, 128])
        fb3 = sb("fb3", [128, KD])
        fW2 = sb("fW2", [128, 128])
        fb1 = sb("fb1", [128, 1])
        fb2 = sb("fb2", [128, 1])
        blocks = sb("blocks", [128, 128])
        groups_before = sb("groups_before", [128, 128])
        M_T = sb("M_T", [H, H])
        M_half = sb("M_half", [128, 128])
        M_full = sb("M_full", [128, 128])
        M_six = sb("M_six", [128, 128])
        slope = sb("slope", [128, 1])
        bias_half = sb("bias_half", [128, 1])
        bias_full = sb("bias_full", [128, 1])
        y0 = sb("y0", [1, D])
        y0_x1 = sb("y0_x1", [1, D])
        y0_beta = sb("y0_beta", [1, D])
        y0_st = sb("y0_st", [1, 6])
        y0_mv = sb("y0_mv", [1, 2])
        y0_s = sb("y0_s", [1, 4])
        y0b3 = sb("y0b3", [128, KD, 2])
        a0 = sb("a0", [128, 1])
        V = sb("V", [64, H])
        gq = sb("gq", [H, NQ])
        hq = sb("hq", [H, NQ])
        A_guess = sb("A_guess", [128, T])
        A_base = sb("A_base", [128, T])
        times = sb("times", [128, T])
        zst = sb("zst", [128, 2, C])
        gst = sb("gst", [128, 4, C])
        hst = sb("hst", [128, NC + 1, C])
        Ssum = sb("Ssum", [128, NC, C])
        zeros = sb("zeros", [128, C])
        Pex = sb("Pex", [128, T + 1])
        off = sb("off", [128, 1])
        base = sb("base", [128, 1])
        dev = sb("dev", [128, 2, C])
        devmax = sb("devmax", [128, NC])
        devtop = sb("devtop", [128, 1])
        devrow = sb("devrow", [1, 1])
        flag = sb("flag", [1, 1], i32)
        seq_a = sb("seq_a", [H, 1])
        seq_bias = sb("seq_bias", [H, 3])
        seq_g = sb("seq_g", [H, 1])
        seq_h = sb("seq_h", [H, 4])
        seq_P = sb("seq_P", [H, 1])
        seq_S = sb("seq_S", [H, 3])
        seq_blk = sb("seq_blk", [H, C])
        seq_t = sb("seq_t", [H, C])
        ode_scope.close()
        node_scope.close()

        s = {}
        for name in (
            "consts_set diag_made spare_made smalls_in dstf_made table_filled staged split_hi split_lo "
            "staged1 idx_copied rows_in attr_in stats_done aggr_done ln_log ln_guess newton rows_normed rows_normed_dve groups_up "
            "group_hi group_lo layer_up exp_done cut_done t_done log_done r_done w_done m_done hi_done lo_done "
            "z_up z_hi z_lo c_up c_out drow_in seg same_made sumrow_made scattered "
            "n_staged1 n_staged n_hi n_lo x_in x_in1 x_in2 x_in3 agg_in agg_in1 xs_done aggr2 lns_log lns_guess lns_newton xn_done xnb_done "
            "xt_up xt_hi xt_lo ut_up ut_hi ut_lo u_up z_done ne_done nc_done nt_done nl_done nr_done nw_done u_done "
            "y_up y_added ys_done yn_done yg_done yx_done o_up o_added ob_in ob_in1 stored "
            "p_in p_in1 first_done "
            "o_set o_loaded o_mat_up o_mats o_slope_up o_slope y0_stat y0_log y0_guess y0_newton y0_made y0T_up y0T "
            "y0_row a_up a_made V_made q_a q_g q_w q_h q_v ag_up ag_out ab_made st_z st_zs st_g st_x st_h st_acc "
            "scan_done of_up of_done bs_up bs_done an_up an_dev an_dif an_max dv_row dv_rowed dv_top flag_made "
            "pg_made sums_out sq_in sq_set sq_bias sq_pre sq_g sq_x sq_h sq_sum sq_blk sq_stored "
            "edges_over first_over scan_over"
        ).split():
            s[name] = sem(name)

        x_rows = x.rearrange("(j p s) d -> j p s d", p=P, s=S)
        out_rows = out.rearrange("(j p s) d -> j p s d", p=P, s=S)
        agg_rows = message_sums[0:N, :].rearrange("(j p s) d -> j p s d", p=P, s=S)
        attr_rows = edge_attr.rearrange("(i s p) d -> i p s d", s=S, p=P)
        dst_rows = dst.rearrange("(i r) -> i r", r=R)
        W1v = W1[0:2 * D, :].rearrange("(k p) n -> p k n", p=128)
        W2v = W2.rearrange("(k p) n -> p k n", p=128)
        W3av = W3[0:D, :].rearrange("(k p) n -> p k n", p=128)
        W3bv = W3[D:2 * D, :].rearrange("(k p) n -> p k n", p=128)
        W4v = W4.rearrange("(k p) n -> p k n", p=128)
        EW = 5
        staging = [tmp[:, 0:4, :], tmp[:, 4:8, :]]
        edge_pieces = [
            (W1v[:, 0:KD, :], W1h[:, 0:KD, :], W1l[:, 0:KD, :], 128),
            (W1v[:, KD:2 * KD, :], W1h[:, KD:2 * KD, :], W1l[:, KD:2 * KD, :], 128),
            (W1[2 * D:2 * D + DE, :], W1h[0:DE, 2 * KD, :], W1l[0:DE, 2 * KD, :], DE),
            (W2v, W2h[:, :, :], W2l[:, :, :], 128),
            (W3bv, W3h[:, :, :], W3l[:, :, :], 128),
        ]
        node_pieces = [(W3av, W3ah[:, :, :], W3al[:, :, :]), (W4v, W4h[:, :, :], W4l[:, :, :])]

        def piece_in(n):
            st = staging[n % 2]
            return st[0:DE, 0, :] if edge_pieces[n][3] == DE else st

        SMALLS = 10
        STAGED = ("staged", "staged1")
        FILLS = 20
        FILL_ROWS = message_sums.shape[0] // FILLS
        assert FILL_ROWS == 4 * 128 and FILLS * FILL_ROWS >= N + P
        CHUNKS = [(g, c) for c in range(NC) for g in range(G)]
        STAGES = [(st, c) for st in range(4) for c in range(NC)]

        L3_ORDER = [("z", 0), ("z", 1), ("c", 0), ("z", 2), ("c", 1), ("z", 3), ("c", 2), ("c", 3)]
        O_LOADS = 2 + 2 + 5 * G + G
        O_SET = 6 + G + G * (G - 1) // 2
        STAGE_LAG = 2
        SUM_LAG = 3

        def group_of(g):
            bank = banks[4 + g % 4]
            if g == 2 * S:
                return bank[0:DE, 0:R]
            return bank[:, :].rearrange("p (k c) -> p k c", k=KD)[:, :, 0:P]

        def group_to(g, to):
            if g == 2 * S:
                return to[0:DE, 2 * KD, :]
            side, q = g // S, g % S
            return to[:, side * KD:(side + 1) * KD, q * P:(q + 1) * P]

        def turned_of(bank):
            return banks[bank][:, :].rearrange("p (k c) -> p k c", k=KD)[:, :, 0:P]

        def wait_apart(eng, semaphore, value):
            if isinstance(value, int):
                eng.wait_ge(semaphore, value)
            else:
                held = eng.to_reg(value)
                eng.wait_ge(s["consts_set"], 5)
                eng.wait_ge(semaphore, held)

        def has(j, q, lag, low=S):
            return not isinstance(j, int) or low <= S * j + q + lag < S * NN

        def slot(b, q, lag):
            return (b + (q + lag) // S) % 2, (q + lag) % S

        def norms(j):
            at_x, at_y = has(j, 0, S), has(j, 0, -2 * S)
            return slice(0 if at_x else S, 2 * S if at_y else S) if at_x or at_y else None

        def aggregated(j):
            if not isinstance(j, int):
                return 2 * S + 3 * S + 2 * S * (j - 2)
            spans = [norms(i) for i in range(j + 1)]
            return 2 * S + sum(at.stop - at.start for at in spans if at)

        X_IN = (("x_in", "x_in1"), ("x_in2", "x_in3"))
        AGG_IN = ("agg_in", "agg_in1")

        def loads_by_parity(j, parity):
            return 16 * (j - parity) + 32

        LOOP = (4, NN - 4)

        def run_nodes(eng, nodes, first=-1):
            for j in range(first, LOOP[0]):
                nodes(j, j % 2)
            with eng.Fori(LOOP[0], LOOP[1], 2) as j:
                nodes(j, 0)
                nodes(j + 1, 1)
            for j in range(LOOP[1], NN + 3):
                nodes(j, j % 2)

        block = ctx.enter_context(nc.Block())

        @block.sync
        def _(sp):
            def row(v):
                return v.rearrange("(a n) -> a n", a=1)

            for to, of in (
                (b3_bc[:, :], row(b3).to_broadcast([128, D])),
                (src_all[:, :], src_cols),
                (dst_all[:, :], dst_cols),
                (b1_col[:, :], b1.rearrange("(k p) -> p k", p=128)),
                (b2_col[:, :], b2.rearrange("(k p) -> p k", p=128)),
                (gamma_bc[:, :], row(gamma).to_broadcast([P, D])),
                (beta_bc[:, :], row(beta).to_broadcast([P, D])),
                (b4_bc[:, :], row(b4).to_broadcast([P, D])),
                (steps_rhs[H + 1:H + 2, :], row(F_b3)),
                (steps_rhs[0:H, :], F_W3T),
            ):
                sp.dma_start(to, of, allow_slow_non_contiguous=True).then_inc(s["smalls_in"], 16)
            for n in range(EW):
                if n >= 2:
                    sp.wait_ge(s["split_lo"], n - 1)
                sp.dma_start(piece_in(n), edge_pieces[n][0]).then_inc(s[STAGED[n % 2]], 16)
            sp.dma_start(attr[:, :, :], attr_rows[0]).then_inc(s["attr_in"], 16)
            sp.wait_ge(s["smalls_in"], 16 * SMALLS)
            with sp.Fori(0, FILLS) as f:
                sp.dma_start(
                    message_sums[bass.ds(f * FILL_ROWS, FILL_ROWS), :].rearrange("(p s) d -> p s d", p=128),
                    b3_bc[:, :].unsqueeze(1).to_broadcast([128, S, D]),
                ).then_inc(s["table_filled"], 16)

            def attr_load(i):
                sp.wait_ge(s["groups_up"], NT * i)
                sp.dma_start(attr[:, :, :], attr_rows[i]).then_inc(s["attr_in"], 16)

            def dst_row_load(i):
                sp.dma_start(drow_i[:, :], dst_rows[bass.ds(i, 1), :].to_broadcast([P, R])).then_inc(s["drow_in"], 16)

            attr_load(1)
            dst_row_load(0)
            with sp.Fori(1, NE - 1) as i:
                attr_load(i + 1)
                sp.wait_ge(s["same_made"], S * i)
                dst_row_load(i)
            sp.wait_ge(s["same_made"], S * (NE - 1))
            dst_row_load(NE - 1)
            sp.drain().then_inc(s["edges_over"], 1)
            sp.wait_ge(s["edges_over"], 5)

            for n in range(2):
                sp.dma_start(ob[:, n, :, :], node_pieces[n][0]).then_inc(s[("n_staged", "n_staged1")[n]], 16)


            def x_load(j, b, h):
                w = slice(2 * h, 2 * h + 2)
                sp.dma_start(xraw[0:SPLIT, b, w], x_rows[j, 0:SPLIT, w]).then_inc(s[X_IN[b][h]], 16)
                sp.dma_start(xraw[SPLIT:P, b, w], x_rows[j, SPLIT:P, w]).then_inc(s[X_IN[b][h]], 16)

            def agg_load(j, h):
                w = slice(2 * h, 2 * h + 2)
                sp.dma_start(agg[0:SPLIT, w], agg_rows[j, 0:SPLIT, w]).then_inc(s[AGG_IN[h]], 16)
                sp.dma_start(agg[SPLIT:P, w], agg_rows[j, SPLIT:P, w]).then_inc(s[AGG_IN[h]], 16)

            def steps_load(j, b):
                done = s[("p_in", "p_in1")[b]]
                sp.dma_start(steps_lhs[0:H, b, :], sums_by_time[:, bass.ds(j * R, R)]).then_inc(done, 16)
                sp.dma_start(steps_lhs[H:KV, b, :], time_rule[H:KV, bass.ds(j * R, R)]).then_inc(done, 16)

            def x_again(j, b):
                done = s[("ob_in", "ob_in1")[b]]
                sp.dma_start(ob[0:SPLIT, b], x_rows[j, 0:SPLIT]).then_inc(done, 16)
                sp.dma_start(ob[SPLIT:P, b], x_rows[j, SPLIT:P]).then_inc(done, 16)

            def store(j, b):
                sp.dma_start(out_rows[j, 0:SPLIT], ob[0:SPLIT, b]).then_inc(s["stored"], 16)
                sp.dma_start(out_rows[j, SPLIT:P], ob[SPLIT:P, b]).then_inc(s["stored"], 16)

            for h in range(2):
                x_load(0, 0, h)
                agg_load(0, h)
            sp.drain().then_inc(s["first_over"], 1)
            sp.wait_ge(s["first_over"], 5)

            sp.dma_start(ruleT[0:H, :], time_rule[0:H, :]).then_inc(s["o_loaded"], 16)
            sp.dma_start(ruleT[H:KV, :], time_rule[H:KV, :]).then_inc(s["o_loaded"], 16)
            sp.wait_ge(s["y0_made"], 2)
            sp.dma_start(steps_rhs[H:H + 1, :], y0_beta[:, :]).then_inc(s["y0_row"], 16)
            sp.wait_ge(s["pg_made"], 1)
            for g in range(G):
                sp.dma_start(sums_by_time[:, g * T:(g + 1) * T], A_base[H * g:H * (g + 1), :]).then_inc(s["sums_out"], 16)
            sp.wait_ge(s["sums_out"], 16 * G)
            sp.wait_ge(s["flag_made"], 1)
            checked = sp.value_load(flag[0:1, 0:1], min_val=0, max_val=1)
            with sp.If(checked == 0):
                with sp.Fori(0, N // C) as b:
                    sp.dma_start(
                        seq_t[:, :], time_rule[KV - 1:KV, bass.ds(b * C, C)].to_broadcast([H, C])
                    ).then_inc(s["sq_in"], 16)
                    wait_apart(sp, s["sq_sum"], (b + 1) * C + 1)
                    sp.dma_start(sums_by_time[:, bass.ds(b * C, C)], seq_blk[:, :]).then_inc(s["sq_stored"], 16)
                    wait_apart(sp, s["sq_stored"], 16 * (b + 1))
            sp.drain().then_inc(s["scan_over"], 1)
            sp.wait_ge(s["scan_over"], 5)

            for h in range(2):
                x_load(1, 1, h)
                agg_load(1, h)
            for h in range(2):
                x_load(2, 0, h)

            def nodes(j, b):
                if has(j, 0, -3 * S, 0):
                    sp.wait_ge(s["o_added"], S * (j - 2))
                    store(j - 3, 1 - b)
                if has(j, 0, -S, 0):
                    steps_load(j - 1, 1 - b)
                for h in range(2):
                    if has(j, 0, 3 * S, S) and has(j, 0, S, S):
                        sp.wait_ge(s["xn_done"], S * (j + 1) + 2 * h + 2)
                        x_load(j + 3, 1 - b, h)
                    if has(j, 0, S, 2 * S):
                        sp.wait_ge(s["z_done"], S * j + 2 * h + 2)
                        agg_load(j + 1, h)
                    if h == 0:
                        if has(j, 0, -3 * S, 0):
                            sp.wait_ge(s["stored"], 32 * (j - 2))
                        if has(j, 0, -S, S):
                            x_again(j - 1, 1 - b)

            run_nodes(sp, nodes, first=0)
            sp.wait_ge(s["stored"], 32 * NN)

        @block.gpsimd
        def _(pool):
            nc.gpsimd.memset(ident[:, :], 0.0).then_inc(s["consts_set"], 1)
            nc.gpsimd.memset(earlier[:, :], 1.0).then_inc(s["consts_set"], 1)
            nc.gpsimd.memset(eps_col[:, :], EPS).then_inc(s["consts_set"], 1)
            nc.gpsimd.memset(one_col[:, :], 1.0).then_inc(s["consts_set"], 1)
            nc.gpsimd.memset(two_col[:, :], 2.0).then_inc(s["consts_set"], 1)
            pool.wait_ge(s["consts_set"], 5)
            nc.gpsimd.affine_select(
                out=ident[:, :], in_=ident[:, :], compare_op=ALU.not_equal, fill=1.0,
                base=0, pattern=[[-1, 128]], channel_multiplier=1,
            ).then_inc(s["diag_made"], 1)
            nc.gpsimd.affine_select(
                out=earlier[:, :], in_=earlier[:, :], compare_op=ALU.is_gt, fill=0.0,
                base=0, pattern=[[-1, P]], channel_multiplier=1,
            ).then_inc(s["diag_made"], 1)
            nc.gpsimd.iota(spare_i[:, :], pattern=[[0, 1]], base=N, channel_multiplier=1).then_inc(s["diag_made"], 1)
            pool.wait_ge(s["diag_made"], 3)
            nc.gpsimd.tensor_copy(spare_row[:, :], spare_i[:, :]).then_inc(s["spare_made"], 1)

            def gather(i):
                nc.gpsimd.tensor_copy(src_cur[:, :], src_all[:, bass.ds(i * S, S)]).then_inc(s["idx_copied"], 1)
                nc.gpsimd.tensor_copy(dst_cur[:, :], dst_all[:, bass.ds(i * S, S)]).then_inc(s["idx_copied"], 1)
                wait_apart(pool, s["idx_copied"], 2 * i + 2)
                for side, idx in ((0, src_cur), (1, dst_cur)):
                    for q in range(S):
                        nc.gpsimd.indirect_dma_start(
                            rows[:, side * S + q, :], None, x[:, :],
                            bass.IndirectOffsetOnAxis(ap=idx[:, q:q + 1], axis=0),
                        ).then_inc(s["rows_in"], 16)

            def scatter(i, first=False):
                pool.wait_ge(s["sumrow_made"], i + 1)
                for q in range(S):
                    pool.wait_ge(s["c_out"], S * i + q + 1)
                    if not (first and q == 0):
                        wait_apart(pool, s["scattered"], 16 * (S * i + q))
                    nc.gpsimd.indirect_dma_start(
                        message_sums[:, :], bass.IndirectOffsetOnAxis(ap=sum_row_i[:, q:q + 1], axis=0),
                        zsum[:, q, :], None, compute_op=ALU.add,
                    ).then_inc(s["scattered"], 16)

            pool.wait_ge(s["smalls_in"], 16 * SMALLS)
            gather(0)
            pool.wait_ge(s["groups_up"], NT)
            gather(1)
            pool.wait_ge(s["groups_up"], 2 * NT)
            gather(2)
            pool.wait_ge(s["table_filled"], 16 * FILLS)
            scatter(0, first=True)
            pool.wait_ge(s["groups_up"], 3 * NT)
            gather(3)
            with pool.Fori(2, NE - 2) as i:
                scatter(i - 1)
                pool.wait_ge(s["groups_up"], NT * (i + 2))
                gather(i + 2)
            for i in range(NE - 2, NE + 1):
                scatter(i - 1)
            pool.wait_ge(s["scattered"], 16 * S * NE)
            pool.drain().then_inc(s["edges_over"], 1)
            pool.wait_ge(s["edges_over"], 5)

            def norm_plus(q):
                pool.wait_ge(s["xn_done"], q + 1)
                nc.gpsimd.tensor_tensor(xnb[:, 0, q, :], xn[:, q, :], b4_bc[:, :], ALU.add).then_inc(s["xnb_done"], 1)

            for q in range(S):
                norm_plus(q)
            for q in range(S):
                pool.wait_ge(s["yn_done"], q + 1)
                nc.gpsimd.tensor_tensor(yb[:, 0, q, :], yb[:, 0, q, :], gamma_bc[:, :], ALU.mult).then_inc(s["yg_done"], 1)
            for q in range(S):
                pool.wait_ge(s["yg_done"], q + 1)
                nc.gpsimd.tensor_tensor(x1_first[:, q, :], yb[:, 0, q, :], xraw[:, 0, q, :], ALU.add).then_inc(s["yx_done"], 1)
            pool.drain().then_inc(s["first_over"], 1)
            pool.wait_ge(s["first_over"], 5)

            nc.gpsimd.memset(blocks[:, :], 0.0).then_inc(s["o_set"], 1)
            nc.gpsimd.memset(groups_before[:, :], 0.0).then_inc(s["o_set"], 1)
            nc.gpsimd.memset(fW2[:, :], 0.0).then_inc(s["o_set"], 1)
            nc.gpsimd.memset(V[:, :], 0.0).then_inc(s["o_set"], 1)
            nc.gpsimd.memset(zeros[:, :], 0.0).then_inc(s["o_set"], 1)
            nc.gpsimd.memset(Pex[:, 0:1], 0.0).then_inc(s["o_set"], 1)
            pool.wait_ge(s["o_set"], 6)
            for g in range(G):
                nc.gpsimd.memset(blocks[H * g:H * (g + 1), H * g:H * (g + 1)], 1.0).then_inc(s["o_set"], 1)
                for later in range(g + 1, G):
                    nc.gpsimd.tensor_copy(
                        groups_before[H * g:H * (g + 1), H * later:H * (later + 1)],
                        ident[H * g:H * (g + 1), H * g:H * (g + 1)],
                    ).then_inc(s["o_set"], 1)
            pool.drain().then_inc(s["scan_over"], 1)
            pool.wait_ge(s["scan_over"], 5)

            def nodes(j, b):
                for q in range(S):
                    n = S * j + q
                    if has(j, q, -1):
                        k = (q - 1) % 2
                        pool.wait_ge(s["nt_done"], n)
                        pool.wait_ge(s["ut_up"], n - 2)
                        nc.gpsimd.tensor_tensor(u[:, k, :], nz[:, k, :], nt[:, k, :], ALU.mult).then_inc(s["nw_done"], 1)
                    if has(j, q, -9):
                        m = n - 9
                        c, w = slot(b, q, -9)
                        pool.wait_ge(s["yn_done"], m + 1)
                        nc.gpsimd.tensor_tensor(yb[:, c, w, :], yb[:, c, w, :], gamma_bc[:, :], ALU.mult).then_inc(s["yg_done"], 1)
                        if w == 0:
                            wait_apart(pool, s[("ob_in", "ob_in1")[c]], 16 * (j - 2 + c))
                        pool.wait_ge(s["yg_done"], m + 1)
                        nc.gpsimd.tensor_tensor(ob[0:P, c, w, :], ob[0:P, c, w, :], yb[:, c, w, :], ALU.add).then_inc(s["yx_done"], 1)
                    if has(j, q, 3):
                        m = n + 3
                        c, w = slot(b, q, 3)
                        pool.wait_ge(s["xn_done"], m + 1)
                        if has(j, q, -5):
                            pool.wait_ge(s["y_added"], m - 7)
                        nc.gpsimd.tensor_tensor(xnb[:, c, w, :], xn[:, w, :], b4_bc[:, :], ALU.add).then_inc(s["xnb_done"], 1)

            run_nodes(pool, nodes)

        @block.scalar
        def _(act):
            def split_high(n, to, of):
                nc.scalar.activation(to, of, ACT.Copy).then_inc(s["split_hi"], 1)

            act.preload_act_table_set("natural_log_exp_and_others")
            act.wait_ge(s["consts_set"], 5)
            for n in range(EW):
                act.wait_ge(s[STAGED[n % 2]], 16 * (n // 2 + 1))
                split_high(n, edge_pieces[n][1], piece_in(n))

            def rows_rstd(i):
                act.wait_ge(s["aggr_done"], 2 * S * (i + 1))
                nc.scalar.activation(e_lnv[:, :], e_mv[:, :, 1], ACT.Ln, bias=eps_col[0:P, :]).then_inc(s["ln_log"], 1)
                act.wait_ge(s["ln_log"], i + 1)
                nc.scalar.activation(e_rstd[:, :], e_lnv[:, :], ACT.Exp, scale=-0.5).then_inc(s["ln_guess"], 1)

            def groups(i):
                for g in range(NT):
                    act.wait_ge(s["groups_up"], NT * i + g + 1)
                    nc.scalar.activation(group_to(g, fTh), group_of(g), ACT.Copy).then_inc(s["group_hi"], 1)

            def rows_norm(i, part):
                act.wait_ge(s["newton"], 6 * (i + 1))
                for a in (2 * part, 2 * part + 1):
                    nc.scalar.activation(rows[:, a, :], rows[:, a, :], ACT.Identity, bias=e_shift[:, a:a + 1],
                                         scale=e_rstd[:, a:a + 1]).then_inc(s["rows_normed"], 1)

            def z_high(i, q, first=False):
                act.wait_ge(s["z_up"], S * i + q + 1)
                if not (first and q < 2):
                    act.wait_ge(s["c_up"], S * i + q - 1)
                nc.scalar.activation(zh[:, q % 2, :], banks[4 + q % 2][0:P, :], ACT.Copy).then_inc(s["z_hi"], 1)

            def layer1(i, ahead=True, sums_ahead=True, first=False):
                for m in range(KD):
                    n, k = 2 * KD * i + m, m % 2
                    act.wait_ge(s["layer_up"], n + 1)
                    if not (first and m < 2):
                        act.wait_ge(s["t_done"], n - 1)
                    nc.scalar.activation(tmp[:, k, 0:R], banks[m][:, 0:R], ACT.Exp,
                                         bias=b1_col[:, m:m + 1]).then_inc(s["exp_done"], 1)
                    if ahead and m == KD - 1:
                        rows_rstd(i + 1)
                    act.wait_ge(s["t_done"], n + 1)
                    if not (first and m < 2):
                        act.wait_ge(s["m_done"], n - 1)
                    nc.scalar.activation(tmp[:, 4 + k, 0:R], tmp[:, 2 + k, 0:R], ACT.Ln,
                                         bias=two_col[:, :]).then_inc(s["log_done"], 1)
                    act.wait_ge(s["log_done"], n + 1)
                    nc.scalar.activation(tmp[:, 4 + k, 0:R], tmp[:, 4 + k, 0:R], ACT.Exp,
                                         scale=-1.0).then_inc(s["r_done"], 1)
                    if sums_ahead and m == KD - 1:
                        z_high(i - 1, 0, first=isinstance(i, int) and i == 1)
                    act.wait_ge(s["m_done"], n + 1)
                    nc.scalar.activation(h1h[:, m, :], tmp[:, 6 + k, 0:R], ACT.Copy).then_inc(s["hi_done"], 1)
                if ahead:
                    rows_norm(i + 1, 0)
                if sums_ahead:
                    z_high(i - 1, 1, first=isinstance(i, int) and i == 1)
                if ahead:
                    rows_norm(i + 1, 1)

            def layer2(i):
                n0 = 2 * KD * i + KD
                for step in range(KD + 2):
                    if step < KD:
                        n, k = n0 + step, step % 2
                        act.wait_ge(s["layer_up"], n + 1)
                        act.wait_ge(s["t_done"], n - 1)
                        nc.scalar.activation(tmp[:, k, 0:R], banks[step][:, 0:R], ACT.Exp,
                                             bias=b2_col[:, step:step + 1]).then_inc(s["exp_done"], 1)
                    if 1 <= step <= KD:
                        n, k = n0 + step - 1, (step - 1) % 2
                        act.wait_ge(s["t_done"], n + 1)
                        act.wait_ge(s["m_done"], n - 1)
                        nc.scalar.activation(tmp[:, 4 + k, 0:R], tmp[:, 2 + k, 0:R], ACT.Ln,
                                             bias=two_col[:, :]).then_inc(s["log_done"], 1)
                        act.wait_ge(s["log_done"], n + 1)
                        nc.scalar.activation(tmp[:, 4 + k, 0:R], tmp[:, 4 + k, 0:R], ACT.Exp,
                                             scale=-1.0).then_inc(s["r_done"], 1)
                    if step >= 2:
                        n, k = n0 + step - 2, (step - 2) % 2
                        act.wait_ge(s["m_done"], n + 1)
                        nc.scalar.activation(msgh[:, step - 2, :], tmp[:, 6 + k, 0:R], ACT.Copy).then_inc(s["hi_done"], 1)

            def sums(i, first=False):
                for kind, q in (("z", 2), ("c", 0), ("z", 3), ("c", 1), ("c", 2), ("c", 3)):
                    if kind == "z":
                        z_high(i, q)
                    else:
                        act.wait_ge(s["c_up"], S * i + q + 1)
                        if not first:
                            act.wait_ge(s["scattered"], 16 * S * i)
                        nc.scalar.activation(zsum[:, q, :], banks[6 + q % 2][0:P, :], ACT.Copy).then_inc(s["c_out"], 1)

            rows_rstd(0)
            rows_norm(0, 0)
            rows_norm(0, 1)
            groups(0)
            layer1(0, sums_ahead=False, first=True)
            groups(1)
            layer2(0)
            layer1(1)
            sums(0, first=True)
            groups(2)
            layer2(1)
            with act.Fori(2, NE - 1) as i:
                layer1(i)
                sums(i - 1)
                groups(i + 1)
                layer2(i)
            layer1(NE - 1, ahead=False)
            sums(NE - 2)
            layer2(NE - 1)
            z_high(NE - 1, 0)
            z_high(NE - 1, 1)
            sums(NE - 1)
            act.drain().then_inc(s["edges_over"], 1)
            act.wait_ge(s["edges_over"], 5)

            for n in range(2):
                act.wait_ge(s[("n_staged", "n_staged1")[n]], 16)
                nc.scalar.activation(node_pieces[n][1], ob[:, n, :, :], ACT.Copy).then_inc(s["n_hi"], 1)

            def norm_guess(at, aggregated, n):
                act.wait_ge(s["aggr2"], aggregated)
                nc.scalar.activation(lnv[:, at], mv[:, at, 1], ACT.Ln, bias=eps_col[0:P, :]).then_inc(s["lns_log"], 1)
                act.wait_ge(s["lns_log"], n)
                nc.scalar.activation(rstd[:, at], lnv[:, at], ACT.Exp, scale=-0.5).then_inc(s["lns_guess"], 1)

            def turned(up, done, bank, to):
                for q in range(S):
                    act.wait_ge(s[up], q + 1)
                    nc.scalar.activation(to[:, q, :, 0:P], turned_of(bank), ACT.Copy).then_inc(s[done], 1)

            norm_guess(slice(0, S), S, 1)
            turned("xt_up", "xt_hi", 4, xTh)
            for step in range(S + 2):
                if step < S:
                    k = step % 2
                    act.wait_ge(s["z_done"], step + 1)
                    if step >= 2:
                        act.wait_ge(s["nt_done"], step - 1)
                    nc.scalar.activation(ne[:, k, :], nz[:, k, :], ACT.Exp).then_inc(s["ne_done"], 1)
                if 1 <= step <= S:
                    k = (step - 1) % 2
                    act.wait_ge(s["nt_done"], step)
                    if step >= 3:
                        act.wait_ge(s["u_done"], step - 2)
                    nc.scalar.activation(nr[:, k, :], nt[:, k, :], ACT.Ln, bias=two_col[0:P, :]).then_inc(s["nl_done"], 1)
                    act.wait_ge(s["nl_done"], step)
                    nc.scalar.activation(nr[:, k, :], nr[:, k, :], ACT.Exp, scale=-1.0).then_inc(s["nr_done"], 1)
                if step >= 2:
                    act.wait_ge(s["ut_up"], step - 1)
                    nc.scalar.activation(uTh[:, step - 2, :, 0:P], turned_of(5), ACT.Copy).then_inc(s["ut_hi"], 1)
            norm_guess(slice(S, 2 * S), 2 * S, 2)
            act.drain().then_inc(s["first_over"], 1)
            act.wait_ge(s["first_over"], 5)

            for to, of in (
                [(rule[:, :], node_rule), (fb3[:, :], F_b3.rearrange("(k p) -> p k", p=128))]
                + [(fW1T[:, :, H * g:H * (g + 1)], F_W1T.rearrange("(k p) h -> p k h", p=128)) for g in range(G)]
                + [(fW3[:, :, H * g:H * (g + 1)], F_W3.rearrange("(k p) h -> p k h", p=128)) for g in range(G)]
                + [(fb1[H * g:H * (g + 1), :], F_b1.rearrange("(h a) -> h a", a=1)) for g in range(G)]
                + [(fb2[H * g:H * (g + 1), :], F_b2.rearrange("(h a) -> h a", a=1)) for g in range(G)]
                + [(times[H * g:H * (g + 1), :], time_rule[KV - 1:KV, g * T:(g + 1) * T].to_broadcast([H, T]))
                   for g in range(G)]
            ):
                act.dma_start(to, of, allow_slow_non_contiguous=True).then_inc(s["o_loaded"], 16)
            act.wait_ge(s["o_set"], 6)
            for g in range(G):
                act.dma_start(fW2[H * g:H * (g + 1), H * g:H * (g + 1)], F_W2T).then_inc(s["o_loaded"], 16)
            act.wait_ge(s["y0_stat"], 3)
            nc.scalar.activation(y0_s[:, 0:1], y0_mv[:, 1:2], ACT.Ln, bias=eps_col[0:1, :]).then_inc(s["y0_log"], 1)
            act.wait_ge(s["y0_log"], 1)
            nc.scalar.activation(y0_s[:, 1:2], y0_s[:, 0:1], ACT.Exp, scale=-0.5).then_inc(s["y0_guess"], 1)
            act.wait_ge(s["o_loaded"], 16 * O_LOADS)
            with act.Fori(0, PICARD) as it:
                act.wait_ge(s["q_a"], it + 1)
                nc.scalar.activation(gq[:, :], banks[0][0:H, 0:NQ], ACT.Tanh, bias=fb1[0:H, :]).then_inc(s["q_g"], 1)
                act.wait_ge(s["q_w"], it + 1)
                nc.scalar.activation(hq[:, :], banks[1][0:H, 0:NQ], ACT.Tanh, bias=fb2[0:H, :]).then_inc(s["q_h"], 1)
            act.wait_ge(s["o_slope"], 3)
            for n in range(len(STAGES) + STAGE_LAG):
                if n < len(STAGES):
                    st, c = STAGES[n]
                    bias = (fb1, bias_half, bias_half, bias_full)[st]
                    if n >= 4:
                        act.wait_ge(s["st_x"], n - 3)
                    if st == 0:
                        act.wait_ge(s["ag_out"], c + 1)
                        of = A_guess[:, c * C:(c + 1) * C]
                    else:
                        act.wait_ge(s["st_zs"], n - NC + 1)
                        of = zst[:, n % 2, :]
                    nc.scalar.activation(gst[:, n % 4, :], of, ACT.Tanh, bias=bias[:, :]).then_inc(s["st_g"], 1)
                if n >= STAGE_LAG:
                    m = n - STAGE_LAG
                    st, c = STAGES[m]
                    act.wait_ge(s["st_x"], m + 1)
                    if st > 0:
                        act.wait_ge(s["st_acc"], m - NC + 1)
                    nc.scalar.activation(hst[:, c, :], banks[4 + m % 4][:, 0:C], ACT.Tanh, bias=fb2[:, :]).then_inc(s["st_h"], 1)
            act.wait_ge(s["flag_made"], 1)
            checked = act.value_load(flag[0:1, 0:1], min_val=0, max_val=1)
            with act.If(checked == 0):
                with act.Fori(0, N) as t:
                    act.wait_ge(s["sq_bias"], t + 1)
                    for st in range(4):
                        act.wait_ge(s["sq_pre"], 4 * t + st + 1)
                        nc.scalar.activation(seq_g[:, :], banks[0][0:H, 0:1], ACT.Tanh,
                                             bias=seq_bias[:, (0, 1, 1, 2)[st]:(0, 1, 1, 2)[st] + 1]).then_inc(s["sq_g"], 1)
                        act.wait_ge(s["sq_x"], 4 * t + st + 1)
                        nc.scalar.activation(seq_h[:, st:st + 1], banks[1][0:H, 0:1], ACT.Tanh,
                                             bias=fb2[0:H, :]).then_inc(s["sq_h"], 1)
            act.drain().then_inc(s["scan_over"], 1)
            act.wait_ge(s["scan_over"], 5)

            act.preload_act_table_set("natural_log_exp_and_others")
            def nodes(j, b):
                for q in range(S):
                    n = S * j + q
                    if has(j, q, 2):
                        act.wait_ge(s["xt_up"], n + 3)
                        nc.scalar.activation(xTh[:, (q + 2) % S, :, 0:P], turned_of(4), ACT.Copy).then_inc(s["xt_hi"], 1)
                    if has(j, q, -2):
                        act.wait_ge(s["ut_up"], n - 1)
                        nc.scalar.activation(uTh[:, (q - 2) % S, :, 0:P], turned_of(5), ACT.Copy).then_inc(s["ut_hi"], 1)
                    if has(j, q, -1):
                        k = (q - 1) % 2
                        act.wait_ge(s["nt_done"], n)
                        act.wait_ge(s["u_done"], n - 2)
                        nc.scalar.activation(nr[:, k, :], nt[:, k, :], ACT.Ln, bias=two_col[0:P, :]).then_inc(s["nl_done"], 1)
                        act.wait_ge(s["nl_done"], n)
                        nc.scalar.activation(nr[:, k, :], nr[:, k, :], ACT.Exp, scale=-1.0).then_inc(s["nr_done"], 1)
                    if q == 0 and norms(j):
                        norm_guess(norms(j), aggregated(j), j + 3)
                    if has(j, q, 0):
                        act.wait_ge(s["z_done"], n + 1)
                        act.wait_ge(s["nt_done"], n - 1)
                        nc.scalar.activation(ne[:, q % 2, :], nz[:, q % 2, :], ACT.Exp).then_inc(s["ne_done"], 1)
                    if has(j, q, 4):
                        if q == 0:
                            act.wait_ge(s["lns_newton"], 6 * (j + 3))
                        act.wait_ge(s["xt_up"], n + 1)
                        act.wait_ge(s["xnb_done"], n + 1)
                        nc.scalar.activation(xn[:, q, :], xraw[:, 1 - b, q, :], ACT.Identity, bias=shift[:, q:q + 1],
                                             scale=rstd[:, q:q + 1]).then_inc(s["xn_done"], 1)
                    if has(j, q, -8):
                        if q == 0:
                            act.wait_ge(s["lns_newton"], 6 * (j + 3))
                        nc.scalar.activation(yb[:, b, q, :], yb[:, b, q, :], ACT.Identity, bias=shift[:, S + q:S + q + 1],
                                             scale=rstd[:, S + q:S + q + 1]).then_inc(s["yn_done"], 1)

            run_nodes(act, nodes)

        @block.vector
        def _(dve):
            dve.wait_ge(s["smalls_in"], 16 * SMALLS)
            nc.vector.tensor_copy(dst_allf[:, :], dst_all[:, :]).then_inc(s["dstf_made"], 1)
            for n in range(EW):
                _, hi, lo, _ = edge_pieces[n]
                dve.wait_ge(s["split_hi"], n + 1)
                nc.vector.tensor_tensor(lo, piece_in(n), hi.bitcast(f32), ALU.subtract).then_inc(s["split_lo"], 1)
            dve.wait_ge(s["dstf_made"], 1)
            dve.wait_ge(s["spare_made"], 1)

            def refine(small, var, chain, count):
                v, r, sq = small
                nc.vector.tensor_scalar(v, var, EPS, None, ALU.add).then_inc(s[chain], 1)
                nc.vector.tensor_tensor(sq, r, r, ALU.mult).then_inc(s[chain], 1)
                dve.wait_ge(s[chain], count + 2)
                nc.vector.tensor_tensor(sq, sq, v, ALU.mult).then_inc(s[chain], 1)
                dve.wait_ge(s[chain], count + 3)
                nc.vector.tensor_scalar(sq, sq, -0.5, 1.5, ALU.mult, ALU.add).then_inc(s[chain], 1)
                dve.wait_ge(s[chain], count + 4)
                nc.vector.tensor_tensor(r, r, sq, ALU.mult).then_inc(s[chain], 1)
                dve.wait_ge(s[chain], count + 5)

            def rows_stats(i, part):
                if part == 0:
                    dve.wait_ge(s["rows_in"], 16 * 2 * S * (i + 1))
                for a in (2 * part, 2 * part + 1):
                    nc.vector.bn_stats(e_stats[:, a, :], rows[:, a, :]).then_inc(s["stats_done"], 1)

            def rows_aggregate(i):
                wait_apart(dve, s["stats_done"], 2 * S * (i + 1))
                for a in range(2 * S):
                    nc.vector.bn_aggr(e_mv[:, a, :], e_stats[:, a, :]).then_inc(s["aggr_done"], 1)

            def rows_factors(i):
                dve.wait_ge(s["aggr_done"], 2 * S * (i + 1))
                dve.wait_ge(s["ln_guess"], i + 1)
                refine((e_var[:, :], e_rstd[:, :], e_sq[:, :]), e_mv[:, :, 1], "newton", 6 * i)
                nc.vector.scalar_tensor_tensor(e_shift[:, :], e_mv[:, :, 0], -1.0, e_rstd[:, :], ALU.mult,
                                               ALU.mult).then_inc(s["newton"], 1)

            def rows_norm(i, part):
                for a in (S + 2 * part, S + 2 * part + 1):
                    nc.vector.tensor_scalar(rows[:, a, :], rows[:, a, :], e_mv[:, a, 0:1], e_rstd[:, a:a + 1],
                                            ALU.subtract, ALU.mult).then_inc(s["rows_normed_dve"], 1)

            def groups(i):
                for g in range(NT):
                    dve.wait_ge(s["group_hi"], NT * i + g + 1)
                    nc.vector.tensor_tensor(group_to(g, fTl), group_of(g), group_to(g, fTh).bitcast(f32),
                                            ALU.subtract).then_inc(s["group_lo"], 1)

            def layer1(i, sums_ahead=True, ahead=True, first=False):
                for m in range(KD):
                    n, k = 2 * KD * i + m, m % 2
                    e, t, r, v = (tmp[:, 2 * a + k, 0:R] for a in range(4))
                    dve.wait_ge(s["exp_done"], n + 1)
                    nc.vector.tensor_scalar(e, e, EXP_MAX, None, ALU.min).then_inc(s["cut_done"], 1)
                    dve.wait_ge(s["cut_done"], n + 1)
                    if not (first and m < 2):
                        dve.wait_ge(s["log_done"], n - 1)
                        dve.wait_ge(s["w_done"], n - 1)
                    nc.vector.scalar_tensor_tensor(t, e, 2.0, e, ALU.add, ALU.mult).then_inc(s["t_done"], 1)
                    dve.wait_ge(s["t_done"], n + 1)
                    if not (first and m < 2):
                        dve.wait_ge(s["lo_done"], n - 1)
                    nc.vector.scalar_tensor_tensor(v, banks[m][:, 0:R], b1_col[:, m:m + 1], t, ALU.add,
                                                   ALU.mult).then_inc(s["w_done"], 1)
                    if m == 0 and sums_ahead:
                        shared(i - 1)
                    if ahead and m in (1, 2):
                        rows_stats(i + 1, 2 * m - 2)
                    if ahead and m == 3:
                        rows_factors(i + 1)
                    dve.wait_ge(s["w_done"], n + 1)
                    dve.wait_ge(s["r_done"], n + 1)
                    nc.vector.tensor_tensor(v, v, r, ALU.mult).then_inc(s["m_done"], 1)
                    if ahead and m in (1, 2):
                        rows_stats(i + 1, 2 * m - 1)
                    if sums_ahead and m == 3:
                        z_low(i - 1, 0)
                    dve.wait_ge(s["hi_done"], n + 1)
                    nc.vector.tensor_tensor(h1l[:, m, :], v, h1h[:, m, :].bitcast(f32), ALU.subtract).then_inc(s["lo_done"], 1)
                    if ahead and m == 2:
                        rows_aggregate(i + 1)
                if ahead:
                    rows_norm(i + 1, 0)
                if sums_ahead:
                    z_low(i - 1, 1)
                if ahead:
                    rows_norm(i + 1, 1)

            def layer2(i):
                n0 = 2 * KD * i + KD
                for step in range(KD + 2):
                    if step < KD:
                        n, k = n0 + step, step % 2
                        e, t = tmp[:, k, 0:R], tmp[:, 2 + k, 0:R]
                        dve.wait_ge(s["exp_done"], n + 1)
                        nc.vector.tensor_scalar(e, e, EXP_MAX, None, ALU.min).then_inc(s["cut_done"], 1)
                        dve.wait_ge(s["cut_done"], n + 1)
                        dve.wait_ge(s["log_done"], n - 1)
                        dve.wait_ge(s["w_done"], n - 1)
                        nc.vector.scalar_tensor_tensor(t, e, 2.0, e, ALU.add, ALU.mult).then_inc(s["t_done"], 1)
                    if 1 <= step <= KD:
                        n, k, m = n0 + step - 1, (step - 1) % 2, step - 1
                        t, r, v = tmp[:, 2 + k, 0:R], tmp[:, 4 + k, 0:R], tmp[:, 6 + k, 0:R]
                        dve.wait_ge(s["t_done"], n + 1)
                        dve.wait_ge(s["lo_done"], n - 1)
                        nc.vector.scalar_tensor_tensor(v, banks[m][:, 0:R], b2_col[:, m:m + 1], t, ALU.add,
                                                       ALU.mult).then_inc(s["w_done"], 1)
                        dve.wait_ge(s["w_done"], n + 1)
                        dve.wait_ge(s["r_done"], n + 1)
                        nc.vector.tensor_tensor(v, v, r, ALU.mult).then_inc(s["m_done"], 1)
                    if step >= 2:
                        n, k = n0 + step - 2, (step - 2) % 2
                        dve.wait_ge(s["hi_done"], n + 1)
                        nc.vector.tensor_tensor(msgl[:, step - 2, :], tmp[:, 6 + k, 0:R], msgh[:, step - 2, :].bitcast(f32),
                                                ALU.subtract).then_inc(s["lo_done"], 1)

            def shared(i):
                dve.wait_ge(s["drow_in"], 16 * (i + 1))
                nc.vector.tensor_copy(drow_f[:, :], drow_i[:, :]).then_inc(s["seg"], 1)
                nc.vector.tensor_copy(dcol_f[:, :], dst_allf[:, bass.ds(i * S, S)]).then_inc(s["seg"], 1)
                dve.wait_ge(s["seg"], 7 * i + 2)
                if not (isinstance(i, int) and i == 0):
                    dve.wait_ge(s["c_up"], S * i)
                for q in range(S):
                    nc.vector.tensor_scalar(same[:, q, 0:P], drow_f[:, q * P:(q + 1) * P], dcol_f[:, q:q + 1], None,
                                            ALU.is_equal).then_inc(s["same_made"], 1)

            def sum_rows(i):
                dve.wait_ge(s["same_made"], S * (i + 1))
                nc.vector.tensor_tensor(same_earlier[:, :, :], same[:, :, 0:P].bitcast(f32),
                                        earlier[:, :].unsqueeze(1).to_broadcast([P, S, P]), ALU.mult).then_inc(s["seg"], 1)
                dve.wait_ge(s["seg"], 7 * i + 3)
                nc.vector.tensor_reduce(n_earlier[:, :], same_earlier[:, :, :], AX.X, ALU.add).then_inc(s["seg"], 1)
                nc.vector.tensor_scalar(to_spare[:, :], dcol_f[:, :], -1.0, spare_row[:, :], ALU.mult, ALU.add).then_inc(s["seg"], 1)
                dve.wait_ge(s["seg"], 7 * i + 5)
                nc.vector.tensor_scalar(n_earlier[:, :], n_earlier[:, :], 1.0, None, ALU.min).then_inc(s["seg"], 1)
                dve.wait_ge(s["seg"], 7 * i + 6)
                nc.vector.tensor_tensor(sum_row[:, :], to_spare[:, :], n_earlier[:, :], ALU.mult).then_inc(s["seg"], 1)
                dve.wait_ge(s["seg"], 7 * i + 7)
                if not (isinstance(i, int) and i == 0):
                    dve.wait_ge(s["scattered"], 16 * S * i)
                nc.vector.tensor_tensor(sum_row_i[:, :], sum_row[:, :], dcol_f[:, :], ALU.add).then_inc(s["sumrow_made"], 1)

            def z_low(i, q):
                dve.wait_ge(s["z_hi"], S * i + q + 1)
                nc.vector.tensor_tensor(zl[:, q % 2, :], banks[4 + q % 2][0:P, :], zh[:, q % 2, :].bitcast(f32),
                                        ALU.subtract).then_inc(s["z_lo"], 1)

            def rest_of_sums(i):
                z_low(i, 2)
                sum_rows(i)
                z_low(i, 3)

            for part in range(S):
                rows_stats(0, part)
            rows_aggregate(0)
            rows_factors(0)
            rows_norm(0, 0)
            rows_norm(0, 1)
            groups(0)
            layer1(0, sums_ahead=False, first=True)
            groups(1)
            layer2(0)
            layer1(1)
            rest_of_sums(0)
            groups(2)
            layer2(1)
            with dve.Fori(2, NE - 1) as i:
                layer1(i)
                rest_of_sums(i - 1)
                groups(i + 1)
                layer2(i)
            layer1(NE - 1, ahead=False)
            rest_of_sums(NE - 2)
            layer2(NE - 1)
            shared(NE - 1)
            z_low(NE - 1, 0)
            z_low(NE - 1, 1)
            rest_of_sums(NE - 1)
            dve.drain().then_inc(s["edges_over"], 1)
            dve.wait_ge(s["edges_over"], 5)

            for n in range(2):
                _, hi, lo = node_pieces[n]
                dve.wait_ge(s["n_hi"], n + 1)
                nc.vector.tensor_tensor(lo, ob[:, n, :, :], hi.bitcast(f32), ALU.subtract).then_inc(s["n_lo"], 1)

            def aggregate(at, stats_x, stats_y, before):
                if at.start == 0:
                    wait_apart(dve, s["xs_done"], stats_x)
                if at.stop == 2 * S:
                    wait_apart(dve, s["ys_done"], stats_y)
                for a in range(at.start, at.stop):
                    nc.vector.bn_aggr(mv[:, a, :], stats[:, a, :]).then_inc(s["aggr2"], 1)
                dve.wait_ge(s["aggr2"], before)

            def norm_factors(at, n):
                dve.wait_ge(s["lns_guess"], n)
                refine((var_eps[:, at], rstd[:, at], sq[:, at]), mv[:, at, 1], "lns_newton", 6 * (n - 1))
                nc.vector.scalar_tensor_tensor(shift[:, at], mv[:, at, 0], -1.0, rstd[:, at], ALU.mult,
                                               ALU.mult).then_inc(s["lns_newton"], 1)

            def turned(high, done, bank, hi, lo):
                for q in range(S):
                    dve.wait_ge(s[high], q + 1)
                    nc.vector.tensor_tensor(lo[:, q, :, 0:P], turned_of(bank), hi[:, q, :, 0:P].bitcast(f32),
                                            ALU.subtract).then_inc(s[done], 1)

            for q in range(S):
                dve.wait_ge(s[X_IN[0][q // 2]], 32)
                nc.vector.bn_stats(stats[:, q, :], xraw[:, 0, q, :]).then_inc(s["xs_done"], 1)
            aggregate(slice(0, S), S, 0, S)
            norm_factors(slice(0, S), 1)
            dve.wait_ge(s["lns_newton"], 6)
            for q in range(S):
                nc.vector.tensor_scalar(xn[:, q, :], xraw[:, 0, q, :], mv[:, q, 0:1], rstd[:, q:q + 1],
                                        ALU.subtract, ALU.mult).then_inc(s["xn_done"], 1)
            turned("xt_hi", "xt_lo", 4, xTh, xTl)
            for step in range(S + 3):
                if 2 <= step < S + 2:
                    n, k = step - 2, (step - 2) % 2
                    dve.wait_ge(s["nt_done"], n + 1)
                    if n >= 2:
                        dve.wait_ge(s["ut_up"], n - 1)
                    nc.vector.tensor_tensor(u[:, k, :], nz[:, k, :], nt[:, k, :], ALU.mult).then_inc(s["nw_done"], 1)
                    dve.wait_ge(s["nw_done"], n + 1)
                    dve.wait_ge(s["nr_done"], n + 1)
                    nc.vector.tensor_tensor(u[:, k, :], u[:, k, :], nr[:, k, :], ALU.mult).then_inc(s["u_done"], 1)
                if 3 <= step:
                    q = step - 3
                    dve.wait_ge(s["ut_hi"], q + 1)
                    nc.vector.tensor_tensor(uTl[:, q, :, 0:P], turned_of(5), uTh[:, q, :, 0:P].bitcast(f32),
                                            ALU.subtract).then_inc(s["ut_lo"], 1)
                if step < S:
                    n, k = step, step % 2
                    dve.wait_ge(s["u_up"], n + 1)
                    dve.wait_ge(s[AGG_IN[step // 2]], 32)
                    if step >= 2:
                        dve.wait_ge(s["ne_done"], n - 1)
                        dve.wait_ge(s["nw_done"], n - 1)
                    nc.vector.tensor_tensor(nz[:, k, :], banks[k][0:P, :], agg[:, step, :], ALU.add).then_inc(s["z_done"], 1)
                if 1 <= step <= S:
                    n, k = step - 1, (step - 1) % 2
                    dve.wait_ge(s["ne_done"], n + 1)
                    nc.vector.tensor_scalar(ne[:, k, :], ne[:, k, :], EXP_MAX, None, ALU.min).then_inc(s["nc_done"], 1)
                    dve.wait_ge(s["nc_done"], n + 1)
                    if step >= 3:
                        dve.wait_ge(s["nl_done"], n - 1)
                        dve.wait_ge(s["nw_done"], n - 1)
                    nc.vector.scalar_tensor_tensor(nt[:, k, :], ne[:, k, :], 2.0, ne[:, k, :], ALU.add,
                                                   ALU.mult).then_inc(s["nt_done"], 1)
            for q in range(S):
                dve.wait_ge(s["y_up"], q + 1)
                dve.wait_ge(s["xnb_done"], q + 1)
                nc.vector.tensor_tensor(yb[:, 0, q, :], banks[2 + q % 2][0:P, :], xnb[:, 0, q, :], ALU.add).then_inc(s["y_added"], 1)
                dve.wait_ge(s["y_added"], q + 1)
                nc.vector.bn_stats(stats[:, S + q, :], yb[:, 0, q, :]).then_inc(s["ys_done"], 1)
            aggregate(slice(S, 2 * S), 0, S, 2 * S)
            norm_factors(slice(S, 2 * S), 2)
            dve.wait_ge(s["lns_newton"], 12)
            for q in range(S):
                nc.vector.tensor_scalar(yb[:, 0, q, :], yb[:, 0, q, :], mv[:, S + q, 0:1], rstd[:, S + q:S + q + 1],
                                        ALU.subtract, ALU.mult).then_inc(s["yn_done"], 1)
            dve.wait_ge(s["yx_done"], S)
            dve.drain().then_inc(s["first_over"], 1)
            dve.wait_ge(s["first_over"], 5)

            nc.vector.tensor_tensor(y0_x1[:, :], x1_first[0:1, 0, :], beta_bc[0:1, :], ALU.add).then_inc(s["y0_stat"], 1)
            dve.wait_ge(s["y0_stat"], 1)
            nc.vector.bn_stats(y0_st[:, :], y0_x1[:, :]).then_inc(s["y0_stat"], 1)
            dve.wait_ge(s["y0_stat"], 2)
            nc.vector.bn_aggr(y0_mv[:, :], y0_st[:, :]).then_inc(s["y0_stat"], 1)
            dve.wait_ge(s["y0_stat"], 3)
            dve.wait_ge(s["y0_guess"], 1)
            refine((y0_s[:, 2:3], y0_s[:, 1:2], y0_s[:, 3:4]), y0_mv[:, 1:2], "y0_newton", 0)
            nc.vector.tensor_scalar(y0[:, :], y0_x1[:, :], y0_mv[:, 0:1], y0_s[:, 1:2],
                                    ALU.subtract, ALU.mult).then_inc(s["y0_made"], 1)
            dve.wait_ge(s["y0_made"], 1)
            nc.vector.tensor_tensor(y0_beta[:, :], y0[:, :], beta_bc[0:1, :], ALU.add).then_inc(s["y0_made"], 1)
            dve.wait_ge(s["o_loaded"], 16 * O_LOADS)
            dve.wait_ge(s["o_set"], O_SET)
            dve.wait_ge(s["o_mat_up"], 1)
            nc.vector.tensor_copy(M_T[:, :], banks[0][0:H, 0:H]).then_inc(s["o_mats"], 1)
            for to, scale in ((M_half, DT / 2), (M_full, DT), (M_six, DT / 6)):
                nc.vector.scalar_tensor_tensor(to[:, :], banks[0][:, 0:128], scale, blocks[:, :], ALU.mult,
                                               ALU.mult).then_inc(s["o_mats"], 1)
            dve.wait_ge(s["o_slope_up"], 1)
            nc.vector.tensor_copy(slope[:, :], banks[1][:, 0:1]).then_inc(s["o_slope"], 1)
            dve.wait_ge(s["o_slope"], 1)
            nc.vector.tensor_scalar(bias_half[:, :], slope[:, :], DT / 2, fb1[:, :], ALU.mult, ALU.add).then_inc(s["o_slope"], 1)
            nc.vector.tensor_scalar(bias_full[:, :], slope[:, :], DT, fb1[:, :], ALU.mult, ALU.add).then_inc(s["o_slope"], 1)
            nc.vector.tensor_copy(y0b3[:, :, 1], fb3[:, :]).then_inc(s["y0T"], 1)
            dve.wait_ge(s["y0T_up"], 1)
            nc.vector.tensor_copy(y0b3[:, :, 0], banks[2][:, 0:KD]).then_inc(s["y0T"], 1)
            dve.wait_ge(s["a_up"], 2)
            nc.vector.tensor_copy(a0[:, :], banks[3][:, 0:1]).then_inc(s["a_made"], 1)
            nc.vector.tensor_copy(V[H:KV, :], banks[4][H:KV, 0:H]).then_inc(s["V_made"], 1)
            with dve.Fori(0, PICARD) as it:
                dve.wait_ge(s["q_v"], it + 1)
                nc.vector.tensor_copy(V[0:NQ, :], banks[2][0:NQ, 0:H]).then_inc(s["V_made"], 1)
            for c in range(NC):
                dve.wait_ge(s["ag_up"], c + 1)
                nc.vector.tensor_copy(A_guess[:, c * C:(c + 1) * C], banks[c % 4][:, 0:C]).then_inc(s["ag_out"], 1)
            for n in range(NC, len(STAGES) + SUM_LAG):
                if n < len(STAGES):
                    st, c = STAGES[n]
                    dve.wait_ge(s["st_z"], n - NC + 1)
                    dve.wait_ge(s["ag_out"], c + 1)
                    if n >= NC + 2:
                        dve.wait_ge(s["st_g"], n - 1)
                    nc.vector.tensor_tensor(zst[:, n % 2, :], banks[n % 4][:, 0:C], A_guess[:, c * C:(c + 1) * C],
                                            ALU.add).then_inc(s["st_zs"], 1)
                for m in ((n - SUM_LAG,) if n > NC else range(n - SUM_LAG + 1)):
                    st, c = STAGES[m]
                    dve.wait_ge(s["st_h"], m + 1)
                    h, S_c = hst[:, c, :], Ssum[:, c, :]
                    if st > 0:
                        dve.wait_ge(s["st_acc"], m - NC + 1)
                    if st == 0:
                        op = nc.vector.tensor_copy(S_c, h)
                    elif st < 3:
                        op = nc.vector.scalar_tensor_tensor(S_c, h, 2.0, S_c, ALU.mult, ALU.add)
                    else:
                        op = nc.vector.tensor_tensor(S_c, h, S_c, ALU.add)
                    op.then_inc(s["st_acc"], 1)
            for c in range(NC):
                dve.wait_ge(s["st_acc"], 3 * NC + c + 1)
                if c:
                    dve.wait_ge(s["scan_done"], c)
                nc.vector.tensor_tensor_scan(Pex[:, 1 + c * C:1 + (c + 1) * C], zeros[:, :], Ssum[:, c, :],
                                             Pex[:, c * C:c * C + 1], ALU.add, ALU.add).then_inc(s["scan_done"], 1)
            dve.wait_ge(s["of_up"], 1)
            nc.vector.tensor_copy(off[:, :], banks[4][:, 0:1]).then_inc(s["of_done"], 1)
            dve.wait_ge(s["bs_up"], 1)
            dve.wait_ge(s["a_made"], 1)
            nc.vector.tensor_tensor(base[:, :], banks[5][:, 0:1], a0[:, :], ALU.add).then_inc(s["bs_done"], 1)
            dve.wait_ge(s["bs_done"], 1)
            nc.vector.tensor_scalar(A_base[:, :], times[:, :], slope[:, :], base[:, :], ALU.mult, ALU.add).then_inc(s["ab_made"], 1)
            dve.wait_ge(s["ab_made"], 1)
            for c in range(NC):
                dve.wait_ge(s["an_up"], c + 1)
                if c >= 2:
                    dve.wait_ge(s["an_max"], c - 1)
                nc.vector.tensor_tensor(dev[:, c % 2, :], banks[c % 4][:, 0:C], A_base[:, c * C:(c + 1) * C],
                                        ALU.add).then_inc(s["an_dev"], 1)
                dve.wait_ge(s["an_dev"], c + 1)
                nc.vector.tensor_tensor(dev[:, c % 2, :], dev[:, c % 2, :], A_guess[:, c * C:(c + 1) * C],
                                        ALU.subtract).then_inc(s["an_dif"], 1)
                dve.wait_ge(s["an_dif"], c + 1)
                nc.vector.tensor_reduce(devmax[:, c:c + 1], dev[:, c % 2, :], AX.X, ALU.max,
                                        apply_absolute_value=True).then_inc(s["an_max"], 1)
            dve.wait_ge(s["an_max"], NC)
            nc.vector.tensor_reduce(devtop[:, :], devmax[:, :], AX.X, ALU.max).then_inc(s["dv_top"], 1)
            nc.vector.tensor_scalar(A_base[:, :], Pex[:, 0:T], off[:, :], DT / 6, ALU.add, ALU.mult).then_inc(s["pg_made"], 1)
            dve.wait_ge(s["dv_row"], 1)
            nc.vector.tensor_reduce(devrow[:, :], banks[6][0:1, 0:128], AX.X, ALU.max).then_inc(s["dv_rowed"], 1)
            dve.wait_ge(s["dv_rowed"], 1)
            nc.vector.tensor_scalar(flag[:, :], devrow[:, :], TOL, None, ALU.is_le).then_inc(s["flag_made"], 1)
            dve.wait_ge(s["flag_made"], 1)
            checked = dve.value_load(flag[0:1, 0:1], min_val=0, max_val=1)
            with dve.If(checked == 0):
                nc.vector.memset(seq_P[:, :], 0.0).then_inc(s["sq_sum"], 1)
                nc.vector.tensor_tensor(seq_a[:, :], a0[0:H, :], fb1[0:H, :], ALU.add).then_inc(s["sq_set"], 1)
                dve.wait_ge(s["sq_set"], 1)
                dve.wait_ge(s["sq_sum"], 1)
                with dve.Fori(0, N // C) as b:
                    wait_apart(dve, s["sq_in"], 16 * (b + 1))
                    with dve.Fori(0, C) as i:
                        t = b * C + i
                        nc.vector.tensor_scalar(seq_blk[:, bass.ds(i, 1)], seq_P[:, :], DT / 6, None, ALU.mult).then_inc(s["sq_blk"], 1)
                        nc.vector.tensor_scalar(seq_bias[:, 0:1], seq_t[:, bass.ds(i, 1)], slope[0:H, :], seq_a[:, :],
                                                ALU.mult, ALU.add).then_inc(s["sq_blk"], 1)
                        dve.wait_ge(s["sq_blk"], 3 * t + 2)
                        nc.vector.tensor_scalar(seq_bias[:, 1:2], slope[0:H, :], DT / 2, seq_bias[:, 0:1],
                                                ALU.mult, ALU.add).then_inc(s["sq_blk"], 1)
                        nc.vector.tensor_scalar(seq_bias[:, 2:3], slope[0:H, :], DT, seq_bias[:, 0:1],
                                                ALU.mult, ALU.add).then_inc(s["sq_bias"], 1)
                        dve.wait_ge(s["sq_h"], 4 * t + 4)
                        nc.vector.tensor_tensor(seq_S[:, 0:1], seq_h[:, 1:2], seq_h[:, 2:3], ALU.add).then_inc(s["sq_set"], 1)
                        dve.wait_ge(s["sq_set"], 3 * t + 2)
                        nc.vector.scalar_tensor_tensor(seq_S[:, 1:2], seq_S[:, 0:1], 2.0, seq_h[:, 0:1],
                                                       ALU.mult, ALU.add).then_inc(s["sq_set"], 1)
                        dve.wait_ge(s["sq_set"], 3 * t + 3)
                        nc.vector.tensor_tensor(seq_S[:, 2:3], seq_S[:, 1:2], seq_h[:, 3:4], ALU.add).then_inc(s["sq_set"], 1)
                        dve.wait_ge(s["sq_set"], 3 * t + 4)
                        nc.vector.tensor_tensor(seq_P[:, :], seq_P[:, :], seq_S[:, 2:3], ALU.add).then_inc(s["sq_sum"], 1)
                        dve.wait_ge(s["sq_sum"], t + 2)
            dve.drain().then_inc(s["scan_over"], 1)
            dve.wait_ge(s["scan_over"], 5)

            def nodes(j, b):
                for q in range(S):
                    n = S * j + q
                    if q == 0 and norms(j):
                        aggregate(norms(j), S * (j + 2), S * (j - 1), aggregated(j))
                    if has(j, q, 2):
                        w = (q + 2) % S
                        dve.wait_ge(s["xt_hi"], n + 3)
                        nc.vector.tensor_tensor(xTl[:, w, :, 0:P], turned_of(4), xTh[:, w, :, 0:P].bitcast(f32),
                                                ALU.subtract).then_inc(s["xt_lo"], 1)
                    if has(j, q, -2):
                        w = (q - 2) % S
                        dve.wait_ge(s["ut_hi"], n - 1)
                        nc.vector.tensor_tensor(uTl[:, w, :, 0:P], turned_of(5), uTh[:, w, :, 0:P].bitcast(f32),
                                                ALU.subtract).then_inc(s["ut_lo"], 1)
                    if has(j, q, -1):
                        k = (q - 1) % 2
                        dve.wait_ge(s["nw_done"], n)
                        dve.wait_ge(s["nr_done"], n)
                        nc.vector.tensor_tensor(u[:, k, :], u[:, k, :], nr[:, k, :], ALU.mult).then_inc(s["u_done"], 1)
                    if q == 0 and norms(j):
                        norm_factors(norms(j), j + 3)
                    if has(j, q, 0):
                        k = q % 2
                        dve.wait_ge(s["u_up"], n + 1)
                        dve.wait_ge(s[AGG_IN[q // 2]], 32 * (j + 1))
                        dve.wait_ge(s["ne_done"], n - 1)
                        dve.wait_ge(s["nw_done"], n - 1)
                        nc.vector.tensor_tensor(nz[:, k, :], banks[k][0:P, :], agg[:, q, :], ALU.add).then_inc(s["z_done"], 1)
                    if has(j, q, 8):
                        wait_apart(dve, s[X_IN[b][q // 2]], loads_by_parity(j + 2, b))
                        nc.vector.bn_stats(stats[:, q, :], xraw[:, b, q, :]).then_inc(s["xs_done"], 1)
                    if has(j, q, -9, 0):
                        m = n - 9
                        c, w = slot(b, q, -9)
                        dve.wait_ge(s["o_up"], m + 1)
                        if has(j, q, -9):
                            dve.wait_ge(s["yx_done"], m + 1)
                            so_far = ob[0:P, c, w, :]
                        else:
                            so_far = x1_first[:, w, :]
                        nc.vector.tensor_tensor(ob[0:P, c, w, :], banks[6 + (q + 1) % 2][0:P, :], so_far, ALU.add).then_inc(s["o_added"], 1)
                    if has(j, q, 0):
                        k = q % 2
                        dve.wait_ge(s["ne_done"], n + 1)
                        nc.vector.tensor_scalar(ne[:, k, :], ne[:, k, :], EXP_MAX, None, ALU.min).then_inc(s["nc_done"], 1)
                        dve.wait_ge(s["nc_done"], n + 1)
                        dve.wait_ge(s["nl_done"], n - 1)
                        dve.wait_ge(s["nw_done"], n - 1)
                        nc.vector.scalar_tensor_tensor(nt[:, k, :], ne[:, k, :], 2.0, ne[:, k, :], ALU.add,
                                                       ALU.mult).then_inc(s["nt_done"], 1)
                    if has(j, q, -4):
                        m, c = n - 4, 1 - b
                        dve.wait_ge(s["y_up"], m + 1)
                        dve.wait_ge(s["xnb_done"], m + 1)
                        if has(j, q, -12):
                            dve.wait_ge(s["yx_done"], m - 7)
                        nc.vector.tensor_tensor(yb[:, c, q, :], banks[2 + q % 2][0:P, :], xnb[:, c, q, :], ALU.add).then_inc(s["y_added"], 1)
                        dve.wait_ge(s["y_added"], m + 1)
                        nc.vector.bn_stats(stats[:, S + q, :], yb[:, c, q, :]).then_inc(s["ys_done"], 1)

            run_nodes(dve, nodes)

        @block.tensor
        def _(pe):
            def product(to, chunks, signal):
                passes = [(l[a], r[b]) for l, r in chunks for a, b in ((0, 0), (0, 1), (1, 0))]
                for m, (l, r) in enumerate(passes):
                    op = nc.tensor.matmul(to, l, r, start=(m == 0), stop=(m == len(passes) - 1))
                op.then_inc(signal, 1)

            def turn(to, of, signal=None):
                op = nc.tensor.transpose(to, of, ident[0:P, 0:P])
                if signal is not None:
                    op.then_inc(signal, 1)

            def group(i, g, peeled=False):
                if g < 2 * S:
                    wait_apart(pe, s["rows_normed" if g < S else "rows_normed_dve"], S * i + g % S + 1)
                else:
                    wait_apart(pe, s["attr_in"], 16 * (i + 1))
                bank = banks[4 + g % 4]
                if g >= 4:
                    wait_apart(pe, s["group_lo"], NT * i + g - 3)
                elif not peeled:
                    wait_apart(pe, s["z_lo"] if g < 2 else s["c_out"], S * (i - 1) - 1 + g % 2)
                for k in range(KD):
                    of = rows[:, g, k * 128:(k + 1) * 128] if g < 2 * S else attr[:, k, :]
                    to = bank[:, k * 128:k * 128 + P] if g < 2 * S else bank[0:DE, k * P:(k + 1) * P]
                    turn(to, of, s["groups_up"] if k == KD - 1 else None)

            def groups(i, start=0, peeled=False):
                for g in range(start, NT):
                    group(i, g, peeled)

            def layer1(i, first=False):
                pe.wait_ge(s["group_lo"], NT * (i + 1))
                if first:
                    pe.wait_ge(s["split_lo"], 3)
                for m in range(KD):
                    cols = slice(m * 128, (m + 1) * 128)
                    if not first:
                        pe.wait_ge(s["w_done"], 2 * KD * i + m - 3)
                    product(banks[m][:, 0:R],
                            [((W1h[0:w, k, cols], W1l[0:w, k, cols]), (fTh[0:w, k, :], fTl[0:w, k, :]))
                             for k, w in [(k, 128) for k in range(2 * KD)] + [(2 * KD, DE)]], s["layer_up"])

            def layer2(i, first=False):
                pe.wait_ge(s["lo_done"], 2 * KD * i + KD)
                if first:
                    pe.wait_ge(s["split_lo"], EW)
                for m in range(KD):
                    cols = slice(m * 128, (m + 1) * 128)
                    pe.wait_ge(s["w_done"], 2 * KD * i + KD + m - 3)
                    product(banks[m][:, 0:R],
                            [((W2h[:, k, cols], W2l[:, k, cols]), (h1h[:, k, :], h1l[:, k, :])) for k in range(KD)],
                            s["layer_up"])

            def sums(i, ahead=True):
                pe.wait_ge(s["lo_done"], 2 * KD * (i + 1))
                for kind, q in L3_ORDER:
                    n = S * i + q
                    cols = slice(q * P, (q + 1) * P)
                    if kind == "z":
                        if q >= 2:
                            pe.wait_ge(s["z_lo"], n - 1)
                        product(banks[4 + q % 2][0:P, :],
                                [((msgh[:, k, cols], msgl[:, k, cols]), (W3h[:, k, :], W3l[:, k, :])) for k in range(KD)],
                                s["z_up"])
                    else:
                        if q == S - 1 and ahead:
                            group(i + 2, 0)
                        pe.wait_ge(s["z_lo"], n + 1)
                        pe.wait_ge(s["same_made"], S * (i + 1))
                        if q >= 2:
                            pe.wait_ge(s["c_out"], n - 1)
                        nc.tensor.matmul(banks[6 + q % 2][0:P, :], same[:, q, 0:P], zh[:, q % 2, :], start=True, stop=False)
                        nc.tensor.matmul(banks[6 + q % 2][0:P, :], same[:, q, 0:P], zl[:, q % 2, :], start=False,
                                         stop=True).then_inc(s["c_up"], 1)

            pe.wait_ge(s["diag_made"], 3)
            groups(0, peeled=True)
            layer1(0, first=True)
            groups(1, peeled=True)
            layer2(0, first=True)
            layer1(1)
            sums(0)
            groups(2, start=1)
            layer2(1)
            with pe.Fori(2, NE - 1) as i:
                layer1(i)
                sums(i - 1)
                groups(i + 1, start=1)
                layer2(i)
            layer1(NE - 1)
            sums(NE - 2, ahead=False)
            layer2(NE - 1)
            sums(NE - 1, ahead=False)
            pe.drain().then_inc(s["edges_over"], 1)
            pe.wait_ge(s["edges_over"], 5)

            def turn_tile(bank, of, done):
                for k in range(KD):
                    turn(banks[bank][:, k * 128:k * 128 + P], of[:, k * 128:(k + 1) * 128], s[done] if k == KD - 1 else None)

            def update1(w):
                product(banks[w % 2][0:P, :],
                        [((xTh[:, w, k, 0:P], xTl[:, w, k, 0:P]), (W3ah[:, k, :], W3al[:, k, :])) for k in range(KD)],
                        s["u_up"])

            def update2(w):
                product(banks[2 + w % 2][0:P, :],
                        [((uTh[:, w, k, 0:P], uTl[:, w, k, 0:P]), (W4h[:, k, :], W4l[:, k, :])) for k in range(KD)],
                        s["y_up"])

            for q in range(S):
                pe.wait_ge(s["xn_done"], q + 1)
                if q:
                    pe.wait_ge(s["xt_lo"], q)
                turn_tile(4, xn[:, q, :], "xt_up")
            pe.wait_ge(s["n_lo"], 2)
            for q in range(S + 1):
                if q < S:
                    pe.wait_ge(s["xt_lo"], q + 1)
                    if q >= 2:
                        pe.wait_ge(s["z_done"], q - 1)
                    update1(q)
                if q >= 1:
                    pe.wait_ge(s["u_done"], q)
                    if q >= 2:
                        pe.wait_ge(s["ut_lo"], q - 1)
                    turn_tile(5, u[:, (q - 1) % 2, :], "ut_up")
            for q in range(S):
                pe.wait_ge(s["ut_lo"], q + 1)
                if q >= 2:
                    pe.wait_ge(s["y_added"], q - 1)
                update2(q)
            pe.drain().then_inc(s["first_over"], 1)
            pe.wait_ge(s["first_over"], 5)

            pe.wait_ge(s["o_loaded"], 16 * O_LOADS)
            pe.wait_ge(s["o_set"], O_SET)
            for k in range(KD):
                op = nc.tensor.matmul(banks[0][:, 0:128], fW3[:, k, :], fW1T[:, k, :], start=(k == 0), stop=(k == KD - 1))
            op.then_inc(s["o_mat_up"], 1)
            for k in range(KD):
                op = nc.tensor.matmul(banks[1][:, 0:1], fW1T[:, k, :], fb3[:, k:k + 1], start=(k == 0), stop=(k == KD - 1))
            op.then_inc(s["o_slope_up"], 1)
            pe.wait_ge(s["y0_made"], 1)
            for k in range(KD):
                op = nc.tensor.matmul(banks[2][:, k:k + 1], y0[:, k * 128:(k + 1) * 128], one_col[0:1, :], start=True, stop=True)
            op.then_inc(s["y0T_up"], 1)
            pe.wait_ge(s["y0T"], 2)
            for k in range(KD):
                op = nc.tensor.matmul(banks[3][:, 0:1], fW1T[:, k, :], y0b3[:, k, 0:1], start=(k == 0), stop=(k == KD - 1))
            op.then_inc(s["a_up"], 1)
            for k in range(KD):
                op = nc.tensor.matmul(banks[4][H:KV, 0:H], y0b3[:, k, :], fW1T[:, k, 0:H], start=(k == 0), stop=(k == KD - 1))
            op.then_inc(s["a_up"], 1)
            pe.wait_ge(s["o_mats"], 4)
            pe.wait_ge(s["o_slope"], 3)
            with pe.Fori(0, PICARD) as it:
                wait_apart(pe, s["V_made"], it + 1)
                nc.tensor.matmul(banks[0][0:H, 0:NQ], V[0:KV, :], rule[:, :], start=True, stop=True).then_inc(s["q_a"], 1)
                wait_apart(pe, s["q_g"], it + 1)
                nc.tensor.matmul(banks[1][0:H, 0:NQ], fW2[0:H, 0:H], gq[:, :], start=True, stop=True).then_inc(s["q_w"], 1)
                wait_apart(pe, s["q_h"], it + 1)
                nc.tensor.matmul(banks[2][0:NQ, 0:H], hq[:, :], M_T[:, :], start=True, stop=True).then_inc(s["q_v"], 1)
            pe.wait_ge(s["V_made"], PICARD + 1)
            for c in range(NC):
                if c >= 4:
                    pe.wait_ge(s["ag_out"], c - 3)
                for g in range(G):
                    at = g * T + c * C
                    op = nc.tensor.matmul(banks[c % 4][H * g:H * (g + 1), 0:C], V[0:KV, :], ruleT[:, at:at + C],
                                          start=True, stop=True)
                op.then_inc(s["ag_up"], 1)
            pe.wait_ge(s["ag_out"], NC)
            for n in range(len(STAGES) + STAGE_LAG):
                if NC <= n < len(STAGES):
                    st, c = STAGES[n]
                    pe.wait_ge(s["st_h"], n - NC + 1)
                    if n >= NC + 4:
                        pe.wait_ge(s["st_zs"], n - NC - 3)
                    nc.tensor.matmul(banks[n % 4][:, 0:C], (M_full if st == 3 else M_half)[:, :], hst[:, c, :],
                                     start=True, stop=True).then_inc(s["st_z"], 1)
                if n >= STAGE_LAG:
                    m = n - STAGE_LAG
                    pe.wait_ge(s["st_g"], m + 1)
                    if m >= 4:
                        pe.wait_ge(s["st_h"], m - 3)
                    nc.tensor.matmul(banks[4 + m % 4][:, 0:C], fW2[:, :], gst[:, m % 4, :], start=True,
                                     stop=True).then_inc(s["st_x"], 1)
            pe.wait_ge(s["scan_done"], NC)
            nc.tensor.matmul(banks[4][:, 0:1], groups_before[:, :], Pex[:, T:T + 1], start=True, stop=True).then_inc(s["of_up"], 1)
            pe.wait_ge(s["of_done"], 1)
            nc.tensor.matmul(banks[5][:, 0:1], M_six[:, :], off[:, :], start=True, stop=True).then_inc(s["bs_up"], 1)
            for c in range(NC):
                if c >= 4:
                    pe.wait_ge(s["an_dev"], c - 3)
                nc.tensor.matmul(banks[c % 4][:, 0:C], M_six[:, :], Pex[:, c * C:(c + 1) * C], start=True, stop=True).then_inc(s["an_up"], 1)
            pe.wait_ge(s["dv_top"], 1)
            nc.tensor.transpose(banks[6][0:1, 0:128], devtop[:, :], ident[:, :]).then_inc(s["dv_row"], 1)
            pe.wait_ge(s["flag_made"], 1)
            checked = pe.value_load(flag[0:1, 0:1], min_val=0, max_val=1)
            with pe.If(checked == 0):
                with pe.Fori(0, N) as t:
                    wait_apart(pe, s["sq_sum"], t + 1)
                    for st in range(4):
                        if st == 0:
                            nc.tensor.matmul(banks[0][0:H, 0:1], M_six[0:H, 0:H], seq_P[:, :], start=True, stop=True).then_inc(s["sq_pre"], 1)
                        else:
                            wait_apart(pe, s["sq_h"], 4 * t + st)
                            nc.tensor.matmul(banks[0][0:H, 0:1], M_six[0:H, 0:H], seq_P[:, :], start=True, stop=False)
                            nc.tensor.matmul(banks[0][0:H, 0:1], (M_full if st == 3 else M_half)[0:H, 0:H],
                                             seq_h[:, st - 1:st], start=False, stop=True).then_inc(s["sq_pre"], 1)
                        wait_apart(pe, s["sq_g"], 4 * t + st + 1)
                        nc.tensor.matmul(banks[1][0:H, 0:1], fW2[0:H, 0:H], seq_g[:, :], start=True, stop=True).then_inc(s["sq_x"], 1)
            pe.drain().then_inc(s["scan_over"], 1)
            pe.wait_ge(s["scan_over"], 5)

            pe.wait_ge(s["y0_row"], 16)

            def nodes(j, b):
                for q in range(S):
                    n = S * j + q
                    if has(j, q, -9, 0):
                        m = n - 9
                        c, w = slot(b, q, -9)
                        if w == 0:
                            wait_apart(pe, s[("p_in", "p_in1")[c]], loads_by_parity(j - 2, c))
                        if has(j, q, -11, 0):
                            wait_apart(pe, s["o_added"], m - 1)
                        lhs = steps_lhs[:, c, :].rearrange("k (p s) -> k s p", s=S)[:, w, :]
                        nc.tensor.matmul(banks[6 + w % 2][0:P, :], lhs, steps_rhs[:, :], start=True, stop=True).then_inc(s["o_up"], 1)
                    if has(j, q, 0):
                        pe.wait_ge(s["xt_lo"], n + 1)
                        pe.wait_ge(s["z_done"], n - 1)
                        update1(q)
                    if has(j, q, -4):
                        pe.wait_ge(s["ut_lo"], n - 3)
                        pe.wait_ge(s["y_added"], n - 5)
                        update2(q)
                    if has(j, q, 3):
                        pe.wait_ge(s["xn_done"], n + 4)
                        pe.wait_ge(s["xt_lo"], n + 3)
                        turn_tile(4, xn[:, (q + 3) % S, :], "xt_up")
                    if has(j, q, -1):
                        pe.wait_ge(s["u_done"], n)
                        pe.wait_ge(s["ut_lo"], n - 1)
                        turn_tile(5, u[:, (q - 1) % 2, :], "ut_up")

            run_nodes(pe, nodes)


NODES = 16


def rules(n_times):
    import numpy as np

    k = np.arange(NODES)
    at = 0.5 * (1 - np.cos((2 * k + 1) * np.pi / (2 * NODES)))
    cheb = np.polynomial.chebyshev
    unit = np.eye(NODES)
    inverse = np.linalg.inv(np.stack([cheb.chebval(2 * at - 1, unit[j]) for j in range(NODES)]))

    def table(t):
        whole = [cheb.chebint(unit[j]) * 0.5 for j in range(NODES)]
        to_t = np.stack([cheb.chebval(2 * t - 1, w) - cheb.chebval(-1, w) for w in whole])
        out = np.zeros((34, t.size))
        out[0:NODES] = inverse @ to_t
        out[32] = 1.0
        out[33] = t
        return out.astype(np.float32)

    return table(at), table(np.arange(n_times) / (n_times - 1))


_NAMES = ["x", "src_cols", "dst", "dst_cols", "edge_attr_64"] + [
    "L0_gnn_" + n for n in ("W1", "b1", "W2", "b2", "W3", "b3", "W4", "b4", "gamma", "beta")]


def kernel(**inputs):
    import numpy as _np
    import concourse.bacc as _bacc
    from concourse import mybir as _mybir
    from concourse.bass_utils import run_bass_kernel_spmd as _run

    nc = _bacc.Bacc("TRN2", target_bir_lowering=False, num_devices=1)
    f = {n: _np.asarray(inputs["L0_ffn_" + n]) for n in ("W1", "b1", "W2", "b2", "W3", "b3")}
    n_rows, d = inputs["x"].shape
    node_rule, time_rule = rules(n_rows)
    for side in ("src", "dst"):
        inputs[side + "_cols"] = _np.asarray(inputs[side]).reshape(-1, 125).T
    given = [(n, inputs[n]) for n in _NAMES] + [
        ("F_W1T", f["W1"].T), ("F_b1", f["b1"]), ("F_W2T", f["W2"].T), ("F_b2", f["b2"]),
        ("F_W3", f["W3"]), ("F_W3T", f["W3"].T), ("F_b3", f["b3"]), ("node_rule", node_rule), ("time_rule", time_rule)]
    arrays, args = {}, []
    for name, a in given:
        a = _np.ascontiguousarray(a)
        arrays[f"in_{name}_dram"] = a
        args.append(nc.dram_tensor(f"in_{name}_dram", a.shape, _mybir.dt.from_np(a.dtype), kind="ExternalInput").ap())
    f32 = _mybir.dt.float32
    args.append(nc.dram_tensor("out_0_dram", (n_rows, d), f32, kind="ExternalOutput").ap())
    args.append(nc.dram_tensor("message_sums", (10240, d), f32).ap())
    args.append(nc.dram_tensor("sums_by_time", (f["b1"].shape[0], n_rows), f32).ap())
    gnn_ffn_kernel(nc, *args)
    r = _run(nc, [arrays], core_ids=[0])
    return r.results[0]["out_0_dram"]
```

```python
import concourse.bass as bass
from concourse import mybir
from contextlib import ExitStack


def gnn_ffn_kernel(
    nc: bass.Bass,
    x: bass.AP,
    src_cols: bass.AP,
    dst: bass.AP,
    dst_cols: bass.AP,
    edge_attr: bass.AP,
    W1: bass.AP,
    b1: bass.AP,
    W2: bass.AP,
    b2: bass.AP,
    W3: bass.AP,
    b3: bass.AP,
    W4: bass.AP,
    b4: bass.AP,
    gamma: bass.AP,
    beta: bass.AP,
    F_W1T: bass.AP,
    F_b1: bass.AP,
    F_W2T: bass.AP,
    F_b2: bass.AP,
    F_W3: bass.AP,
    F_W3T: bass.AP,
    F_b3: bass.AP,
    node_rule: bass.AP,
    time_rule: bass.AP,
    time_parts: bass.AP,
    out: bass.AP,
    message_sums: bass.AP,
    sums_by_time: bass.AP,
):
    f32 = mybir.dt.float32
    f32r = mybir.dt.float32r
    i32 = mybir.dt.int32
    ALU = mybir.AluOpType
    ACT = mybir.ActivationFunctionType
    AX = mybir.AxisListType

    N, D = x.shape
    E = dst.shape[0]
    DE = edge_attr.shape[1]
    H = F_b1.shape[0]
    P = 125
    S = 4
    R = P * S
    KD = D // 128
    KF = 2 * KD + 1
    NE = E // R
    NN = N // R
    NT = 2 * S + 1
    EPS = 1e-5
    EXP_MAX = 4.0e8
    SPLIT = 112

    DT = 1.0 / (N - 1)
    G = 4
    T = N // G
    C = 500
    NC = T // C
    NQ = node_rule.shape[1]
    PICARD = 9
    KV = node_rule.shape[0]
    TOL = 2e-5

    ctx = ExitStack()
    with ctx:
        def sem(name):
            return ctx.enter_context(nc.semaphore(name))

        def psum(name, n=1):
            return ctx.enter_context(nc.psum_tensor(name, [128, n * 512], f32))

        def sb_in(scope):
            return lambda name, shape, dt=f32: scope.enter_context(nc.sbuf_tensor(name, shape, dt))

        banks = [psum(f"bank{i}") for i in range(8)]

        sb = sb_in(ctx)
        ident = sb("ident", [128, 128])
        eps_col = sb("eps_col", [128, 1])
        one_col = sb("one_col", [128, 1])
        two_col = sb("two_col", [128, 1])
        gamma_bc = sb("gamma_bc", [P, D])
        beta_bc = sb("beta_bc", [P, D])
        b4_bc = sb("b4_bc", [P, D])
        b3_bc = sb("b3_bc", [128, D])
        b1_col = sb("b1_col", [128, KD])
        b2_col = sb("b2_col", [128, KD])
        src_all = sb("src_all", [P, NE * S], i32)
        dst_all = sb("dst_all", [P, NE * S], i32)
        dst_allf = sb("dst_allf", [P, NE * S])
        steps_rhs = sb("steps_rhs", [3 * H + 5, D], f32r)

        edge_scope = ExitStack()
        sb = sb_in(edge_scope)
        W1h = sb("W1h", [128, KF, D], f32r)
        W1l = sb("W1l", [128, KF, D], f32r)
        W2h = sb("W2h", [128, KD, D], f32r)
        W2l = sb("W2l", [128, KD, D], f32r)
        W3h = sb("W3h", [128, KD, D], f32r)
        W3l = sb("W3l", [128, KD, D], f32r)
        rows = sb("rows", [P, 2 * S, D])
        attr = sb("attr", [P, S, DE])
        fTh = sb("fTh", [128, KF, R], f32r)
        fTl = sb("fTl", [128, KF, R], f32r)
        h1h = sb("h1h", [128, KD, R], f32r)
        h1l = sb("h1l", [128, KD, R], f32r)
        msgh = sb("msgh", [128, KD, R], f32r)
        msgl = sb("msgl", [128, KD, R], f32r)
        tmp = sb("tmp", [128, 8, 512])
        zh = sb("zh", [P, 2, D], f32r)
        zl = sb("zl", [P, 2, D], f32r)
        zsum = sb("zsum", [P, S, D])
        e_stats = sb("e_stats", [P, 2 * S, 6])
        e_mv = sb("e_mv", [P, 2 * S, 2])
        e_lnv = sb("e_lnv", [P, 2 * S])
        e_rstd = sb("e_rstd", [P, 2 * S])
        e_var = sb("e_var", [P, 2 * S])
        e_sq = sb("e_sq", [P, 2 * S])
        e_shift = sb("e_shift", [P, 2 * S])
        src_cur = sb("src_cur", [P, S], i32)
        dst_cur = sb("dst_cur", [P, S], i32)
        drow_i = sb("drow_i", [P, R], i32)
        drow_f = sb("drow_f", [P, R])
        dcol_f = sb("dcol_f", [P, S])
        same = sb("same", [P, S, 126], f32r)
        earlier = sb("earlier", [P, P])
        same_earlier = sb("same_earlier", [P, S, P])
        n_earlier = sb("n_earlier", [P, S])
        spare_i = sb("spare_i", [P, 1], i32)
        spare_row = sb("spare_row", [P, 1])
        to_spare = sb("to_spare", [P, S])
        sum_row = sb("sum_row", [P, S])
        sum_row_i = sb("sum_row_i", [P, S], i32)
        edge_scope.close()

        node_scope = ExitStack()
        sb = sb_in(node_scope)
        W3ah = sb("W3ah", [128, KD, D], f32r)
        W3al = sb("W3al", [128, KD, D], f32r)
        W4h = sb("W4h", [128, KD, D], f32r)
        W4l = sb("W4l", [128, KD, D], f32r)
        steps_in = sb("steps_in", [3 * H + 5, D])
        steps_lhs = sb("steps_lhs", [3 * H + 5, 2, S, P + 1], f32r)
        keep_top = ExitStack()
        sb = sb_in(keep_top)
        xraw = sb("xraw", [P, 2, S, D])
        xn = sb("xn", [P, S, D])
        agg = sb("agg", [P, S, D])
        xTh = sb("xTh", [128, S, KD, P + 1], f32r)
        xTl = sb("xTl", [128, S, KD, P + 1], f32r)
        nz = sb("nz", [P, 2, D])
        ne = sb("ne", [P, 2, D])
        nt = sb("nt", [P, 2, D])
        nr = sb("nr", [P, 2, D])
        u = sb("u", [P, 2, D])
        uTh = sb("uTh", [128, S, KD, P + 1], f32r)
        uTl = sb("uTl", [128, S, KD, P + 1], f32r)
        xnb = sb("xnb", [P, 2, S, D])
        yb = sb("yb", [P, 2, S, D])
        ob = sb("ob", [P, 2, S, D])
        stats = sb("stats", [P, 2 * S, 6])
        mv = sb("mv", [P, 2 * S, 2])
        lnv = sb("lnv", [P, 2 * S])
        rstd = sb("rstd", [P, 2 * S])
        var_eps = sb("var_eps", [P, 2 * S])
        sq = sb("sq", [P, 2 * S])
        shift = sb("shift", [P, 2 * S])
        keep_top.close()

        ode_scope = ExitStack()
        sb = sb_in(ode_scope)
        ruleT = sb("ruleT", [KV, N])
        node_staging = sb("node_staging", [128, 2, KD, D])
        row_x = sb("row_x", [1, D])
        row_norm = sb("row_norm", [1, D])
        row_norm_b4 = sb("row_norm_b4", [1, D])
        row_x_beta = sb("row_x_beta", [1, D])
        row_agg = sb("row_agg", [1, D])
        row_y = sb("row_y", [1, D])
        row_st = sb("row_st", [1, 2, 6])
        row_mv = sb("row_mv", [1, 2, 2])
        row_s = sb("row_s", [1, 2, 4])
        row_cols = sb("row_cols", [128, 7, KD])
        rule = sb("rule", [KV, NQ])
        fW1T = sb("fW1T", [128, KD, 128])
        fW3 = sb("fW3", [128, KD, 128])
        fb3 = sb("fb3", [128, KD])
        fb1 = sb("fb1", [128, 1])
        fb2 = sb("fb2", [128, 1])
        fW2 = sb("fW2", [128, 128])
        blocks = sb("blocks", [128, 128])
        groups_before = sb("groups_before", [128, 128])
        M_T = sb("M_T", [H, H])
        M_half = sb("M_half", [128, 128])
        M_full = sb("M_full", [128, 128])
        M_six = sb("M_six", [128, 128])
        slope = sb("slope", [128, 1])
        bias_half = sb("bias_half", [128, 1])
        bias_full = sb("bias_full", [128, 1])
        y0 = sb("y0", [1, D])
        y0_x1 = sb("y0_x1", [1, D])
        y0_beta = sb("y0_beta", [1, D])
        y0_st = sb("y0_st", [1, 6])
        y0_mv = sb("y0_mv", [1, 2])
        y0_s = sb("y0_s", [1, 4])
        y0b3 = sb("y0b3", [128, KD, 2])
        a0 = sb("a0", [128, 1])
        V = sb("V", [64, H])
        gq = sb("gq", [H, NQ])
        hq = sb("hq", [H, NQ])
        A_guess = sb("A_guess", [128, T])
        A_rest = sb("A_rest", [128, T])
        times = sb("times", [128, T])
        zst = sb("zst", [128, 2, C])
        gst = sb("gst", [128, 4, C])
        hst = sb("hst", [128, NC + 1, C])
        Ssum = sb("Ssum", [128, NC, C])
        zeros = sb("zeros", [128, C])
        Pex = sb("Pex", [128, T + 1])
        off = sb("off", [128, 1])
        base = sb("base", [128, 1])
        dev = gst[:, 0:2, :]
        devmax = sb("devmax", [128, NC])
        devtop = sb("devtop", [128, 1])
        devrow = sb("devrow", [1, 1])
        flag = sb("flag", [1, 1], i32)
        seq_a = sb("seq_a", [H, 1])
        seq_bias = sb("seq_bias", [H, 3])
        seq_g = sb("seq_g", [H, 1])
        seq_h = sb("seq_h", [H, 4])
        seq_P = sb("seq_P", [H, 1])
        seq_S = sb("seq_S", [H, 3])
        seq_blk, seq_t = dev[0:H, 0, :], dev[0:H, 1, :]
        ode_scope.close()
        node_scope.close()

        s = {}
        for name in (
            "consts_set diag_made spare_made idx_in smalls_in dstf_made table_filled staged split_hi split_lo "
            "staged1 idx_copied rows_in attr_in stats_done aggr_done ln_guess newton rows_normed rows_normed_dve groups_up "
            "group_hi group_lo layer_up exp_done cut_done t_done log_done r_done w_done m_done hi_done lo_done "
            "z_up z_hi z_lo c_up c_out drow_in seg same_made sumrow_made scattered "
            "n_staged1 n_staged n_hi n_lo x_in x_in1 x_in2 x_in3 agg_in agg_in1 xs_done aggr2 lns_guess lns_newton xn_done xnb_done "
            "xt_up xt_hi xt_lo ut_up ut_hi ut_lo u_up z_done ne_done nc_done nt_done nl_done nr_done nw_done u_done "
            "y_up y_added ys_done yn_done yg_done yx_done o_up o_added ob_in ob_in1 stored "
            "p_in steps_hi steps_lo rhs_hi rhs_lo "
            "o_set o_loaded o_mat_up o_mats o_slope_up o_slope y0_stat y0_guess y0_newton y0_made y0T_up y0T "
            "y0_row a_up a_made V_made q_a q_g q_w q_h q_v ag_up ag_out ab_made st_z st_zs st_g st_x st_h st_acc "
            "scan_done of_up of_done bs_done an_up an_dev an_max dv_row dv_rowed dv_top flag_made "
            "pg_made sums_out sq_in sq_set sq_bias sq_pre sq_g sq_x sq_h sq_sum sq_blk sq_stored "
            "o_consts_in row_in row_agg_in row_steps row_sides row_newton edges_over scan_over"
        ).split():
            s[name] = sem(name)

        x_rows = x.rearrange("(j p s) d -> j p s d", p=P, s=S)
        out_rows = out.rearrange("(j p s) d -> j p s d", p=P, s=S)
        agg_rows = message_sums[0:N, :].rearrange("(j p s) d -> j p s d", p=P, s=S)
        attr_rows = edge_attr.rearrange("(i s p) d -> i p s d", s=S, p=P)
        dst_rows = dst.rearrange("(i r) -> i r", r=R)
        W1v = W1[0:2 * D, :].rearrange("(k p) n -> p k n", p=128)
        W2v = W2.rearrange("(k p) n -> p k n", p=128)
        W3av = W3[0:D, :].rearrange("(k p) n -> p k n", p=128)
        W3bv = W3[D:2 * D, :].rearrange("(k p) n -> p k n", p=128)
        W4v = W4.rearrange("(k p) n -> p k n", p=128)
        EW = 5
        staging = [tmp[:, 0:4, :], tmp[:, 4:8, :]]
        edge_pieces = [
            (W1v[:, 0:KD, :], W1h[:, 0:KD, :], W1l[:, 0:KD, :], 128),
            (W1v[:, KD:2 * KD, :], W1h[:, KD:2 * KD, :], W1l[:, KD:2 * KD, :], 128),
            (W1[2 * D:2 * D + DE, :], W1h[0:DE, 2 * KD, :], W1l[0:DE, 2 * KD, :], DE),
            (W2v, W2h[:, :, :], W2l[:, :, :], 128),
            (W3bv, W3h[:, :, :], W3l[:, :, :], 128),
        ]
        node_pieces = [(W3av, W3ah[:, :, :], W3al[:, :, :]), (W4v, W4h[:, :, :], W4l[:, :, :])]

        def piece_in(n):
            st = staging[n % 2]
            return st[0:DE, 0, :] if edge_pieces[n][3] == DE else st

        SMALLS = 6
        STAGED = ("staged", "staged1")
        FILLS = 20
        FILL_ENDS = (4, 12, FILLS)
        FILL_ROWS = message_sums.shape[0] // FILLS
        assert FILL_ROWS == 4 * 128 and FILLS * FILL_ROWS >= N + P
        CHUNKS = [(g, c) for c in range(NC) for g in range(G)]
        STAGES = [(st, c) for st in range(4) for c in range(NC)]

        L3_ORDER = [("z", 0), ("z", 1), ("c", 0), ("z", 2), ("c", 1), ("z", 3), ("c", 2), ("c", 3)]
        O_CONSTS = 2 + 4 * G
        O_LOADS = 2 + 4 + 2 * G

        def b3_parts(n):
            return hst[0:1, :, :].rearrange("a c t -> a (c t)")[:, n * D:(n + 1) * D]
        O_SET = 6 + G + G * (G - 1) // 2
        STAGE_LAG = 2
        SUM_LAG = 3

        def group_of(g):
            bank = banks[4 + g % 4]
            if g == 2 * S:
                return bank[0:DE, 0:R]
            return bank[:, :].rearrange("p (k c) -> p k c", k=KD)[:, :, 0:P]

        def group_to(g, to):
            if g == 2 * S:
                return to[0:DE, 2 * KD, :]
            side, q = g // S, g % S
            return to[:, side * KD:(side + 1) * KD, q * P:(q + 1) * P]

        def turned_of(bank):
            return banks[bank][:, :].rearrange("p (k c) -> p k c", k=KD)[:, :, 0:P]

        def wait_apart(eng, semaphore, value):
            if isinstance(value, int):
                eng.wait_ge(semaphore, value)
            else:
                held = eng.to_reg(value)
                eng.wait_ge(s["consts_set"], 5)
                eng.wait_ge(semaphore, held)

        def has(j, q, lag):
            return not isinstance(j, int) or 0 <= S * j + q + lag < S * NN

        def slot(b, q, lag):
            return (b + (q + lag) // S) % 2, (q + lag) % S

        def norms(j):
            at_x, at_y = has(j, 0, S), has(j, 0, -2 * S)
            return slice(0 if at_x else S, 2 * S if at_y else S) if at_x or at_y else None

        def aggregated(j):
            if not isinstance(j, int):
                return 3 * S + 2 * S * (j - 1)
            spans = [norms(i) for i in range(-2, j + 1)]
            return sum(at.stop - at.start for at in spans if at)

        X_IN = (("x_in", "x_in1"), ("x_in2", "x_in3"))
        AGG_IN = ("agg_in", "agg_in1")

        def loads_by_parity(j, parity):
            return 16 * (j - parity) + 32

        LOOP = (4, NN - 4)

        def run_nodes(eng, nodes):
            for j in range(-2, LOOP[0]):
                nodes(j, j % 2)
            with eng.Fori(LOOP[0], LOOP[1], 2) as j:
                nodes(j, 0)
                nodes(j + 1, 1)
            for j in range(LOOP[1], NN + 3):
                nodes(j, j % 2)

        block = ctx.enter_context(nc.Block())

        @block.sync
        def _(sp):
            def row(v):
                return v.rearrange("(a n) -> a n", a=1)

            sp.dma_start(src_all[:, :], src_cols).then_inc(s["idx_in"], 16)
            sp.dma_start(dst_all[:, :], dst_cols).then_inc(s["idx_in"], 16)
            for to, of in (
                (b3_bc[:, :], row(b3).to_broadcast([128, D])),
                (b1_col[:, :], b1.rearrange("(k p) -> p k", p=128)),
                (b2_col[:, :], b2.rearrange("(k p) -> p k", p=128)),
                (gamma_bc[:, :], row(gamma).to_broadcast([P, D])),
                (beta_bc[:, :], row(beta).to_broadcast([P, D])),
                (b4_bc[:, :], row(b4).to_broadcast([P, D])),
            ):
                sp.dma_start(to, of, allow_slow_non_contiguous=True).then_inc(s["smalls_in"], 16)
            for n in range(EW):
                if n >= 2:
                    sp.wait_ge(s["split_lo"], n - 1)
                sp.dma_start(piece_in(n), edge_pieces[n][0]).then_inc(s[STAGED[n % 2]], 16)
                if n == 1:
                    sp.dma_start(attr[:, :, :], attr_rows[0]).then_inc(s["attr_in"], 16)

            def fill(first, last):
                with sp.Fori(first, last) as f:
                    sp.dma_start(
                        message_sums[bass.ds(f * FILL_ROWS, FILL_ROWS), :].rearrange("(p s) d -> p s d", p=128),
                        b3_bc[:, :].unsqueeze(1).to_broadcast([128, S, D]),
                    ).then_inc(s["table_filled"], 16)

            sp.wait_ge(s["smalls_in"], 16 * SMALLS)
            fill(0, FILL_ENDS[0])

            def attr_load(i):
                sp.wait_ge(s["groups_up"], NT * i)
                sp.dma_start(attr[:, :, :], attr_rows[i]).then_inc(s["attr_in"], 16)

            def dst_row_load(i):
                sp.dma_start(drow_i[:, :], dst_rows[bass.ds(i, 1), :].to_broadcast([P, R])).then_inc(s["drow_in"], 16)

            attr_load(1)
            dst_row_load(0)
            sp.wait_ge(s["rows_in"], 16 * 2 * S * 2)
            fill(FILL_ENDS[0], FILL_ENDS[1])
            attr_load(2)
            sp.wait_ge(s["rows_in"], 16 * 2 * S * 3)
            fill(FILL_ENDS[1], FILL_ENDS[2])
            sp.wait_ge(s["same_made"], S)
            dst_row_load(1)
            with sp.Fori(2, NE - 1) as i:
                attr_load(i + 1)
                sp.wait_ge(s["same_made"], S * i)
                dst_row_load(i)
            sp.wait_ge(s["same_made"], S * (NE - 1))
            dst_row_load(NE - 1)
            sp.wait_ge(s["layer_up"], 2 * KD * (NE - 1) + KD)
            for n in range(2):
                sp.dma_start(node_staging[:, n, :, :], node_pieces[n][0]).then_inc(s[("n_staged", "n_staged1")[n]], 16)
            sp.dma_start(row_x[:, :], x[0:1, :]).then_inc(s["row_in"], 16)
            for to, of in (
                [(fb3[:, :], F_b3.rearrange("(k p) -> p k", p=128)), (rule[:, :], node_rule)]
                + [(fW1T[:, :, H * g:H * (g + 1)], F_W1T.rearrange("(k p) h -> p k h", p=128)) for g in range(G)]
                + [(fW3[:, :, H * g:H * (g + 1)], F_W3.rearrange("(k p) h -> p k h", p=128)) for g in range(G)]
                + [(fb1[H * g:H * (g + 1), :], F_b1.rearrange("(h a) -> h a", a=1)) for g in range(G)]
                + [(fb2[H * g:H * (g + 1), :], F_b2.rearrange("(h a) -> h a", a=1)) for g in range(G)]
            ):
                sp.dma_start(to, of, allow_slow_non_contiguous=True).then_inc(s["o_consts_in"], 16)
            sp.drain().then_inc(s["edges_over"], 1)
            sp.wait_ge(s["edges_over"], 5)

            sp.dma_start(row_agg[:, :], message_sums[0:1, :]).then_inc(s["row_agg_in"], 16)
            sp.dma_start(ruleT[0:H, :], time_rule[0:H, :]).then_inc(s["o_loaded"], 16)
            sp.dma_start(ruleT[H:KV, :], time_rule[H:KV, :]).then_inc(s["o_loaded"], 16)
            for part in range(3):
                sp.dma_start(steps_in[H * part:H * (part + 1), :], F_W3T).then_inc(s["o_loaded"], 16)
            sp.dma_start(b3_parts(0), row(F_b3)).then_inc(s["o_loaded"], 16)
            sp.wait_ge(s["o_set"], 6)
            for g in range(G):
                sp.dma_start(fW2[H * g:H * (g + 1), H * g:H * (g + 1)], F_W2T).then_inc(s["o_loaded"], 16)
            for g in range(G):
                sp.dma_start(times[H * g:H * (g + 1), :], time_rule[KV - 1:KV, g * T:(g + 1) * T].to_broadcast([H, T])
                             ).then_inc(s["o_loaded"], 16)

            def x_load(j, b, h):
                w = slice(2 * h, 2 * h + 2)
                sp.dma_start(xraw[0:SPLIT, b, w], x_rows[j, 0:SPLIT, w]).then_inc(s[X_IN[b][h]], 16)
                sp.dma_start(xraw[SPLIT:P, b, w], x_rows[j, SPLIT:P, w]).then_inc(s[X_IN[b][h]], 16)

            def agg_load(j, h):
                w = slice(2 * h, 2 * h + 2)
                sp.dma_start(agg[0:SPLIT, w], agg_rows[j, 0:SPLIT, w]).then_inc(s[AGG_IN[h]], 16)
                sp.dma_start(agg[SPLIT:P, w], agg_rows[j, SPLIT:P, w]).then_inc(s[AGG_IN[h]], 16)

            def steps_load(j):
                for part in range(3):
                    sp.dma_start(steps_in[H * part:H * (part + 1), 0:R], sums_by_time[:, bass.ds(j * R, R)]).then_inc(s["p_in"], 16)
                sp.dma_start(steps_in[3 * H:, 0:R], time_parts[:, bass.ds(j * R, R)]).then_inc(s["p_in"], 16)

            def x_again(j, b):
                done = s[("ob_in", "ob_in1")[b]]
                sp.dma_start(ob[0:SPLIT, b], x_rows[j, 0:SPLIT]).then_inc(done, 16)
                sp.dma_start(ob[SPLIT:P, b], x_rows[j, SPLIT:P]).then_inc(done, 16)

            def store(j, b):
                sp.dma_start(out_rows[j, 0:SPLIT], ob[0:SPLIT, b]).then_inc(s["stored"], 16)
                sp.dma_start(out_rows[j, SPLIT:P], ob[SPLIT:P, b]).then_inc(s["stored"], 16)

            sp.wait_ge(s["rhs_hi"], 3)
            sp.wait_ge(s["rhs_lo"], 3)
            for to, of in enumerate((3, 4, 1, 1, 2)):
                sp.dma_start(steps_in[3 * H + to:3 * H + to + 1, :], b3_parts(of)).then_inc(s["y0_row"], 16)
            sp.wait_ge(s["ag_up"], NC)
            for h in range(2):
                x_load(0, 0, h)
                agg_load(0, h)
            for h in range(2):
                x_load(1, 1, h)
            sp.wait_ge(s["pg_made"], 1)
            for g in range(G):
                sp.dma_start(sums_by_time[:, g * T:(g + 1) * T], times[H * g:H * (g + 1), :]).then_inc(s["sums_out"], 16)
            sp.wait_ge(s["sums_out"], 16 * G)
            sp.wait_ge(s["flag_made"], 1)
            checked = sp.value_load(flag[0:1, 0:1], min_val=0, max_val=1)
            with sp.If(checked == 0):
                with sp.Fori(0, N // C) as b:
                    sp.dma_start(
                        seq_t[:, :], time_rule[KV - 1:KV, bass.ds(b * C, C)].to_broadcast([H, C])
                    ).then_inc(s["sq_in"], 16)
                    wait_apart(sp, s["sq_sum"], (b + 1) * C + 1)
                    sp.dma_start(sums_by_time[:, bass.ds(b * C, C)], seq_blk[:, :]).then_inc(s["sq_stored"], 16)
                    wait_apart(sp, s["sq_stored"], 16 * (b + 1))
            sp.drain().then_inc(s["scan_over"], 1)
            sp.wait_ge(s["scan_over"], 5)

            def nodes(j, b):
                if has(j, 0, -3 * S):
                    sp.wait_ge(s["o_added"], S * (j - 2))
                    store(j - 3, 1 - b)
                if has(j, 0, -S):
                    if has(j, 0, -2 * S):
                        sp.wait_ge(s["steps_lo"], j - 1)
                    steps_load(j - 1)
                for h in range(2):
                    if has(j, 0, 3 * S) and has(j, 0, S):
                        sp.wait_ge(s["xn_done"], S * (j + 1) + 2 * h + 2)
                        x_load(j + 3, 1 - b, h)
                    if has(j, 0, 0) and has(j, 0, S):
                        sp.wait_ge(s["z_done"], S * j + 2 * h + 2)
                        agg_load(j + 1, h)
                    if h == 0:
                        if has(j, 0, -3 * S):
                            sp.wait_ge(s["stored"], 32 * (j - 2))
                        if has(j, 0, -S):
                            x_again(j - 1, 1 - b)

            run_nodes(sp, nodes)
            sp.wait_ge(s["stored"], 32 * NN)

        @block.gpsimd
        def _(pool):
            nc.gpsimd.memset(ident[:, :], 0.0).then_inc(s["consts_set"], 1)
            nc.gpsimd.memset(earlier[:, :], 1.0).then_inc(s["consts_set"], 1)
            nc.gpsimd.memset(eps_col[:, :], EPS).then_inc(s["consts_set"], 1)
            nc.gpsimd.memset(one_col[:, :], 1.0).then_inc(s["consts_set"], 1)
            nc.gpsimd.memset(two_col[:, :], 2.0).then_inc(s["consts_set"], 1)
            pool.wait_ge(s["consts_set"], 5)
            nc.gpsimd.affine_select(
                out=ident[:, :], in_=ident[:, :], compare_op=ALU.not_equal, fill=1.0,
                base=0, pattern=[[-1, 128]], channel_multiplier=1,
            ).then_inc(s["diag_made"], 1)
            nc.gpsimd.affine_select(
                out=earlier[:, :], in_=earlier[:, :], compare_op=ALU.is_gt, fill=0.0,
                base=0, pattern=[[-1, P]], channel_multiplier=1,
            ).then_inc(s["diag_made"], 1)
            nc.gpsimd.iota(spare_i[:, :], pattern=[[0, 1]], base=N, channel_multiplier=1).then_inc(s["diag_made"], 1)
            pool.wait_ge(s["diag_made"], 3)
            nc.gpsimd.tensor_copy(spare_row[:, :], spare_i[:, :]).then_inc(s["spare_made"], 1)

            def gather(i):
                nc.gpsimd.tensor_copy(src_cur[:, :], src_all[:, bass.ds(i * S, S)]).then_inc(s["idx_copied"], 1)
                nc.gpsimd.tensor_copy(dst_cur[:, :], dst_all[:, bass.ds(i * S, S)]).then_inc(s["idx_copied"], 1)
                wait_apart(pool, s["idx_copied"], 2 * i + 2)
                for side, idx in ((0, src_cur), (1, dst_cur)):
                    for q in range(S):
                        nc.gpsimd.indirect_dma_start(
                            rows[:, side * S + q, :], None, x[:, :],
                            bass.IndirectOffsetOnAxis(ap=idx[:, q:q + 1], axis=0),
                        ).then_inc(s["rows_in"], 16)

            def scatter(i, first=False):
                pool.wait_ge(s["sumrow_made"], i + 1)
                for q in range(S):
                    pool.wait_ge(s["c_out"], S * i + q + 1)
                    if not (first and q == 0):
                        wait_apart(pool, s["scattered"], 16 * (S * i + q))
                    nc.gpsimd.indirect_dma_start(
                        message_sums[:, :], bass.IndirectOffsetOnAxis(ap=sum_row_i[:, q:q + 1], axis=0),
                        zsum[:, q, :], None, compute_op=ALU.add,
                    ).then_inc(s["scattered"], 16)

            pool.wait_ge(s["idx_in"], 32)
            gather(0)
            pool.wait_ge(s["groups_up"], NT)
            gather(1)
            pool.wait_ge(s["groups_up"], 2 * NT)
            gather(2)
            pool.wait_ge(s["table_filled"], 16 * FILLS)
            scatter(0, first=True)
            pool.wait_ge(s["groups_up"], 3 * NT)
            gather(3)
            with pool.Fori(2, NE - 2) as i:
                scatter(i - 1)
                pool.wait_ge(s["groups_up"], NT * (i + 2))
                gather(i + 2)
            for i in range(NE - 2, NE + 1):
                scatter(i - 1)
            pool.wait_ge(s["scattered"], 16 * S * NE)
            pool.drain().then_inc(s["edges_over"], 1)
            pool.wait_ge(s["edges_over"], 5)

            nc.gpsimd.memset(blocks[:, :], 0.0).then_inc(s["o_set"], 1)
            nc.gpsimd.memset(groups_before[:, :], 0.0).then_inc(s["o_set"], 1)
            nc.gpsimd.memset(fW2[:, :], 0.0).then_inc(s["o_set"], 1)
            nc.gpsimd.memset(V[:, :], 0.0).then_inc(s["o_set"], 1)
            nc.gpsimd.memset(zeros[:, :], 0.0).then_inc(s["o_set"], 1)
            nc.gpsimd.memset(Pex[:, 0:1], 0.0).then_inc(s["o_set"], 1)
            pool.wait_ge(s["o_set"], 6)
            for g in range(G):
                nc.gpsimd.memset(blocks[H * g:H * (g + 1), H * g:H * (g + 1)], 1.0).then_inc(s["o_set"], 1)
                for later in range(g + 1, G):
                    nc.gpsimd.tensor_copy(
                        groups_before[H * g:H * (g + 1), H * later:H * (later + 1)],
                        ident[H * g:H * (g + 1), H * g:H * (g + 1)],
                    ).then_inc(s["o_set"], 1)
            pool.drain().then_inc(s["scan_over"], 1)
            pool.wait_ge(s["scan_over"], 5)

            def nodes(j, b):
                for q in range(S):
                    n = S * j + q
                    if has(j, q, -1):
                        k = (q - 1) % 2
                        pool.wait_ge(s["nt_done"], n)
                        if has(j, q, -3):
                            pool.wait_ge(s["ut_up"], n - 2)
                        nc.gpsimd.tensor_tensor(u[:, k, :], nz[:, k, :], nt[:, k, :], ALU.mult).then_inc(s["nw_done"], 1)
                    if has(j, q, -9):
                        m = n - 9
                        c, w = slot(b, q, -9)
                        pool.wait_ge(s["yn_done"], m + 1)
                        nc.gpsimd.tensor_tensor(yb[:, c, w, :], yb[:, c, w, :], gamma_bc[:, :], ALU.mult).then_inc(s["yg_done"], 1)
                        if w == 0:
                            wait_apart(pool, s[("ob_in", "ob_in1")[c]], loads_by_parity(j - 2, c))
                        pool.wait_ge(s["yg_done"], m + 1)
                        nc.gpsimd.tensor_tensor(ob[:, c, w, :], ob[:, c, w, :], yb[:, c, w, :], ALU.add).then_inc(s["yx_done"], 1)
                    if has(j, q, 3):
                        m = n + 3
                        c, w = slot(b, q, 3)
                        pool.wait_ge(s["xn_done"], m + 1)
                        if has(j, q, -5):
                            pool.wait_ge(s["y_added"], m - 7)
                        nc.gpsimd.tensor_tensor(xnb[:, c, w, :], xn[:, w, :], b4_bc[:, :], ALU.add).then_inc(s["xnb_done"], 1)

            run_nodes(pool, nodes)

        @block.scalar
        def _(act):
            def split_high(n, to, of):
                nc.scalar.activation(to, of, ACT.Copy).then_inc(s["split_hi"], 1)

            act.preload_act_table_set("natural_log_exp_and_others")
            act.wait_ge(s["consts_set"], 5)

            def edge_weights(first, last):
                for n in range(first, last):
                    act.wait_ge(s[STAGED[n % 2]], 16 * (n // 2 + 1))
                    split_high(n, edge_pieces[n][1], piece_in(n))

            edge_weights(0, 2)

            def rows_rstd(i):
                act.wait_ge(s["aggr_done"], 2 * S * (i + 1))
                nc.scalar.activation(e_lnv[:, :], e_mv[:, :, 1], ACT.Ln, bias=eps_col[0:P, :]).then_inc(s["ln_guess"], 1)
                act.wait_ge(s["ln_guess"], 2 * i + 1)
                nc.scalar.activation(e_rstd[:, :], e_lnv[:, :], ACT.Exp, scale=-0.5).then_inc(s["ln_guess"], 1)

            def groups(i):
                for g in range(NT):
                    act.wait_ge(s["groups_up"], NT * i + g + 1)
                    nc.scalar.activation(group_to(g, fTh), group_of(g), ACT.Copy).then_inc(s["group_hi"], 1)

            def rows_norm(i, part):
                act.wait_ge(s["newton"], 6 * (i + 1))
                for a in (2 * part, 2 * part + 1):
                    nc.scalar.activation(rows[:, a, :], rows[:, a, :], ACT.Identity, bias=e_shift[:, a:a + 1],
                                         scale=e_rstd[:, a:a + 1]).then_inc(s["rows_normed"], 1)

            def z_high(i, q, first=False):
                act.wait_ge(s["z_up"], S * i + q + 1)
                if not (first and q < 2):
                    act.wait_ge(s["c_up"], S * i + q - 1)
                nc.scalar.activation(zh[:, q % 2, :], banks[4 + q % 2][0:P, :], ACT.Copy).then_inc(s["z_hi"], 1)

            def layer1(i, ahead=True, sums_ahead=True, first=False):
                for m in range(KD):
                    n, k = 2 * KD * i + m, m % 2
                    act.wait_ge(s["layer_up"], n + 1)
                    if not (first and m < 2):
                        act.wait_ge(s["t_done"], n - 1)
                    nc.scalar.activation(tmp[:, k, 0:R], banks[m][:, 0:R], ACT.Exp,
                                         bias=b1_col[:, m:m + 1]).then_inc(s["exp_done"], 1)
                    if ahead and m == KD - 1:
                        rows_rstd(i + 1)
                    act.wait_ge(s["t_done"], n + 1)
                    if not (first and m < 2):
                        act.wait_ge(s["m_done"], n - 1)
                    nc.scalar.activation(tmp[:, 4 + k, 0:R], tmp[:, 2 + k, 0:R], ACT.Ln,
                                         bias=two_col[:, :]).then_inc(s["log_done"], 1)
                    act.wait_ge(s["log_done"], n + 1)
                    nc.scalar.activation(tmp[:, 4 + k, 0:R], tmp[:, 4 + k, 0:R], ACT.Exp,
                                         scale=-1.0).then_inc(s["r_done"], 1)
                    if sums_ahead and m == KD - 1:
                        z_high(i - 1, 0, first=isinstance(i, int) and i == 1)
                    act.wait_ge(s["m_done"], n + 1)
                    nc.scalar.activation(h1h[:, m, :], tmp[:, 6 + k, 0:R], ACT.Copy).then_inc(s["hi_done"], 1)
                if ahead:
                    rows_norm(i + 1, 0)
                if sums_ahead:
                    z_high(i - 1, 1, first=isinstance(i, int) and i == 1)
                if ahead:
                    rows_norm(i + 1, 1)

            def layer2(i):
                n0 = 2 * KD * i + KD
                for step in range(KD + 2):
                    if step < KD:
                        n, k = n0 + step, step % 2
                        act.wait_ge(s["layer_up"], n + 1)
                        act.wait_ge(s["t_done"], n - 1)
                        nc.scalar.activation(tmp[:, k, 0:R], banks[step][:, 0:R], ACT.Exp,
                                             bias=b2_col[:, step:step + 1]).then_inc(s["exp_done"], 1)
                    if 1 <= step <= KD:
                        n, k = n0 + step - 1, (step - 1) % 2
                        act.wait_ge(s["t_done"], n + 1)
                        act.wait_ge(s["m_done"], n - 1)
                        nc.scalar.activation(tmp[:, 4 + k, 0:R], tmp[:, 2 + k, 0:R], ACT.Ln,
                                             bias=two_col[:, :]).then_inc(s["log_done"], 1)
                        act.wait_ge(s["log_done"], n + 1)
                        nc.scalar.activation(tmp[:, 4 + k, 0:R], tmp[:, 4 + k, 0:R], ACT.Exp,
                                             scale=-1.0).then_inc(s["r_done"], 1)
                    if step >= 2:
                        n, k = n0 + step - 2, (step - 2) % 2
                        act.wait_ge(s["m_done"], n + 1)
                        nc.scalar.activation(msgh[:, step - 2, :], tmp[:, 6 + k, 0:R], ACT.Copy).then_inc(s["hi_done"], 1)

            def sums(i, first=False):
                for kind, q in (("z", 2), ("c", 0), ("z", 3), ("c", 1), ("c", 2), ("c", 3)):
                    if kind == "z":
                        z_high(i, q)
                    else:
                        act.wait_ge(s["c_up"], S * i + q + 1)
                        if not first:
                            act.wait_ge(s["scattered"], 16 * S * i)
                        nc.scalar.activation(zsum[:, q, :], banks[6 + q % 2][0:P, :], ACT.Copy).then_inc(s["c_out"], 1)

            rows_rstd(0)
            edge_weights(2, 3)
            rows_norm(0, 0)
            rows_norm(0, 1)
            groups(0)
            edge_weights(3, EW)
            act.wait_ge(s["smalls_in"], 16 * SMALLS)
            act.wait_ge(s["split_lo"], EW)
            layer1(0, sums_ahead=False, first=True)
            groups(1)
            layer2(0)
            layer1(1)
            sums(0, first=True)
            groups(2)
            layer2(1)
            with act.Fori(2, NE - 1) as i:
                layer1(i)
                sums(i - 1)
                groups(i + 1)
                layer2(i)
            layer1(NE - 1, ahead=False)
            sums(NE - 2)
            layer2(NE - 1)
            z_high(NE - 1, 0)
            z_high(NE - 1, 1)
            sums(NE - 1)
            def row_guess(n, at):
                act.wait_ge(s["row_steps"], n)
                nc.scalar.activation(row_s[:, at, 0:1], row_mv[:, at, 1:2], ACT.Ln, bias=eps_col[0:1, :]).then_inc(s["row_steps"], 1)
                act.wait_ge(s["row_steps"], n + 1)
                nc.scalar.activation(row_s[:, at, 1:2], row_s[:, at, 0:1], ACT.Exp, scale=-0.5).then_inc(s["row_steps"], 1)

            row_guess(2, 0)
            for n in range(2):
                act.wait_ge(s[("n_staged", "n_staged1")[n]], 16)
                nc.scalar.activation(node_pieces[n][1], node_staging[:, n, :, :], ACT.Copy).then_inc(s["n_hi"], 1)
            act.drain().then_inc(s["edges_over"], 1)
            act.wait_ge(s["edges_over"], 5)

            act.wait_ge(s["row_steps"], 11)
            nc.scalar.activation(row_cols[:, 3, :], row_cols[:, 2, :], ACT.Exp).then_inc(s["row_steps"], 1)
            act.wait_ge(s["row_steps"], 14)
            nc.scalar.activation(row_cols[:, 5, :], row_cols[:, 4, :], ACT.Ln, bias=two_col[:, :]).then_inc(s["row_steps"], 1)
            act.wait_ge(s["row_steps"], 15)
            nc.scalar.activation(row_cols[:, 5, :], row_cols[:, 5, :], ACT.Exp, scale=-1.0).then_inc(s["row_steps"], 1)
            act.wait_ge(s["o_loaded"], 16 * O_LOADS)
            nc.scalar.activation(steps_rhs[0:3 * H, :], steps_in[0:3 * H, :], ACT.Copy).then_inc(s["rhs_hi"], 1)
            nc.scalar.activation(b3_parts(1).bitcast(f32r), b3_parts(0), ACT.Copy).then_inc(s["rhs_hi"], 1)
            row_guess(21, 1)
            act.wait_ge(s["y0_stat"], 3)
            nc.scalar.activation(y0_s[:, 0:1], y0_mv[:, 1:2], ACT.Ln, bias=eps_col[0:1, :]).then_inc(s["y0_guess"], 1)
            act.wait_ge(s["y0_guess"], 1)
            nc.scalar.activation(y0_s[:, 1:2], y0_s[:, 0:1], ACT.Exp, scale=-0.5).then_inc(s["y0_guess"], 1)
            act.wait_ge(s["o_consts_in"], 16 * O_CONSTS)
            act.preload_act_table_set("exp_and_others")
            act.wait_ge(s["y0_made"], 2)
            nc.scalar.activation(b3_parts(3).bitcast(f32r), y0_beta[:, :], ACT.Copy).then_inc(s["rhs_hi"], 1)
            with act.Fori(0, PICARD) as it:
                act.wait_ge(s["q_a"], it + 1)
                nc.scalar.activation(gq[:, :], banks[0][0:H, 0:NQ], ACT.Tanh, bias=fb1[0:H, :]).then_inc(s["q_g"], 1)
                act.wait_ge(s["q_w"], it + 1)
                nc.scalar.activation(hq[:, :], banks[1][0:H, 0:NQ], ACT.Tanh, bias=fb2[0:H, :]).then_inc(s["q_h"], 1)
            act.wait_ge(s["o_slope"], 3)
            act.wait_ge(s["y0_row"], 16 * 5)
            nc.scalar.activation(steps_rhs[3 * H:, :], steps_in[3 * H:, :], ACT.Copy).then_inc(s["rhs_hi"], 1)
            for n in range(len(STAGES) + STAGE_LAG):
                if n < len(STAGES):
                    st, c = STAGES[n]
                    bias = (fb1, bias_half, bias_half, bias_full)[st]
                    if n >= 4:
                        act.wait_ge(s["st_x"], n - 3)
                    if st == 0:
                        act.wait_ge(s["ag_out"], c + 1)
                        of = A_guess[:, c * C:(c + 1) * C]
                    else:
                        act.wait_ge(s["st_zs"], n - NC + 1)
                        of = zst[:, n % 2, :]
                    nc.scalar.activation(gst[:, n % 4, :], of, ACT.Tanh, bias=bias[:, :]).then_inc(s["st_g"], 1)
                if n >= STAGE_LAG:
                    m = n - STAGE_LAG
                    st, c = STAGES[m]
                    act.wait_ge(s["st_x"], m + 1)
                    if st > 0:
                        act.wait_ge(s["st_acc"], m - NC + 1)
                    nc.scalar.activation(hst[:, c, :], banks[4 + m % 4][:, 0:C], ACT.Tanh, bias=fb2[:, :]).then_inc(s["st_h"], 1)
            act.wait_ge(s["flag_made"], 1)
            checked = act.value_load(flag[0:1, 0:1], min_val=0, max_val=1)
            with act.If(checked == 0):
                with act.Fori(0, N) as t:
                    act.wait_ge(s["sq_bias"], t + 1)
                    for st in range(4):
                        act.wait_ge(s["sq_pre"], 4 * t + st + 1)
                        nc.scalar.activation(seq_g[:, :], banks[0][0:H, 0:1], ACT.Tanh,
                                             bias=seq_bias[:, (0, 1, 1, 2)[st]:(0, 1, 1, 2)[st] + 1]).then_inc(s["sq_g"], 1)
                        act.wait_ge(s["sq_x"], 4 * t + st + 1)
                        nc.scalar.activation(seq_h[:, st:st + 1], banks[1][0:H, 0:1], ACT.Tanh,
                                             bias=fb2[0:H, :]).then_inc(s["sq_h"], 1)
            act.drain().then_inc(s["scan_over"], 1)
            act.wait_ge(s["scan_over"], 5)

            act.preload_act_table_set("natural_log_exp_and_others")

            def norm_guess(at, aggregated, n):
                act.wait_ge(s["aggr2"], aggregated)
                nc.scalar.activation(lnv[:, at], mv[:, at, 1], ACT.Ln, bias=eps_col[0:P, :]).then_inc(s["lns_guess"], 1)
                act.wait_ge(s["lns_guess"], 2 * n - 1)
                nc.scalar.activation(rstd[:, at], lnv[:, at], ACT.Exp, scale=-0.5).then_inc(s["lns_guess"], 1)

            def nodes(j, b):
                for q in range(S):
                    n = S * j + q
                    if has(j, q, 2):
                        act.wait_ge(s["xt_up"], n + 3)
                        nc.scalar.activation(xTh[:, (q + 2) % S, :, 0:P], turned_of(4), ACT.Copy).then_inc(s["xt_hi"], 1)
                    if has(j, q, -2):
                        act.wait_ge(s["ut_up"], n - 1)
                        nc.scalar.activation(uTh[:, (q - 2) % S, :, 0:P], turned_of(5), ACT.Copy).then_inc(s["ut_hi"], 1)
                    if has(j, q, -1):
                        k = (q - 1) % 2
                        act.wait_ge(s["nt_done"], n)
                        if has(j, q, -3):
                            act.wait_ge(s["u_done"], n - 2)
                        nc.scalar.activation(nr[:, k, :], nt[:, k, :], ACT.Ln, bias=two_col[0:P, :]).then_inc(s["nl_done"], 1)
                        act.wait_ge(s["nl_done"], n)
                        nc.scalar.activation(nr[:, k, :], nr[:, k, :], ACT.Exp, scale=-1.0).then_inc(s["nr_done"], 1)
                    if has(j, q, 3):
                        c, w = slot(b, q, 3)
                        if w == 0:
                            act.wait_ge(s["lns_newton"], 6 * (j + 2))
                        if has(j, q, -1):
                            act.wait_ge(s["xt_up"], n)
                            act.wait_ge(s["xnb_done"], n)
                        nc.scalar.activation(xn[:, w, :], xraw[:, c, w, :], ACT.Identity, bias=shift[:, w:w + 1],
                                             scale=rstd[:, w:w + 1]).then_inc(s["xn_done"], 1)
                    if q == 0 and norms(j):
                        norm_guess(norms(j), aggregated(j), j + 2)
                    if has(j, q, 0):
                        act.wait_ge(s["z_done"], n + 1)
                        if has(j, q, -2):
                            act.wait_ge(s["nt_done"], n - 1)
                        nc.scalar.activation(ne[:, q % 2, :], nz[:, q % 2, :], ACT.Exp).then_inc(s["ne_done"], 1)
                    if q == S - 1 and has(j, 0, -S):
                        act.wait_ge(s["p_in"], 64 * j)
                        if has(j, 0, -3 * S):
                            act.wait_ge(s["o_up"], S * (j - 2))
                        nc.scalar.activation(steps_lhs[:, 1 - b, :, 0:P],
                                             steps_in[:, 0:R].rearrange("k (p s) -> k s p", s=S), ACT.Copy).then_inc(s["steps_hi"], 1)
                    if has(j, q, -8):
                        if q == 0:
                            act.wait_ge(s["lns_newton"], 6 * (j + 2))
                        nc.scalar.activation(yb[:, b, q, :], yb[:, b, q, :], ACT.Identity, bias=shift[:, S + q:S + q + 1],
                                             scale=rstd[:, S + q:S + q + 1]).then_inc(s["yn_done"], 1)

            run_nodes(act, nodes)

        @block.vector
        def _(dve):
            dve.wait_ge(s["idx_in"], 32)
            nc.vector.tensor_copy(dst_allf[:, :], dst_all[:, :]).then_inc(s["dstf_made"], 1)

            def edge_weights(first, last):
                for n in range(first, last):
                    _, hi, lo, _ = edge_pieces[n]
                    dve.wait_ge(s["split_hi"], n + 1)
                    nc.vector.tensor_tensor(lo, piece_in(n), hi.bitcast(f32), ALU.subtract).then_inc(s["split_lo"], 1)

            edge_weights(0, 2)
            dve.wait_ge(s["dstf_made"], 1)
            dve.wait_ge(s["spare_made"], 1)

            def refine(small, var, chain, count):
                v, r, sq = small
                nc.vector.tensor_scalar(v, var, EPS, None, ALU.add).then_inc(s[chain], 1)
                nc.vector.tensor_tensor(sq, r, r, ALU.mult).then_inc(s[chain], 1)
                dve.wait_ge(s[chain], count + 2)
                nc.vector.tensor_tensor(sq, sq, v, ALU.mult).then_inc(s[chain], 1)
                dve.wait_ge(s[chain], count + 3)
                nc.vector.tensor_scalar(sq, sq, -0.5, 1.5, ALU.mult, ALU.add).then_inc(s[chain], 1)
                dve.wait_ge(s[chain], count + 4)
                nc.vector.tensor_tensor(r, r, sq, ALU.mult).then_inc(s[chain], 1)
                dve.wait_ge(s[chain], count + 5)

            def rows_stats(i, part):
                if part == 0:
                    dve.wait_ge(s["rows_in"], 16 * 2 * S * (i + 1))
                for a in (2 * part, 2 * part + 1):
                    nc.vector.bn_stats(e_stats[:, a, :], rows[:, a, :]).then_inc(s["stats_done"], 1)

            def rows_aggregate(i):
                wait_apart(dve, s["stats_done"], 2 * S * (i + 1))
                for a in range(2 * S):
                    nc.vector.bn_aggr(e_mv[:, a, :], e_stats[:, a, :]).then_inc(s["aggr_done"], 1)

            def rows_factors(i):
                dve.wait_ge(s["aggr_done"], 2 * S * (i + 1))
                dve.wait_ge(s["ln_guess"], 2 * i + 2)
                refine((e_var[:, :], e_rstd[:, :], e_sq[:, :]), e_mv[:, :, 1], "newton", 6 * i)
                nc.vector.scalar_tensor_tensor(e_shift[:, :], e_mv[:, :, 0], -1.0, e_rstd[:, :], ALU.mult,
                                               ALU.mult).then_inc(s["newton"], 1)

            def rows_norm(i, part):
                for a in (S + 2 * part, S + 2 * part + 1):
                    nc.vector.tensor_scalar(rows[:, a, :], rows[:, a, :], e_mv[:, a, 0:1], e_rstd[:, a:a + 1],
                                            ALU.subtract, ALU.mult).then_inc(s["rows_normed_dve"], 1)

            def groups(i):
                for g in range(NT):
                    dve.wait_ge(s["group_hi"], NT * i + g + 1)
                    nc.vector.tensor_tensor(group_to(g, fTl), group_of(g), group_to(g, fTh).bitcast(f32),
                                            ALU.subtract).then_inc(s["group_lo"], 1)

            def layer1(i, sums_ahead=True, ahead=True, first=False):
                for m in range(KD):
                    n, k = 2 * KD * i + m, m % 2
                    e, t, r, v = (tmp[:, 2 * a + k, 0:R] for a in range(4))
                    dve.wait_ge(s["exp_done"], n + 1)
                    nc.vector.tensor_scalar(e, e, EXP_MAX, None, ALU.min).then_inc(s["cut_done"], 1)
                    dve.wait_ge(s["cut_done"], n + 1)
                    if not (first and m < 2):
                        dve.wait_ge(s["log_done"], n - 1)
                        dve.wait_ge(s["w_done"], n - 1)
                    nc.vector.scalar_tensor_tensor(t, e, 2.0, e, ALU.add, ALU.mult).then_inc(s["t_done"], 1)
                    dve.wait_ge(s["t_done"], n + 1)
                    if not (first and m < 2):
                        dve.wait_ge(s["lo_done"], n - 1)
                    nc.vector.scalar_tensor_tensor(v, banks[m][:, 0:R], b1_col[:, m:m + 1], t, ALU.add,
                                                   ALU.mult).then_inc(s["w_done"], 1)
                    if m == 0 and sums_ahead:
                        shared(i - 1)
                    if ahead and m in (1, 2):
                        rows_stats(i + 1, 2 * m - 2)
                    if ahead and m == 3:
                        rows_factors(i + 1)
                    dve.wait_ge(s["w_done"], n + 1)
                    dve.wait_ge(s["r_done"], n + 1)
                    nc.vector.tensor_tensor(v, v, r, ALU.mult).then_inc(s["m_done"], 1)
                    if ahead and m in (1, 2):
                        rows_stats(i + 1, 2 * m - 1)
                    if sums_ahead and m == 3:
                        z_low(i - 1, 0)
                    dve.wait_ge(s["hi_done"], n + 1)
                    nc.vector.tensor_tensor(h1l[:, m, :], v, h1h[:, m, :].bitcast(f32), ALU.subtract).then_inc(s["lo_done"], 1)
                    if ahead and m == 2:
                        rows_aggregate(i + 1)
                if ahead:
                    rows_norm(i + 1, 0)
                if sums_ahead:
                    z_low(i - 1, 1)
                if ahead:
                    rows_norm(i + 1, 1)

            def layer2(i):
                n0 = 2 * KD * i + KD
                for step in range(KD + 2):
                    if step < KD:
                        n, k = n0 + step, step % 2
                        e, t = tmp[:, k, 0:R], tmp[:, 2 + k, 0:R]
                        dve.wait_ge(s["exp_done"], n + 1)
                        nc.vector.tensor_scalar(e, e, EXP_MAX, None, ALU.min).then_inc(s["cut_done"], 1)
                        dve.wait_ge(s["cut_done"], n + 1)
                        dve.wait_ge(s["log_done"], n - 1)
                        dve.wait_ge(s["w_done"], n - 1)
                        nc.vector.scalar_tensor_tensor(t, e, 2.0, e, ALU.add, ALU.mult).then_inc(s["t_done"], 1)
                    if 1 <= step <= KD:
                        n, k, m = n0 + step - 1, (step - 1) % 2, step - 1
                        t, r, v = tmp[:, 2 + k, 0:R], tmp[:, 4 + k, 0:R], tmp[:, 6 + k, 0:R]
                        dve.wait_ge(s["t_done"], n + 1)
                        dve.wait_ge(s["lo_done"], n - 1)
                        nc.vector.scalar_tensor_tensor(v, banks[m][:, 0:R], b2_col[:, m:m + 1], t, ALU.add,
                                                       ALU.mult).then_inc(s["w_done"], 1)
                        dve.wait_ge(s["w_done"], n + 1)
                        dve.wait_ge(s["r_done"], n + 1)
                        nc.vector.tensor_tensor(v, v, r, ALU.mult).then_inc(s["m_done"], 1)
                    if step >= 2:
                        n, k = n0 + step - 2, (step - 2) % 2
                        dve.wait_ge(s["hi_done"], n + 1)
                        nc.vector.tensor_tensor(msgl[:, step - 2, :], tmp[:, 6 + k, 0:R], msgh[:, step - 2, :].bitcast(f32),
                                                ALU.subtract).then_inc(s["lo_done"], 1)

            def shared(i):
                dve.wait_ge(s["drow_in"], 16 * (i + 1))
                nc.vector.tensor_copy(drow_f[:, :], drow_i[:, :]).then_inc(s["seg"], 1)
                nc.vector.tensor_copy(dcol_f[:, :], dst_allf[:, bass.ds(i * S, S)]).then_inc(s["seg"], 1)
                dve.wait_ge(s["seg"], 7 * i + 2)
                if not (isinstance(i, int) and i == 0):
                    dve.wait_ge(s["c_up"], S * i)
                for q in range(S):
                    nc.vector.tensor_scalar(same[:, q, 0:P], drow_f[:, q * P:(q + 1) * P], dcol_f[:, q:q + 1], None,
                                            ALU.is_equal).then_inc(s["same_made"], 1)

            def sum_rows(i):
                dve.wait_ge(s["same_made"], S * (i + 1))
                nc.vector.tensor_tensor(same_earlier[:, :, :], same[:, :, 0:P].bitcast(f32),
                                        earlier[:, :].unsqueeze(1).to_broadcast([P, S, P]), ALU.mult).then_inc(s["seg"], 1)
                dve.wait_ge(s["seg"], 7 * i + 3)
                nc.vector.tensor_reduce(n_earlier[:, :], same_earlier[:, :, :], AX.X, ALU.add).then_inc(s["seg"], 1)
                nc.vector.tensor_scalar(to_spare[:, :], dcol_f[:, :], -1.0, spare_row[:, :], ALU.mult, ALU.add).then_inc(s["seg"], 1)
                dve.wait_ge(s["seg"], 7 * i + 5)
                nc.vector.tensor_scalar(n_earlier[:, :], n_earlier[:, :], 1.0, None, ALU.min).then_inc(s["seg"], 1)
                dve.wait_ge(s["seg"], 7 * i + 6)
                nc.vector.tensor_tensor(sum_row[:, :], to_spare[:, :], n_earlier[:, :], ALU.mult).then_inc(s["seg"], 1)
                dve.wait_ge(s["seg"], 7 * i + 7)
                if not (isinstance(i, int) and i == 0):
                    dve.wait_ge(s["scattered"], 16 * S * i)
                nc.vector.tensor_tensor(sum_row_i[:, :], sum_row[:, :], dcol_f[:, :], ALU.add).then_inc(s["sumrow_made"], 1)

            def z_low(i, q):
                dve.wait_ge(s["z_hi"], S * i + q + 1)
                nc.vector.tensor_tensor(zl[:, q % 2, :], banks[4 + q % 2][0:P, :], zh[:, q % 2, :].bitcast(f32),
                                        ALU.subtract).then_inc(s["z_lo"], 1)

            def rest_of_sums(i):
                z_low(i, 2)
                sum_rows(i)
                z_low(i, 3)

            for part in range(S):
                rows_stats(0, part)
            rows_aggregate(0)
            edge_weights(2, 3)
            rows_factors(0)
            rows_norm(0, 0)
            rows_norm(0, 1)
            groups(0)
            edge_weights(3, EW)
            layer1(0, sums_ahead=False, first=True)
            groups(1)
            layer2(0)
            layer1(1)
            rest_of_sums(0)
            groups(2)
            layer2(1)
            with dve.Fori(2, NE - 1) as i:
                layer1(i)
                rest_of_sums(i - 1)
                groups(i + 1)
                layer2(i)
            layer1(NE - 1, ahead=False)
            rest_of_sums(NE - 2)
            layer2(NE - 1)
            shared(NE - 1)
            z_low(NE - 1, 0)
            z_low(NE - 1, 1)
            rest_of_sums(NE - 1)
            def row_wait(n):
                dve.wait_ge(s["row_steps"], n)

            dve.wait_ge(s["row_in"], 16)
            nc.vector.bn_stats(row_st[:, 0, :], row_x[:, :]).then_inc(s["row_steps"], 1)
            row_wait(1)
            nc.vector.bn_aggr(row_mv[:, 0, :], row_st[:, 0, :]).then_inc(s["row_steps"], 1)
            row_wait(4)
            refine((row_s[:, 0, 2:3], row_s[:, 0, 1:2], row_s[:, 0, 3:4]), row_mv[:, 0, 1:2], "row_newton", 0)
            nc.vector.tensor_scalar(row_norm[:, :], row_x[:, :], row_mv[:, 0, 0:1], row_s[:, 0, 1:2],
                                    ALU.subtract, ALU.mult).then_inc(s["row_steps"], 1)
            nc.vector.tensor_tensor(row_x_beta[:, :], row_x[:, :], beta_bc[0:1, :], ALU.add).then_inc(s["row_sides"], 1)
            row_wait(5)
            nc.vector.tensor_tensor(row_norm_b4[:, :], row_norm[:, :], b4_bc[0:1, :], ALU.add).then_inc(s["row_sides"], 1)
            row_wait(6)
            nc.vector.tensor_copy(row_cols[:, 0, :], banks[0][:, 0:KD]).then_inc(s["row_steps"], 1)
            def update_weights(n):
                _, hi, lo = node_pieces[n]
                dve.wait_ge(s["n_hi"], n + 1)
                nc.vector.tensor_tensor(lo, node_staging[:, n, :, :], hi.bitcast(f32), ALU.subtract).then_inc(s["n_lo"], 1)

            update_weights(0)
            row_wait(8)
            nc.vector.tensor_copy(row_cols[:, 1, :], banks[1][:, 0:KD]).then_inc(s["row_steps"], 1)
            dve.drain().then_inc(s["edges_over"], 1)
            dve.wait_ge(s["edges_over"], 5)

            row_wait(10)
            nc.vector.tensor_tensor(row_cols[:, 2, :], banks[2][:, 0:KD], row_cols[:, 1, :], ALU.add).then_inc(s["row_steps"], 1)
            row_wait(12)
            nc.vector.tensor_scalar(row_cols[:, 3, :], row_cols[:, 3, :], EXP_MAX, None, ALU.min).then_inc(s["row_steps"], 1)
            row_wait(13)
            nc.vector.scalar_tensor_tensor(row_cols[:, 4, :], row_cols[:, 3, :], 2.0, row_cols[:, 3, :], ALU.add,
                                           ALU.mult).then_inc(s["row_steps"], 1)
            row_wait(14)
            nc.vector.tensor_tensor(row_cols[:, 6, :], row_cols[:, 2, :], row_cols[:, 4, :], ALU.mult).then_inc(s["row_sides"], 1)
            row_wait(16)
            dve.wait_ge(s["row_sides"], 3)
            nc.vector.tensor_tensor(row_cols[:, 6, :], row_cols[:, 6, :], row_cols[:, 5, :], ALU.mult).then_inc(s["row_steps"], 1)
            dve.wait_ge(s["o_consts_in"], 16 * O_CONSTS)
            dve.wait_ge(s["o_set"], O_SET)
            dve.wait_ge(s["o_mat_up"], 1)
            nc.vector.tensor_copy(M_T[:, :], banks[0][0:H, 0:H]).then_inc(s["o_mats"], 1)
            for to, scale in ((M_half, DT / 2), (M_full, DT), (M_six, DT / 6)):
                nc.vector.scalar_tensor_tensor(to[:, :], banks[0][:, 0:128], scale, blocks[:, :], ALU.mult,
                                               ALU.mult).then_inc(s["o_mats"], 1)
            dve.wait_ge(s["o_slope_up"], 1)
            nc.vector.tensor_copy(slope[:, :], banks[1][:, 0:1]).then_inc(s["o_slope"], 1)
            dve.wait_ge(s["o_slope"], 1)
            nc.vector.tensor_scalar(bias_half[:, :], slope[:, :], DT / 2, fb1[:, :], ALU.mult, ALU.add).then_inc(s["o_slope"], 1)
            nc.vector.tensor_scalar(bias_full[:, :], slope[:, :], DT, fb1[:, :], ALU.mult, ALU.add).then_inc(s["o_slope"], 1)
            nc.vector.tensor_copy(y0b3[:, :, 1], fb3[:, :]).then_inc(s["y0T"], 1)
            dve.wait_ge(s["rhs_hi"], 2)
            nc.vector.tensor_tensor(steps_rhs[2 * H:3 * H, :], steps_in[2 * H:3 * H, :],
                                    steps_rhs[2 * H:3 * H, :].bitcast(f32), ALU.subtract).then_inc(s["rhs_lo"], 1)
            nc.vector.tensor_tensor(b3_parts(2).bitcast(f32r), b3_parts(0), b3_parts(1), ALU.subtract).then_inc(s["rhs_lo"], 1)
            update_weights(1)
            row_wait(18)
            nc.vector.tensor_tensor(row_y[:, :], banks[3][0:1, :], row_norm_b4[:, :], ALU.add).then_inc(s["row_steps"], 1)
            row_wait(19)
            nc.vector.bn_stats(row_st[:, 1, :], row_y[:, :]).then_inc(s["row_steps"], 1)
            row_wait(20)
            nc.vector.bn_aggr(row_mv[:, 1, :], row_st[:, 1, :]).then_inc(s["row_steps"], 1)
            row_wait(23)
            refine((row_s[:, 1, 2:3], row_s[:, 1, 1:2], row_s[:, 1, 3:4]), row_mv[:, 1, 1:2], "row_newton", 5)
            nc.vector.tensor_scalar(row_y[:, :], row_y[:, :], row_mv[:, 1, 0:1], row_s[:, 1, 1:2],
                                    ALU.subtract, ALU.mult).then_inc(s["row_steps"], 1)
            row_wait(24)
            nc.vector.tensor_tensor(row_y[:, :], row_y[:, :], gamma_bc[0:1, :], ALU.mult).then_inc(s["row_steps"], 1)
            row_wait(25)
            nc.vector.tensor_tensor(y0_x1[:, :], row_y[:, :], row_x_beta[:, :], ALU.add).then_inc(s["y0_stat"], 1)
            dve.wait_ge(s["y0_stat"], 1)
            nc.vector.bn_stats(y0_st[:, :], y0_x1[:, :]).then_inc(s["y0_stat"], 1)
            dve.wait_ge(s["y0_stat"], 2)
            nc.vector.bn_aggr(y0_mv[:, :], y0_st[:, :]).then_inc(s["y0_stat"], 1)
            dve.wait_ge(s["y0_stat"], 3)
            dve.wait_ge(s["y0_guess"], 2)
            refine((y0_s[:, 2:3], y0_s[:, 1:2], y0_s[:, 3:4]), y0_mv[:, 1:2], "y0_newton", 0)
            nc.vector.tensor_scalar(y0[:, :], y0_x1[:, :], y0_mv[:, 0:1], y0_s[:, 1:2],
                                    ALU.subtract, ALU.mult).then_inc(s["y0_made"], 1)
            dve.wait_ge(s["y0_made"], 1)
            nc.vector.tensor_tensor(y0_beta[:, :], y0[:, :], beta_bc[0:1, :], ALU.add).then_inc(s["y0_made"], 1)
            dve.wait_ge(s["rhs_hi"], 3)
            nc.vector.tensor_tensor(b3_parts(4).bitcast(f32r), y0_beta[:, :], b3_parts(3), ALU.subtract).then_inc(s["rhs_lo"], 1)
            dve.wait_ge(s["y0T_up"], 1)
            nc.vector.tensor_copy(y0b3[:, :, 0], banks[2][:, 0:KD]).then_inc(s["y0T"], 1)
            dve.wait_ge(s["a_up"], 2)
            nc.vector.tensor_copy(a0[:, :], banks[3][:, 0:1]).then_inc(s["a_made"], 1)
            nc.vector.tensor_copy(V[H:KV, :], banks[4][H:KV, 0:H]).then_inc(s["V_made"], 1)
            with dve.Fori(0, PICARD) as it:
                dve.wait_ge(s["q_v"], it + 1)
                nc.vector.tensor_copy(V[0:NQ, :], banks[2][0:NQ, 0:H]).then_inc(s["V_made"], 1)
            for c in range(NC):
                dve.wait_ge(s["ag_up"], c + 1)
                nc.vector.tensor_copy(A_guess[:, c * C:(c + 1) * C], banks[c % 4][:, 0:C]).then_inc(s["ag_out"], 1)
            dve.wait_ge(s["ag_out"], NC)
            nc.vector.scalar_tensor_tensor(A_rest[:, :], times[:, :], slope[:, :], A_guess[:, :], ALU.mult,
                                           ALU.subtract).then_inc(s["ab_made"], 1)
            def running_sum(c):
                dve.wait_ge(s["st_acc"], 3 * NC + c + 1)
                if c:
                    dve.wait_ge(s["scan_done"], c)
                nc.vector.tensor_tensor_scan(Pex[:, 1 + c * C:1 + (c + 1) * C], zeros[:, :], Ssum[:, c, :],
                                             Pex[:, c * C:c * C + 1], ALU.add, ALU.add).then_inc(s["scan_done"], 1)

            for n in range(NC, len(STAGES) + SUM_LAG):
                if n < len(STAGES):
                    st, c = STAGES[n]
                    dve.wait_ge(s["st_z"], n - NC + 1)
                    dve.wait_ge(s["ag_out"], c + 1)
                    if n >= NC + 2:
                        dve.wait_ge(s["st_g"], n - 1)
                    nc.vector.tensor_tensor(zst[:, n % 2, :], banks[n % 4][:, 0:C], A_guess[:, c * C:(c + 1) * C],
                                            ALU.add).then_inc(s["st_zs"], 1)
                for m in ((n - SUM_LAG,) if n > NC else range(n - SUM_LAG + 1)):
                    st, c = STAGES[m]
                    dve.wait_ge(s["st_h"], m + 1)
                    h, S_c = hst[:, c, :], Ssum[:, c, :]
                    if st > 0:
                        dve.wait_ge(s["st_acc"], m - NC + 1)
                    if st == 0:
                        op = nc.vector.tensor_copy(S_c, h)
                    elif st < 3:
                        op = nc.vector.scalar_tensor_tensor(S_c, h, 2.0, S_c, ALU.mult, ALU.add)
                    else:
                        op = nc.vector.tensor_tensor(S_c, h, S_c, ALU.add)
                    op.then_inc(s["st_acc"], 1)
                    if st == 3 and c:
                        running_sum(c - 1)
            running_sum(NC - 1)
            dve.wait_ge(s["of_up"], 1)
            nc.vector.tensor_copy(off[:, :], banks[4][:, 0:1]).then_inc(s["of_done"], 1)
            dve.wait_ge(s["of_up"], 2)
            dve.wait_ge(s["a_made"], 1)
            nc.vector.tensor_tensor(base[:, :], banks[5][:, 0:1], a0[:, :], ALU.add).then_inc(s["bs_done"], 1)
            nc.vector.tensor_scalar(times[:, :], Pex[:, 0:T], off[:, :], DT / 6, ALU.add, ALU.mult).then_inc(s["pg_made"], 1)
            dve.wait_ge(s["bs_done"], 1)
            for c in range(NC):
                dve.wait_ge(s["an_up"], c + 1)
                if c >= 2:
                    dve.wait_ge(s["an_max"], c - 1)
                nc.vector.scalar_tensor_tensor(dev[:, c % 2, :], banks[c % 4][:, 0:C], base[:, :],
                                               A_rest[:, c * C:(c + 1) * C], ALU.add, ALU.add).then_inc(s["an_dev"], 1)
                dve.wait_ge(s["an_dev"], c + 1)
                nc.vector.tensor_reduce(devmax[:, c:c + 1], dev[:, c % 2, :], AX.X, ALU.max,
                                        apply_absolute_value=True).then_inc(s["an_max"], 1)
            dve.wait_ge(s["an_max"], NC)
            nc.vector.tensor_reduce(devtop[:, :], devmax[:, :], AX.X, ALU.max).then_inc(s["dv_top"], 1)
            dve.wait_ge(s["dv_row"], 1)
            nc.vector.tensor_reduce(devrow[:, :], banks[6][0:1, 0:128], AX.X, ALU.max).then_inc(s["dv_rowed"], 1)
            dve.wait_ge(s["dv_rowed"], 1)
            nc.vector.tensor_scalar(flag[:, :], devrow[:, :], TOL, None, ALU.is_le).then_inc(s["flag_made"], 1)
            dve.wait_ge(s["flag_made"], 1)
            checked = dve.value_load(flag[0:1, 0:1], min_val=0, max_val=1)
            with dve.If(checked == 0):
                nc.vector.memset(seq_P[:, :], 0.0).then_inc(s["sq_sum"], 1)
                nc.vector.tensor_tensor(seq_a[:, :], a0[0:H, :], fb1[0:H, :], ALU.add).then_inc(s["sq_set"], 1)
                dve.wait_ge(s["sq_set"], 1)
                dve.wait_ge(s["sq_sum"], 1)
                with dve.Fori(0, N // C) as b:
                    wait_apart(dve, s["sq_in"], 16 * (b + 1))
                    with dve.Fori(0, C) as i:
                        t = b * C + i
                        nc.vector.tensor_scalar(seq_blk[:, bass.ds(i, 1)], seq_P[:, :], DT / 6, None, ALU.mult).then_inc(s["sq_blk"], 1)
                        nc.vector.tensor_scalar(seq_bias[:, 0:1], seq_t[:, bass.ds(i, 1)], slope[0:H, :], seq_a[:, :],
                                                ALU.mult, ALU.add).then_inc(s["sq_blk"], 1)
                        dve.wait_ge(s["sq_blk"], 3 * t + 2)
                        nc.vector.tensor_scalar(seq_bias[:, 1:2], slope[0:H, :], DT / 2, seq_bias[:, 0:1],
                                                ALU.mult, ALU.add).then_inc(s["sq_blk"], 1)
                        nc.vector.tensor_scalar(seq_bias[:, 2:3], slope[0:H, :], DT, seq_bias[:, 0:1],
                                                ALU.mult, ALU.add).then_inc(s["sq_bias"], 1)
                        dve.wait_ge(s["sq_h"], 4 * t + 4)
                        nc.vector.tensor_tensor(seq_S[:, 0:1], seq_h[:, 1:2], seq_h[:, 2:3], ALU.add).then_inc(s["sq_set"], 1)
                        dve.wait_ge(s["sq_set"], 3 * t + 2)
                        nc.vector.scalar_tensor_tensor(seq_S[:, 1:2], seq_S[:, 0:1], 2.0, seq_h[:, 0:1],
                                                       ALU.mult, ALU.add).then_inc(s["sq_set"], 1)
                        dve.wait_ge(s["sq_set"], 3 * t + 3)
                        nc.vector.tensor_tensor(seq_S[:, 2:3], seq_S[:, 1:2], seq_h[:, 3:4], ALU.add).then_inc(s["sq_set"], 1)
                        dve.wait_ge(s["sq_set"], 3 * t + 4)
                        nc.vector.tensor_tensor(seq_P[:, :], seq_P[:, :], seq_S[:, 2:3], ALU.add).then_inc(s["sq_sum"], 1)
                        dve.wait_ge(s["sq_sum"], t + 2)
            dve.drain().then_inc(s["scan_over"], 1)
            dve.wait_ge(s["scan_over"], 5)

            def aggregate(at, stats_x, stats_y):
                if at.start == 0:
                    wait_apart(dve, s["xs_done"], stats_x)
                if at.stop == 2 * S:
                    wait_apart(dve, s["ys_done"], stats_y)
                for a in range(at.start, at.stop):
                    nc.vector.bn_aggr(mv[:, a, :], stats[:, a, :]).then_inc(s["aggr2"], 1)

            def factor_step(k, at, n):
                done = 6 * (n - 1)
                if k == 0:
                    dve.wait_ge(s["lns_guess"], 2 * n)
                    nc.vector.tensor_scalar(var_eps[:, at], mv[:, at, 1], EPS, None, ALU.add).then_inc(s["lns_newton"], 1)
                    nc.vector.tensor_tensor(sq[:, at], rstd[:, at], rstd[:, at], ALU.mult).then_inc(s["lns_newton"], 1)
                elif k == 1:
                    dve.wait_ge(s["lns_newton"], done + 2)
                    nc.vector.tensor_tensor(sq[:, at], sq[:, at], var_eps[:, at], ALU.mult).then_inc(s["lns_newton"], 1)
                elif k == 2:
                    dve.wait_ge(s["lns_newton"], done + 3)
                    nc.vector.tensor_scalar(sq[:, at], sq[:, at], -0.5, 1.5, ALU.mult, ALU.add).then_inc(s["lns_newton"], 1)
                elif k == 3:
                    dve.wait_ge(s["lns_newton"], done + 4)
                    nc.vector.tensor_tensor(rstd[:, at], rstd[:, at], sq[:, at], ALU.mult).then_inc(s["lns_newton"], 1)
                else:
                    dve.wait_ge(s["lns_newton"], done + 5)
                    nc.vector.scalar_tensor_tensor(shift[:, at], mv[:, at, 0], -1.0, rstd[:, at], ALU.mult,
                                                   ALU.mult).then_inc(s["lns_newton"], 1)

            def nodes(j, b):
                for q in range(S):
                    n = S * j + q
                    if has(j, q, 2):
                        w = (q + 2) % S
                        dve.wait_ge(s["xt_hi"], n + 3)
                        nc.vector.tensor_tensor(xTl[:, w, :, 0:P], turned_of(4), xTh[:, w, :, 0:P].bitcast(f32),
                                                ALU.subtract).then_inc(s["xt_lo"], 1)
                    if has(j, q, -5):
                        c, w = slot(b, q, -5)
                        dve.wait_ge(s["y_added"], n - 4)
                        nc.vector.bn_stats(stats[:, S + w, :], yb[:, c, w, :]).then_inc(s["ys_done"], 1)
                    if has(j, q, -2):
                        w = (q - 2) % S
                        dve.wait_ge(s["ut_hi"], n - 1)
                        nc.vector.tensor_tensor(uTl[:, w, :, 0:P], turned_of(5), uTh[:, w, :, 0:P].bitcast(f32),
                                                ALU.subtract).then_inc(s["ut_lo"], 1)
                    factors = q == 0 and norms(j)
                    if factors:
                        aggregate(factors, S * (j + 2), S * (j - 1))
                    if has(j, q, -1):
                        k = (q - 1) % 2
                        dve.wait_ge(s["nw_done"], n)
                        dve.wait_ge(s["nr_done"], n)
                        nc.vector.tensor_tensor(u[:, k, :], u[:, k, :], nr[:, k, :], ALU.mult).then_inc(s["u_done"], 1)
                    if factors:
                        factor_step(0, factors, j + 2)
                    if has(j, q, 0):
                        k = q % 2
                        dve.wait_ge(s["u_up"], n + 1)
                        dve.wait_ge(s[AGG_IN[q // 2]], 32 * (j + 1))
                        if has(j, q, -2):
                            dve.wait_ge(s["ne_done"], n - 1)
                            dve.wait_ge(s["nw_done"], n - 1)
                        nc.vector.tensor_tensor(nz[:, k, :], banks[k][0:P, :], agg[:, q, :], ALU.add).then_inc(s["z_done"], 1)
                    if factors:
                        factor_step(1, factors, j + 2)
                    if has(j, q, 8):
                        wait_apart(dve, s[X_IN[b][q // 2]], loads_by_parity(j + 2, b))
                        nc.vector.bn_stats(stats[:, q, :], xraw[:, b, q, :]).then_inc(s["xs_done"], 1)
                    if factors:
                        factor_step(2, factors, j + 2)
                    if has(j, q, 0):
                        k = q % 2
                        dve.wait_ge(s["ne_done"], n + 1)
                        nc.vector.tensor_scalar(ne[:, k, :], ne[:, k, :], EXP_MAX, None, ALU.min).then_inc(s["nc_done"], 1)
                    if factors:
                        factor_step(3, factors, j + 2)
                    if has(j, q, -9):
                        m = n - 9
                        c, w = slot(b, q, -9)
                        dve.wait_ge(s["o_up"], m + 1)
                        dve.wait_ge(s["yx_done"], m + 1)
                        nc.vector.tensor_tensor(ob[:, c, w, :], banks[6 + w % 2][0:P, :], ob[:, c, w, :], ALU.add).then_inc(s["o_added"], 1)
                    if factors:
                        factor_step(4, factors, j + 2)
                    if has(j, q, 0):
                        k = q % 2
                        dve.wait_ge(s["nc_done"], n + 1)
                        if has(j, q, -2):
                            dve.wait_ge(s["nl_done"], n - 1)
                            dve.wait_ge(s["nw_done"], n - 1)
                        nc.vector.scalar_tensor_tensor(nt[:, k, :], ne[:, k, :], 2.0, ne[:, k, :], ALU.add,
                                                       ALU.mult).then_inc(s["nt_done"], 1)
                    if q == S - 1 and has(j, 0, -S):
                        dve.wait_ge(s["steps_hi"], j)
                        low = steps_lhs[H:2 * H, 1 - b, :, 0:P]
                        nc.vector.tensor_tensor(low, steps_in[H:2 * H, 0:R].rearrange("k (p s) -> k s p", s=S),
                                                low.bitcast(f32), ALU.subtract).then_inc(s["steps_lo"], 1)
                    if has(j, q, -4):
                        m, c = n - 4, 1 - b
                        dve.wait_ge(s["y_up"], m + 1)
                        dve.wait_ge(s["xnb_done"], m + 1)
                        if has(j, q, -12):
                            dve.wait_ge(s["yx_done"], m - 7)
                        nc.vector.tensor_tensor(yb[:, c, q, :], banks[2 + q % 2][0:P, :], xnb[:, c, q, :], ALU.add).then_inc(s["y_added"], 1)

            run_nodes(dve, nodes)

        @block.tensor
        def _(pe):
            def product(to, chunks, signal):
                passes = [(l[a], r[b]) for l, r in chunks for a, b in ((0, 0), (0, 1), (1, 0))]
                for m, (l, r) in enumerate(passes):
                    op = nc.tensor.matmul(to, l, r, start=(m == 0), stop=(m == len(passes) - 1))
                op.then_inc(signal, 1)

            def turn(to, of, signal=None):
                op = nc.tensor.transpose(to, of, ident[0:P, 0:P])
                if signal is not None:
                    op.then_inc(signal, 1)

            def group(i, g, peeled=False):
                if g < 2 * S:
                    wait_apart(pe, s["rows_normed" if g < S else "rows_normed_dve"], S * i + g % S + 1)
                else:
                    wait_apart(pe, s["attr_in"], 16 * (i + 1))
                bank = banks[4 + g % 4]
                if g >= 4:
                    wait_apart(pe, s["group_lo"], NT * i + g - 3)
                elif not peeled:
                    wait_apart(pe, s["z_lo"] if g < 2 else s["c_out"], S * (i - 1) - 1 + g % 2)
                for k in range(KD):
                    of = rows[:, g, k * 128:(k + 1) * 128] if g < 2 * S else attr[:, k, :]
                    to = bank[:, k * 128:k * 128 + P] if g < 2 * S else bank[0:DE, k * P:(k + 1) * P]
                    turn(to, of, s["groups_up"] if k == KD - 1 else None)

            def groups(i, start=0, peeled=False):
                for g in range(start, NT):
                    group(i, g, peeled)

            def layer1(i, first=False):
                pe.wait_ge(s["group_lo"], NT * (i + 1))
                if first:
                    pe.wait_ge(s["split_lo"], 3)
                for m in range(KD):
                    cols = slice(m * 128, (m + 1) * 128)
                    if not first:
                        pe.wait_ge(s["w_done"], 2 * KD * i + m - 3)
                    product(banks[m][:, 0:R],
                            [((W1h[0:w, k, cols], W1l[0:w, k, cols]), (fTh[0:w, k, :], fTl[0:w, k, :]))
                             for k, w in [(k, 128) for k in range(2 * KD)] + [(2 * KD, DE)]], s["layer_up"])

            def layer2(i, first=False):
                pe.wait_ge(s["lo_done"], 2 * KD * i + KD)
                if first:
                    pe.wait_ge(s["split_lo"], EW)
                for m in range(KD):
                    cols = slice(m * 128, (m + 1) * 128)
                    pe.wait_ge(s["w_done"], 2 * KD * i + KD + m - 3)
                    product(banks[m][:, 0:R],
                            [((W2h[:, k, cols], W2l[:, k, cols]), (h1h[:, k, :], h1l[:, k, :])) for k in range(KD)],
                            s["layer_up"])

            def sums(i, ahead=True):
                pe.wait_ge(s["lo_done"], 2 * KD * (i + 1))
                for kind, q in L3_ORDER:
                    n = S * i + q
                    cols = slice(q * P, (q + 1) * P)
                    if kind == "z":
                        if q >= 2:
                            pe.wait_ge(s["z_lo"], n - 1)
                        product(banks[4 + q % 2][0:P, :],
                                [((msgh[:, k, cols], msgl[:, k, cols]), (W3h[:, k, :], W3l[:, k, :])) for k in range(KD)],
                                s["z_up"])
                    else:
                        if q == S - 1 and ahead:
                            group(i + 2, 0)
                        pe.wait_ge(s["z_lo"], n + 1)
                        pe.wait_ge(s["same_made"], S * (i + 1))
                        if q >= 2:
                            pe.wait_ge(s["c_out"], n - 1)
                        nc.tensor.matmul(banks[6 + q % 2][0:P, :], same[:, q, 0:P], zh[:, q % 2, :], start=True, stop=False)
                        nc.tensor.matmul(banks[6 + q % 2][0:P, :], same[:, q, 0:P], zl[:, q % 2, :], start=False,
                                         stop=True).then_inc(s["c_up"], 1)

            pe.wait_ge(s["diag_made"], 3)
            groups(0, peeled=True)
            layer1(0, first=True)
            groups(1, peeled=True)
            layer2(0, first=True)
            layer1(1)
            sums(0)
            groups(2, start=1)
            layer2(1)
            with pe.Fori(2, NE - 1) as i:
                layer1(i)
                sums(i - 1)
                groups(i + 1, start=1)
                layer2(i)
            layer1(NE - 1)
            sums(NE - 2, ahead=False)
            layer2(NE - 1)
            sums(NE - 1, ahead=False)
            def to_columns(of, bank, wait_for):
                pe.wait_ge(*wait_for)
                for k in range(KD):
                    op = nc.tensor.matmul(banks[bank][:, k:k + 1], of[:, k * 128:(k + 1) * 128], one_col[0:1, :], start=True, stop=True)
                op.then_inc(s["row_steps"], 1)

            pe.wait_ge(s["w_done"], 2 * KD * NE)
            to_columns(row_norm, 0, (s["row_steps"], 5))
            pe.wait_ge(s["row_steps"], 7)
            pe.wait_ge(s["n_staged"], 16)
            for m in range(KD):
                for k in range(KD):
                    op = nc.tensor.matmul(banks[1][:, m:m + 1], node_staging[:, 0, k, m * 128:(m + 1) * 128],
                                          row_cols[:, 0, k:k + 1], start=(k == 0), stop=(k == KD - 1))
            op.then_inc(s["row_steps"], 1)
            pe.drain().then_inc(s["edges_over"], 1)
            pe.wait_ge(s["edges_over"], 5)

            pe.wait_ge(s["row_agg_in"], 16)
            to_columns(row_agg, 2, (s["row_steps"], 9))
            pe.wait_ge(s["o_consts_in"], 16 * O_CONSTS)
            for k in range(KD):
                op = nc.tensor.matmul(banks[0][:, 0:128], fW3[:, k, :], fW1T[:, k, :], start=(k == 0), stop=(k == KD - 1))
            op.then_inc(s["o_mat_up"], 1)
            for k in range(KD):
                op = nc.tensor.matmul(banks[1][:, 0:1], fW1T[:, k, :], fb3[:, k:k + 1], start=(k == 0), stop=(k == KD - 1))
            op.then_inc(s["o_slope_up"], 1)
            pe.wait_ge(s["row_steps"], 17)
            pe.wait_ge(s["n_staged1"], 16)
            for k in range(KD):
                op = nc.tensor.matmul(banks[3][0:1, :], row_cols[:, 6, k:k + 1], node_staging[:, 1, k, :],
                                      start=(k == 0), stop=(k == KD - 1))
            op.then_inc(s["row_steps"], 1)
            pe.wait_ge(s["o_loaded"], 16 * O_LOADS)
            pe.wait_ge(s["o_set"], O_SET)
            pe.wait_ge(s["y0_made"], 1)
            for k in range(KD):
                op = nc.tensor.matmul(banks[2][:, k:k + 1], y0[:, k * 128:(k + 1) * 128], one_col[0:1, :], start=True, stop=True)
            op.then_inc(s["y0T_up"], 1)
            pe.wait_ge(s["y0T"], 2)
            for k in range(KD):
                op = nc.tensor.matmul(banks[3][:, 0:1], fW1T[:, k, :], y0b3[:, k, 0:1], start=(k == 0), stop=(k == KD - 1))
            op.then_inc(s["a_up"], 1)
            for k in range(KD):
                op = nc.tensor.matmul(banks[4][H:KV, 0:H], y0b3[:, k, :], fW1T[:, k, 0:H], start=(k == 0), stop=(k == KD - 1))
            op.then_inc(s["a_up"], 1)
            pe.wait_ge(s["o_mats"], 4)
            pe.wait_ge(s["o_slope"], 3)
            with pe.Fori(0, PICARD) as it:
                wait_apart(pe, s["V_made"], it + 1)
                nc.tensor.matmul(banks[0][0:H, 0:NQ], V[0:KV, :], rule[:, :], start=True, stop=True).then_inc(s["q_a"], 1)
                wait_apart(pe, s["q_g"], it + 1)
                nc.tensor.matmul(banks[1][0:H, 0:NQ], fW2[0:H, 0:H], gq[:, :], start=True, stop=True).then_inc(s["q_w"], 1)
                wait_apart(pe, s["q_h"], it + 1)
                nc.tensor.matmul(banks[2][0:NQ, 0:H], hq[:, :], M_T[:, :], start=True, stop=True).then_inc(s["q_v"], 1)
            pe.wait_ge(s["V_made"], PICARD + 1)
            for c in range(NC):
                if c >= 4:
                    pe.wait_ge(s["ag_out"], c - 3)
                for g in range(G):
                    at = g * T + c * C
                    op = nc.tensor.matmul(banks[c % 4][H * g:H * (g + 1), 0:C], V[0:KV, :], ruleT[:, at:at + C],
                                          start=True, stop=True)
                op.then_inc(s["ag_up"], 1)
            pe.wait_ge(s["ag_out"], NC)
            for n in range(len(STAGES) + STAGE_LAG):
                if NC <= n < len(STAGES):
                    st, c = STAGES[n]
                    pe.wait_ge(s["st_h"], n - NC + 1)
                    if n >= NC + 4:
                        pe.wait_ge(s["st_zs"], n - NC - 3)
                    nc.tensor.matmul(banks[n % 4][:, 0:C], (M_full if st == 3 else M_half)[:, :], hst[:, c, :],
                                     start=True, stop=True).then_inc(s["st_z"], 1)
                if n >= STAGE_LAG:
                    m = n - STAGE_LAG
                    pe.wait_ge(s["st_g"], m + 1)
                    if m >= 4:
                        pe.wait_ge(s["st_h"], m - 3)
                    nc.tensor.matmul(banks[4 + m % 4][:, 0:C], fW2[:, :], gst[:, m % 4, :], start=True,
                                     stop=True).then_inc(s["st_x"], 1)
            def own_part(c):
                pe.wait_ge(s["scan_done"], c + 1)
                nc.tensor.matmul(banks[c % 4][:, 0:C], M_six[:, :], Pex[:, c * C:(c + 1) * C], start=True, stop=True).then_inc(s["an_up"], 1)

            pe.wait_ge(s["st_zs"], 3 * NC)
            for c in range(4):
                own_part(c)
            pe.wait_ge(s["scan_done"], NC)
            nc.tensor.matmul(banks[4][:, 0:1], groups_before[:, :], Pex[:, T:T + 1], start=True, stop=True).then_inc(s["of_up"], 1)
            pe.wait_ge(s["of_done"], 1)
            nc.tensor.matmul(banks[5][:, 0:1], M_six[:, :], off[:, :], start=True, stop=True).then_inc(s["of_up"], 1)
            for c in range(4, NC):
                pe.wait_ge(s["an_dev"], c - 3)
                own_part(c)
            pe.wait_ge(s["dv_top"], 1)
            nc.tensor.transpose(banks[6][0:1, 0:128], devtop[:, :], ident[:, :]).then_inc(s["dv_row"], 1)
            pe.wait_ge(s["flag_made"], 1)
            checked = pe.value_load(flag[0:1, 0:1], min_val=0, max_val=1)
            with pe.If(checked == 0):
                with pe.Fori(0, N) as t:
                    wait_apart(pe, s["sq_sum"], t + 1)
                    for st in range(4):
                        if st == 0:
                            nc.tensor.matmul(banks[0][0:H, 0:1], M_six[0:H, 0:H], seq_P[:, :], start=True, stop=True).then_inc(s["sq_pre"], 1)
                        else:
                            wait_apart(pe, s["sq_h"], 4 * t + st)
                            nc.tensor.matmul(banks[0][0:H, 0:1], M_six[0:H, 0:H], seq_P[:, :], start=True, stop=False)
                            nc.tensor.matmul(banks[0][0:H, 0:1], (M_full if st == 3 else M_half)[0:H, 0:H],
                                             seq_h[:, st - 1:st], start=False, stop=True).then_inc(s["sq_pre"], 1)
                        wait_apart(pe, s["sq_g"], 4 * t + st + 1)
                        nc.tensor.matmul(banks[1][0:H, 0:1], fW2[0:H, 0:H], seq_g[:, :], start=True, stop=True).then_inc(s["sq_x"], 1)
            pe.drain().then_inc(s["scan_over"], 1)
            pe.wait_ge(s["scan_over"], 5)

            def turn_tile(bank, of, done):
                for k in range(KD):
                    turn(banks[bank][:, k * 128:k * 128 + P], of[:, k * 128:(k + 1) * 128], s[done] if k == KD - 1 else None)

            def update1(w):
                product(banks[w % 2][0:P, :],
                        [((xTh[:, w, k, 0:P], xTl[:, w, k, 0:P]), (W3ah[:, k, :], W3al[:, k, :])) for k in range(KD)],
                        s["u_up"])

            def update2(w):
                product(banks[2 + w % 2][0:P, :],
                        [((uTh[:, w, k, 0:P], uTl[:, w, k, 0:P]), (W4h[:, k, :], W4l[:, k, :])) for k in range(KD)],
                        s["y_up"])

            pe.wait_ge(s["rhs_hi"], 4)

            def nodes(j, b):
                for q in range(S):
                    n = S * j + q
                    if has(j, q, -9):
                        m = n - 9
                        c, w = slot(b, q, -9)
                        if w == 0:
                            wait_apart(pe, s["steps_lo"], j - 1)
                        if has(j, q, -11):
                            wait_apart(pe, s["o_added"], m - 1)
                        nc.tensor.matmul(banks[6 + w % 2][0:P, :], steps_lhs[:, c, w, 0:P], steps_rhs[:, :], start=True, stop=True).then_inc(s["o_up"], 1)
                    if has(j, q, 0):
                        pe.wait_ge(s["xt_lo"], n + 1)
                        if has(j, q, -2):
                            pe.wait_ge(s["z_done"], n - 1)
                        update1(q)
                    if has(j, q, -4):
                        pe.wait_ge(s["ut_lo"], n - 3)
                        if has(j, q, -6):
                            pe.wait_ge(s["y_added"], n - 5)
                        update2(q)
                    if has(j, q, 3):
                        pe.wait_ge(s["xn_done"], n + 4)
                        if has(j, q, 2):
                            pe.wait_ge(s["xt_lo"], n + 3)
                        turn_tile(4, xn[:, (q + 3) % S, :], "xt_up")
                    if has(j, q, -1):
                        pe.wait_ge(s["u_done"], n)
                        if has(j, q, -2):
                            pe.wait_ge(s["ut_lo"], n - 1)
                        turn_tile(5, u[:, (q - 1) % 2, :], "ut_up")

            run_nodes(pe, nodes)


NODES = 16


def rules(n_times):
    import numpy as np

    k = np.arange(NODES)
    at = 0.5 * (1 - np.cos((2 * k + 1) * np.pi / (2 * NODES)))
    cheb = np.polynomial.chebyshev
    unit = np.eye(NODES)
    inverse = np.linalg.inv(np.stack([cheb.chebval(2 * at - 1, unit[j]) for j in range(NODES)]))

    def table(t):
        whole = [cheb.chebint(unit[j]) * 0.5 for j in range(NODES)]
        to_t = np.stack([cheb.chebval(2 * t - 1, w) - cheb.chebval(-1, w) for w in whole])
        out = np.zeros((34, t.size))
        out[0:NODES] = inverse @ to_t
        out[32] = 1.0
        out[33] = t
        return out.astype(np.float32)

    times = table(np.arange(n_times) / (n_times - 1))
    high = ((times[33].view(np.uint32) + 0x800) & 0xFFFFF000).view(np.float32)
    one = np.ones_like(high)
    parts = np.stack([one, one, high, times[33] - high, high])
    return table(at), times, parts


_NAMES = ["x", "src_cols", "dst", "dst_cols", "edge_attr_64"] + [
    "L0_gnn_" + n for n in ("W1", "b1", "W2", "b2", "W3", "b3", "W4", "b4", "gamma", "beta")]


def kernel(**inputs):
    import numpy as _np
    import concourse.bacc as _bacc
    from concourse import mybir as _mybir
    from concourse.bass_utils import run_bass_kernel_spmd as _run

    nc = _bacc.Bacc("TRN2", target_bir_lowering=False, num_devices=1)
    f = {n: _np.asarray(inputs["L0_ffn_" + n]) for n in ("W1", "b1", "W2", "b2", "W3", "b3")}
    n_rows, d = inputs["x"].shape
    node_rule, time_rule, time_parts = rules(n_rows)
    for side in ("src", "dst"):
        inputs[side + "_cols"] = _np.asarray(inputs[side]).reshape(-1, 125).T
    given = [(n, inputs[n]) for n in _NAMES] + [
        ("F_W1T", f["W1"].T), ("F_b1", f["b1"]), ("F_W2T", f["W2"].T), ("F_b2", f["b2"]),
        ("F_W3", f["W3"]), ("F_W3T", f["W3"].T), ("F_b3", f["b3"]), ("node_rule", node_rule), ("time_rule", time_rule), ("time_parts", time_parts)]
    arrays, args = {}, []
    for name, a in given:
        a = _np.ascontiguousarray(a)
        arrays[f"in_{name}_dram"] = a
        args.append(nc.dram_tensor(f"in_{name}_dram", a.shape, _mybir.dt.from_np(a.dtype), kind="ExternalInput").ap())
    f32 = _mybir.dt.float32
    args.append(nc.dram_tensor("out_0_dram", (n_rows, d), f32, kind="ExternalOutput").ap())
    args.append(nc.dram_tensor("message_sums", (10240, d), f32).ap())
    args.append(nc.dram_tensor("sums_by_time", (f["b1"].shape[0], n_rows), f32).ap())
    gnn_ffn_kernel(nc, *args)
    r = _run(nc, [arrays], core_ids=[0])
    return r.results[0]["out_0_dram"]
```
